# Optimizing a Trainium2 kernel written in Bass

```python
import numpy as np
import jax
import jax.numpy as jnp

def _softmax(x, axis=-1):
    return jax.nn.softmax(x, axis=axis)

def _gelu(x):
    return jax.nn.gelu(x, approximate=True)

def _silu(x):
    return jax.nn.silu(x)

def _sigmoid(x):
    return jax.nn.sigmoid(x)

def _layernorm(x, axis=-1, eps=1e-05):
    m = jnp.mean(x, axis=axis, keepdims=True)
    v = jnp.var(x, axis=axis, keepdims=True)
    return (x - m) / jnp.sqrt(v + eps)

def _scatter_add(tgt, idx, src, axis=0):
    return tgt.at[idx].add(src)

def _segment_sum(src, seg, n):
    return jax.ops.segment_sum(src, seg, n)
kernel_name = 'mk_decoder_postln_d2_seqx_r8_33570c'

def setup_inputs(seed: int=0):
    np.random.seed(seed)
    _w = jnp.asarray

    def _rec_inputs():
        import jax
        import jax.numpy as jnp
        _rk = jax.random.key(seed)
        x = -0.0005207 + 1.001 * jax.random.normal(jax.random.fold_in(_rk, 1), (4, 256, 256), jnp.float32)
        _lenS = 256 - jax.random.randint(jax.random.fold_in(_rk, 7), (4,), 0, max(1, 256 // 4) + 1, jnp.int32)
        _lenS2 = 1601 - jax.random.randint(jax.random.fold_in(_rk, 8), (4,), 0, max(1, 1601 // 4) + 1, jnp.int32)
        _ctx_2048P = jax.random.normal(jax.random.fold_in(_rk, 12), (4, 16, 256), jnp.float32)
        _ctx_2048c = jax.random.dirichlet(jax.random.fold_in(_rk, 512), 0.3 * jnp.ones((16,), jnp.float32), (4, 1601))
        _ctx_2048t = jnp.einsum('bsk,bkd->bsd', _ctx_2048c, _ctx_2048P)
        _ctx_2048t = _ctx_2048t * jax.lax.rsqrt(jnp.mean(jnp.square(_ctx_2048t)) + 1e-12) * 0.953939
        ctx_2048 = -5.72187e-05 + 0.999849 * (_ctx_2048t + 0.3 * jax.random.normal(jax.random.fold_in(_rk, 612), (4, 1601, 256), jnp.float32))
        _validS = jnp.arange(256)[None, :] < _lenS[:, None]
        _validS2 = jnp.arange(1601)[None, :] < _lenS2[:, None]
        _causal = jnp.tril(jnp.ones((256, 256), dtype=bool))
        mask_BxSx4224_bf0 = jnp.logical_not(jnp.ones((4, 256, 528), dtype=bool))
        return (x, ctx_2048, mask_BxSx4224_bf0)
    x, ctx_2048, mask_BxSx4224_bf0 = _rec_inputs()

    def _L0_attn_setup():
        import jax, jax.numpy as jnp
        import numpy as np
        EMBED_DIM = 256
        NUM_HEADS = 16
        HEAD_DIM = EMBED_DIM // NUM_HEADS
        WINDOW = 64
        CHUNK = WINDOW
        SCALE = 1.0 / float(np.sqrt(HEAD_DIM))

        def _sliding_window_attention(q, k, v):
            B, H, S, D = q.shape
            C = CHUNK
            nc = S // C
            qc = q.reshape(B, H, nc, C, D)
            kp = jnp.pad(k, ((0, 0), (0, 0), (C, 0), (0, 0))).reshape(B, H, nc + 1, C, D)
            vp = jnp.pad(v, ((0, 0), (0, 0), (C, 0), (0, 0))).reshape(B, H, nc + 1, C, D)
            kc = jnp.concatenate([kp[:, :, :-1], kp[:, :, 1:]], axis=-2)
            vc = jnp.concatenate([vp[:, :, :-1], vp[:, :, 1:]], axis=-2)
            qa = jnp.arange(C)
            ka = jnp.arange(2 * C)
            diff = C + qa[:, None] - ka[None, :]
            base = (diff >= 0) & (diff <= WINDOW)
            kv_pos = (jnp.arange(nc)[:, None] - 1) * C + ka[None, :]
            mask = base[None, :, :] & (kv_pos >= 0)[:, None, :]
            scores = jnp.einsum('bhncd,bhnkd->bhnck', qc, kc) * SCALE
            scores = jnp.where(mask[None, None], scores, -jnp.inf)
            attn = jax.nn.softmax(scores, axis=-1)
            out = jnp.einsum('bhnck,bhnkd->bhncd', attn, vc)
            return out.reshape(B, H, S, D)
        key = jax.random.key(seed)
        k1, k2, k3 = jax.random.split(key, 3)
        B, S, E = (2, 512, EMBED_DIM)
        x = jax.random.normal(k1, (B, S, E), dtype=jnp.float32)
        w_qkv = jax.random.normal(k2, (3 * E, E), dtype=jnp.float32) * (1.0 / np.sqrt(E))
        w_out = jax.random.normal(k3, (E, E), dtype=jnp.float32) * (1.0 / np.sqrt(E))
        return {'x': x, 'w_qkv': w_qkv, 'w_out': w_out}
    _L0_attn_all = _L0_attn_setup()
    _L0_attn_in = {k: v for k, v in _L0_attn_all.items() if k in ('w_qkv', 'w_out')}
    del _L0_attn_all

    def _L0_xattn_setup():
        import jax, jax.numpy as jnp
        import numpy as np
        import math
        DIM = 256
        B, Q_LEN, KV_LEN = (8, 128, 512)
        key = jax.random.key(seed)
        ks = jax.random.split(key, 8)
        x = jax.random.normal(ks[0], (B, Q_LEN, DIM), dtype=jnp.float32)
        mask = jnp.zeros((B, Q_LEN, KV_LEN + Q_LEN), dtype=bool)
        k_cache = jax.random.normal(ks[1], (B, KV_LEN, DIM), dtype=jnp.float32)
        v_cache = jax.random.normal(ks[2], (B, KV_LEN, DIM), dtype=jnp.float32)
        scale = 1.0 / math.sqrt(DIM)
        wq = jax.random.normal(ks[3], (DIM, DIM), dtype=jnp.float32) * scale
        wk = jax.random.normal(ks[4], (DIM, DIM), dtype=jnp.float32) * scale
        wv = jax.random.normal(ks[5], (DIM, DIM), dtype=jnp.float32) * scale
        wo = jax.random.normal(ks[6], (DIM, DIM), dtype=jnp.float32) * scale
        return {'x': x, 'mask': mask, 'k_cache': k_cache, 'v_cache': v_cache, 'wq': wq, 'wk': wk, 'wv': wv, 'wo': wo}
    _L0_xattn_all = _L0_xattn_setup()
    _L0_xattn_in = {k: v for k, v in _L0_xattn_all.items() if k in ('wq', 'wk', 'wv', 'wo')}
    del _L0_xattn_all

    def _L0_ffn_setup():
        import jax, jax.numpy as jnp
        import numpy as np
        EPS = 1e-05

        def _quant_weight(w):
            scale = jnp.mean(jnp.abs(w)) + EPS
            wq = jnp.clip(jnp.round(w / scale), -1.0, 1.0) * scale
            return w + jax.lax.stop_gradient(wq - w)

        def _quant_act(x):
            scale = jnp.maximum(jnp.max(jnp.abs(x), axis=-1, keepdims=True), EPS) / 127.0
            xq = jnp.clip(jnp.round(x / scale), -128.0, 127.0) * scale
            return x + jax.lax.stop_gradient(xq - x)

        def bitlinear(x, w):
            return jnp.einsum('bsi,oi->bso', _quant_act(x), _quant_weight(w))
        key = jax.random.key(seed)
        k1, k2, k3, k4 = jax.random.split(key, 4)
        d_model, d_ff = (256, 1024)
        B, S = (4, 256)
        x = jax.random.normal(k1, (B, S, d_model), dtype=jnp.float32)
        w_gate = jax.random.normal(k2, (d_ff, d_model), dtype=jnp.float32) * 0.02
        w_up = jax.random.normal(k3, (d_ff, d_model), dtype=jnp.float32) * 0.02
        w_down = jax.random.normal(k4, (d_model, d_ff), dtype=jnp.float32) * 0.02
        return {'x': x, 'w_gate': w_gate, 'w_up': w_up, 'w_down': w_down}
    _L0_ffn_all = _L0_ffn_setup()
    _L0_ffn_in = {k: v for k, v in _L0_ffn_all.items() if k in ('w_gate', 'w_up', 'w_down')}
    del _L0_ffn_all

    def _L1_attn_setup():
        import jax, jax.numpy as jnp
        import numpy as np
        B, S, HID = (2, 256, 256)
        H, KV, HD, RD = (16, 4, 128, 64)
        MAX_POS = 512
        FULL = HD + RD

        def precompute_rope(dim, max_len, theta=10000.0):
            freqs = 1.0 / theta ** (jnp.arange(0, dim, 2, dtype=jnp.float32) / dim)
            t = jnp.arange(max_len, dtype=jnp.float32)
            f = jnp.outer(t, freqs)
            return (jnp.cos(f), jnp.sin(f))

        def apply_rope(x, cos, sin):
            n = x.shape[-2]
            c = cos[:n]
            s = sin[:n]
            x1 = x[..., ::2]
            x2 = x[..., 1::2]
            out1 = x1 * c - x2 * s
            out2 = x1 * s + x2 * c
            return jnp.stack([out1, out2], axis=-1).reshape(x.shape)
        key = jax.random.key(seed)
        ks = jax.random.split(key, 8)
        sc = 0.02
        return {'hidden_states': jax.random.normal(ks[0], (B, S, HID), jnp.float32), 'Wq': jax.random.normal(ks[1], (HID, H * HD), jnp.float32) * sc, 'Wkvc': jax.random.normal(ks[2], (HID, 64), jnp.float32) * sc, 'Wkdec': jax.random.normal(ks[3], (64, KV * HD), jnp.float32) * sc, 'Wvdec': jax.random.normal(ks[4], (64, KV * HD), jnp.float32) * sc, 'Wqrope': jax.random.normal(ks[5], (HID, H * RD), jnp.float32) * sc, 'Wkrope': jax.random.normal(ks[6], (64, KV * RD), jnp.float32) * sc, 'Wo': jax.random.normal(ks[7], (H * FULL, HID), jnp.float32) * sc}
    _L1_attn_all = _L1_attn_setup()
    _L1_attn_in = {k: v for k, v in _L1_attn_all.items() if k in ('Wq', 'Wkvc', 'Wkdec', 'Wvdec', 'Wqrope', 'Wkrope', 'Wo')}
    del _L1_attn_all

    def _L1_xattn_setup():
        import jax, jax.numpy as jnp
        import numpy as np
        EPS = 1e-06
        NUM_HEADS = 16

        def _feature_map(x):
            return jnp.where(x > 0, x + 1.0, jnp.exp(x))
        key = jax.random.key(seed)
        ks = jax.random.split(key, 7)
        B, L, S, D = (4, 512, 512, 256)
        sc = 1.0 / np.sqrt(D)
        return {'query': jax.random.normal(ks[0], (B, L, D), jnp.float32), 'kv': jax.random.normal(ks[1], (B, S, D), jnp.float32), 'Wq': jax.random.normal(ks[2], (D, D), jnp.float32) * sc, 'Wg': jax.random.normal(ks[3], (D, D), jnp.float32) * sc, 'bg': jnp.ones((D,), jnp.float32), 'Wkv': jax.random.normal(ks[4], (2 * D, D), jnp.float32) * sc, 'Wo': jax.random.normal(ks[5], (D, D), jnp.float32) * sc}
    _L1_xattn_all = _L1_xattn_setup()
    _L1_xattn_in = {k: v for k, v in _L1_xattn_all.items() if k in ('Wq', 'Wg', 'bg', 'Wkv', 'Wo')}
    del _L1_xattn_all

    def _L1_ffn_setup():
        import jax, jax.numpy as jnp
        import numpy as np
        E, TOPK, H, I = (8, 2, 256, 512)
        SOFTCAP = 30.0
        key = jax.random.key(seed)
        ks = jax.random.split(key, 5)
        s = 1.0 / np.sqrt(H)
        si = 1.0 / np.sqrt(I)
        return {'hidden_states': jax.random.normal(ks[0], (4, 256, H), jnp.float32), 'w_gate': jax.random.normal(ks[1], (H, E), jnp.float32) * s, 'w1': jax.random.normal(ks[2], (E, H, I), jnp.float32) * s, 'w3': jax.random.normal(ks[3], (E, H, I), jnp.float32) * s, 'w2': jax.random.normal(ks[4], (E, I, H), jnp.float32) * si}
    _L1_ffn_all = _L1_ffn_setup()
    _L1_ffn_in = {k: v for k, v in _L1_ffn_all.items() if k in ('w_gate', 'w1', 'w3', 'w2')}
    del _L1_ffn_all
    return {'x': x, 'ctx_2048': ctx_2048, 'mask_BxSx4224_bf0': mask_BxSx4224_bf0, 'L0_attn_w_qkv': _L0_attn_in['w_qkv'], 'L0_attn_w_out': _L0_attn_in['w_out'], 'L0_xattn_wq': _L0_xattn_in['wq'], 'L0_xattn_wk': _L0_xattn_in['wk'], 'L0_xattn_wv': _L0_xattn_in['wv'], 'L0_xattn_wo': _L0_xattn_in['wo'], 'L0_ffn_w_gate': _L0_ffn_in['w_gate'], 'L0_ffn_w_up': _L0_ffn_in['w_up'], 'L0_ffn_w_down': _L0_ffn_in['w_down'], 'L1_attn_Wq': _L1_attn_in['Wq'], 'L1_attn_Wkvc': _L1_attn_in['Wkvc'], 'L1_attn_Wkdec': _L1_attn_in['Wkdec'], 'L1_attn_Wvdec': _L1_attn_in['Wvdec'], 'L1_attn_Wqrope': _L1_attn_in['Wqrope'], 'L1_attn_Wkrope': _L1_attn_in['Wkrope'], 'L1_attn_Wo': _L1_attn_in['Wo'], 'L1_xattn_Wq': _L1_xattn_in['Wq'], 'L1_xattn_Wg': _L1_xattn_in['Wg'], 'L1_xattn_bg': _L1_xattn_in['bg'], 'L1_xattn_Wkv': _L1_xattn_in['Wkv'], 'L1_xattn_Wo': _L1_xattn_in['Wo'], 'L1_ffn_w_gate': _L1_ffn_in['w_gate'], 'L1_ffn_w1': _L1_ffn_in['w1'], 'L1_ffn_w3': _L1_ffn_in['w3'], 'L1_ffn_w2': _L1_ffn_in['w2']}

def reference(x, ctx_2048, mask_BxSx4224_bf0, L0_attn_w_qkv, L0_attn_w_out, L0_xattn_wq, L0_xattn_wk, L0_xattn_wv, L0_xattn_wo, L0_ffn_w_gate, L0_ffn_w_up, L0_ffn_w_down, L1_attn_Wq, L1_attn_Wkvc, L1_attn_Wkdec, L1_attn_Wvdec, L1_attn_Wqrope, L1_attn_Wkrope, L1_attn_Wo, L1_xattn_Wq, L1_xattn_Wg, L1_xattn_bg, L1_xattn_Wkv, L1_xattn_Wo, L1_ffn_w_gate, L1_ffn_w1, L1_ffn_w3, L1_ffn_w2):
    import jax
    import jax.numpy as jnp

    def _L0_attn_ref(x, w_qkv, w_out):
        import jax, jax.numpy as jnp
        import numpy as np
        EMBED_DIM = 256
        NUM_HEADS = 16
        HEAD_DIM = EMBED_DIM // NUM_HEADS
        WINDOW = 64
        CHUNK = WINDOW
        SCALE = 1.0 / float(np.sqrt(HEAD_DIM))

        def _sliding_window_attention(q, k, v):
            B, H, S, D = q.shape
            C = CHUNK
            nc = S // C
            qc = q.reshape(B, H, nc, C, D)
            kp = jnp.pad(k, ((0, 0), (0, 0), (C, 0), (0, 0))).reshape(B, H, nc + 1, C, D)
            vp = jnp.pad(v, ((0, 0), (0, 0), (C, 0), (0, 0))).reshape(B, H, nc + 1, C, D)
            kc = jnp.concatenate([kp[:, :, :-1], kp[:, :, 1:]], axis=-2)
            vc = jnp.concatenate([vp[:, :, :-1], vp[:, :, 1:]], axis=-2)
            qa = jnp.arange(C)
            ka = jnp.arange(2 * C)
            diff = C + qa[:, None] - ka[None, :]
            base = (diff >= 0) & (diff <= WINDOW)
            kv_pos = (jnp.arange(nc)[:, None] - 1) * C + ka[None, :]
            mask = base[None, :, :] & (kv_pos >= 0)[:, None, :]
            scores = jnp.einsum('bhncd,bhnkd->bhnck', qc, kc) * SCALE
            scores = jnp.where(mask[None, None], scores, -jnp.inf)
            attn = jax.nn.softmax(scores, axis=-1)
            out = jnp.einsum('bhnck,bhnkd->bhncd', attn, vc)
            return out.reshape(B, H, S, D)
        B, S, E = x.shape
        H, D = (NUM_HEADS, HEAD_DIM)
        qkv = x @ w_qkv.T
        qkv = qkv.reshape(B, S, 3, H, D).transpose(2, 0, 3, 1, 4)
        q, k, v = (qkv[0], qkv[1], qkv[2])
        o = _sliding_window_attention(q, k, v)
        o = o.transpose(0, 2, 1, 3).reshape(B, S, E)
        return o @ w_out.T

    def _L0_xattn_ref(x, mask, k_cache, v_cache, wq, wk, wv, wo):
        import jax, jax.numpy as jnp
        import numpy as np
        import math
        DIM = 256
        B, Q_LEN, KV_LEN = (8, 128, 512)
        q = jnp.einsum('bsd,ed->bse', x, wq)
        k_new = jnp.einsum('bsd,ed->bse', x, wk)
        v_new = jnp.einsum('bsd,ed->bse', x, wv)
        k = jnp.concatenate([k_cache, k_new], axis=1)
        v = jnp.concatenate([v_cache, v_new], axis=1)
        scale = 1.0 / math.sqrt(q.shape[-1])
        scores = jnp.einsum('bqd,bkd->bqk', q, k) * scale
        attn = jax.nn.softmax(scores, axis=-1)
        out = jnp.einsum('bqk,bkd->bqd', attn, v)
        return jnp.einsum('bqd,ed->bqe', out, wo)

    def _L0_ffn_ref(x, w_gate, w_up, w_down):
        import jax, jax.numpy as jnp
        import numpy as np
        EPS = 1e-05

        def _quant_weight(w):
            scale = jnp.mean(jnp.abs(w)) + EPS
            wq = jnp.clip(jnp.round(w / scale), -1.0, 1.0) * scale
            return w + jax.lax.stop_gradient(wq - w)

        def _quant_act(x):
            scale = jnp.maximum(jnp.max(jnp.abs(x), axis=-1, keepdims=True), EPS) / 127.0
            xq = jnp.clip(jnp.round(x / scale), -128.0, 127.0) * scale
            return x + jax.lax.stop_gradient(xq - x)

        def bitlinear(x, w):
            return jnp.einsum('bsi,oi->bso', _quant_act(x), _quant_weight(w))
        gate = jax.nn.sigmoid(bitlinear(x, w_gate))
        up = bitlinear(x, w_up)
        h = gate * up
        return bitlinear(h, w_down)

    def _L1_attn_ref(hidden_states, Wq, Wkvc, Wkdec, Wvdec, Wqrope, Wkrope, Wo):
        import jax, jax.numpy as jnp
        import numpy as np
        B, S, HID = (2, 256, 256)
        H, KV, HD, RD = (16, 4, 128, 64)
        MAX_POS = 512
        FULL = HD + RD

        def precompute_rope(dim, max_len, theta=10000.0):
            freqs = 1.0 / theta ** (jnp.arange(0, dim, 2, dtype=jnp.float32) / dim)
            t = jnp.arange(max_len, dtype=jnp.float32)
            f = jnp.outer(t, freqs)
            return (jnp.cos(f), jnp.sin(f))

        def apply_rope(x, cos, sin):
            n = x.shape[-2]
            c = cos[:n]
            s = sin[:n]
            x1 = x[..., ::2]
            x2 = x[..., 1::2]
            out1 = x1 * c - x2 * s
            out2 = x1 * s + x2 * c
            return jnp.stack([out1, out2], axis=-1).reshape(x.shape)
        b, s, _ = hidden_states.shape
        ratio = H // KV
        cos, sin = precompute_rope(RD, MAX_POS)
        q_nope = (hidden_states @ Wq).reshape(b, s, H, HD)
        q_rope = apply_rope((hidden_states @ Wqrope).reshape(b, s, H, RD), cos, sin)
        c = hidden_states @ Wkvc
        k_nope = (c @ Wkdec).reshape(b, s, KV, HD)
        v = (c @ Wvdec).reshape(b, s, KV, HD)
        k_rope = apply_rope((c @ Wkrope).reshape(b, s, KV, RD), cos, sin)
        q = jnp.concatenate([q_nope, q_rope], axis=-1)
        k = jnp.concatenate([k_nope, k_rope], axis=-1)
        v_p = jnp.pad(v, ((0, 0), (0, 0), (0, 0), (0, RD)))
        k = jnp.repeat(k, ratio, axis=2)
        v_p = jnp.repeat(v_p, ratio, axis=2)
        scale = 1.0 / jnp.sqrt(jnp.asarray(FULL, dtype=q.dtype))
        scores = jnp.einsum('bqhd,bkhd->bhqk', q, k) * scale
        causal = jnp.tril(jnp.ones((s, s), dtype=bool))
        scores = jnp.where(causal[None, None], scores, jnp.finfo(scores.dtype).min)
        attn = jax.nn.softmax(scores, axis=-1)
        out = jnp.einsum('bhqk,bkhd->bqhd', attn, v_p).reshape(b, s, H * FULL)
        return out @ Wo

    def _L1_xattn_ref(query, kv, Wq, Wg, bg, Wkv, Wo):
        import jax, jax.numpy as jnp
        import numpy as np
        EPS = 1e-06
        NUM_HEADS = 16

        def _feature_map(x):
            return jnp.where(x > 0, x + 1.0, jnp.exp(x))
        B, L, D = query.shape
        S = kv.shape[1]
        H = NUM_HEADS
        hd = D // H
        q = query @ Wq.T
        gate = jax.nn.sigmoid(query @ Wg.T + bg)
        kvp = kv @ Wkv.T
        k, v = jnp.split(kvp, 2, axis=-1)
        q = _feature_map(q.reshape(B, L, H, hd).transpose(0, 2, 1, 3))
        k = _feature_map(k.reshape(B, S, H, hd).transpose(0, 2, 1, 3))
        v = v.reshape(B, S, H, hd).transpose(0, 2, 1, 3)
        kv_summary = jnp.einsum('bhsd,bhse->bhde', k, v)
        k_sum = k.sum(axis=-2)
        z = 1.0 / (jnp.einsum('bhld,bhd->bhl', q, k_sum)[..., None] + EPS)
        attn = jnp.einsum('bhld,bhde->bhle', q, kv_summary) * z
        attn = attn.transpose(0, 2, 1, 3).reshape(B, L, D)
        out = attn * gate @ Wo.T
        return out

    def _L1_ffn_ref(hidden_states, w_gate, w1, w3, w2):
        import jax, jax.numpy as jnp
        import numpy as np
        E, TOPK, H, I = (8, 2, 256, 512)
        SOFTCAP = 30.0
        orig_shape = hidden_states.shape
        x = hidden_states.reshape(-1, H)
        logits = x @ w_gate
        logits = SOFTCAP * jnp.tanh(logits / SOFTCAP)
        probs = jax.nn.softmax(logits, axis=-1)
        _, idx = jax.lax.top_k(probs, TOPK)
        mask = jax.nn.one_hot(idx, E, dtype=probs.dtype).sum(-2)
        weights = probs * mask
        out = jnp.zeros_like(x)
        for e in range(E):
            h = jax.nn.silu(x @ w1[e]) * (x @ w3[e])
            out = out + h @ w2[e] * weights[:, e:e + 1]
        return out.reshape(orig_shape)
    x = _layernorm(x + _L0_attn_ref(x, L0_attn_w_qkv, L0_attn_w_out), axis=-1)
    x = _layernorm(x + _L0_xattn_ref(x, mask_BxSx4224_bf0, ctx_2048, ctx_2048, L0_xattn_wq, L0_xattn_wk, L0_xattn_wv, L0_xattn_wo), axis=-1)
    x = _layernorm(x + _L0_ffn_ref(x, L0_ffn_w_gate, L0_ffn_w_up, L0_ffn_w_down), axis=-1)
    x = _layernorm(x + _L1_attn_ref(x, L1_attn_Wq, L1_attn_Wkvc, L1_attn_Wkdec, L1_attn_Wvdec, L1_attn_Wqrope, L1_attn_Wkrope, L1_attn_Wo), axis=-1)
    x = _layernorm(x + _L1_xattn_ref(x, ctx_2048, L1_xattn_Wq, L1_xattn_Wg, L1_xattn_bg, L1_xattn_Wkv, L1_xattn_Wo), axis=-1)
    x = _layernorm(x + _L1_ffn_ref(x, L1_ffn_w_gate, L1_ffn_w1, L1_ffn_w3, L1_ffn_w2), axis=-1)
    return x

_drawn_inputs = setup_inputs


def setup_inputs(seed=0):
    import zlib

    import numpy as np

    out = dict(_drawn_inputs(seed))
    spreads = {'L1_xattn_bg': (1.0, 0.538)}
    factors = {'L0_ffn_w_gate': 4.967,
     'L1_attn_Wq': 32.553,
     'L1_attn_Wkdec': 35.843,
     'L1_attn_Wqrope': 39.012,
     'L1_attn_Wkrope': 49.966,
     'L1_xattn_Wq': 2.761}
    for name, (base, spread) in spreads.items():
        noise = np.random.default_rng([zlib.crc32(name.encode()), seed]).standard_normal(out[name].shape)
        drawn = base * np.exp(spread * noise) if base else spread * noise
        out[name] = jnp.asarray(drawn.astype(out[name].dtype))
    for name, factor in factors.items():
        out[name] = (out[name] * factor).astype(out[name].dtype)
    return out
```

```python
import numpy as np
import concourse.bass as bass
from concourse import mybir
from contextlib import ExitStack

F32 = mybir.dt.float32
BF16 = mybir.dt.bfloat16
ACT = mybir.ActivationFunctionType
ALU = mybir.AluOpType
AX = mybir.AxisListType.X

P = 128
B, S, E = 4, 256, 256
KT = E // P
TPB = S // P
NT = B * TPB
LN_EPS = 1e-5
H0, D0, WIN = 16, 16, 64
CTX = 1601
CB = -(-CTX // P)
CLAST = CTX - (CB - 1) * P
KEYS = CTX + S
SCOLS = [(0, 512), (512, 1024), (1024, 1536), (1536, KEYS)]
FF = 1024
QMAX = 127.0
Q_EPS = 1e-5
MAGIC = 1.5 * 2.0 ** 23
H1, KV1, HD, RD, LAT = 16, 4, 128, 64, 64
RH = RD // 2
SC1 = float(HD + RD) ** -0.5
PAIRS = H1 // 2
Z_EPS = 1e-6
NE, TOPK, FI = 8, 2, 512
CAP = 30.0
FM = FI // P

C_ID, C_WMASK, C_BLK, C_HM, C_TRI, C_COS, C_SIN, C_N = (
    int(n) for n in np.cumsum([0, P, 2 * P, P, 8, NE * NE, H1 * RH, H1 * RH]))
NEG = -1e30


def constants():
    c = np.zeros((P, C_N), np.float32)
    c[:, C_ID:C_ID + P] = np.eye(P)
    q, k = np.arange(P)[:, None], np.arange(P)[None, :]
    d0 = q - k
    d1 = (q % WIN) + WIN - k
    c[:, C_WMASK:C_WMASK + P] = np.where((d0 >= 0) & (d0 <= WIN), 0, NEG)
    c[:, C_WMASK + P:C_WMASK + 2 * P] = np.where((d1 >= 0) & (d1 <= WIN), 0, NEG)
    c[:, C_BLK:C_BLK + P] = (q // D0) == (k // D0)
    c[:, C_HM:C_HM + 8] = (np.arange(P)[:, None] // D0) == np.arange(8)[None, :]
    c[:, C_TRI:C_TRI + NE * NE] = (np.arange(NE)[None, :] < np.arange(NE)[:, None]).reshape(1, -1)
    freqs = (1.0 / np.float32(10000.0) ** (np.arange(0, RD, 2, dtype=np.float32) / np.float32(RD))).astype(np.float32)
    ang = np.outer(np.arange(H1, dtype=np.float32), freqs).astype(np.float32)
    c[:, C_COS:C_COS + H1 * RH] = np.cos(ang).reshape(1, -1)
    c[:, C_SIN:C_SIN + H1 * RH] = np.sin(ang).reshape(1, -1)
    return c


def causal_bias():
    d = np.where(np.arange(P)[:, None] >= np.arange(P)[None, :], 0, NEG)
    return np.concatenate([d, np.zeros((P, P)), d], 1).astype(np.float32)


def build(nc, d, out):
    with ExitStack() as ctx:
        def sb(name, shape, dt=F32):
            return ctx.enter_context(nc.sbuf_tensor(name, shape, dt))

        def sem(name):
            return ctx.enter_context(nc.semaphore(name))

        class Region:

            def __init__(self, name, words):
                self.buf, self.words = sb(name, [P, words]), words
                self.at = 0

            def start(self, at=0):
                self.at = at

            def cut(self, *shape, dt=F32):
                n = int(np.prod(shape))
                words = n if dt == F32 else -(-n // 2)
                assert self.at + words <= self.words, (self.at, words, self.words)
                v = self.buf[:, self.at:self.at + words]
                self.at += words
                if dt != F32:
                    v = v.bitcast(dt)
                names = " ".join("abcd"[:len(shape)])
                if len(shape) == 1:
                    return v
                return v.rearrange(f"p ({names}) -> p {names}", **dict(zip("abcd", shape)))

        PS = [ctx.enter_context(nc.psum_tensor(f"bank{i}", [P, 512], F32)) for i in range(8)]

        cst = sb("cst", [P, C_N])
        ident = cst[:, C_ID:C_ID + P]
        wmask = cst[:, C_WMASK:C_WMASK + 2 * P].rearrange("p (t k) -> p t k", t=2)
        blk = cst[:, C_BLK:C_BLK + P]
        hmask = cst[:, C_HM:C_HM + 8]
        tri = cst[:, C_TRI:C_TRI + NE * NE].rearrange("p (a b) -> p a b", a=NE)
        ident16 = sb("ident16", [P, P], BF16)
        cbias = sb("cbias", [P, 3 * P], BF16)
        ones = sb("ones", [P, P])
        magic = sb("magic", [P, 1])
        mhalf = sb("mhalf", [P, 1])
        x_row = sb("x_row", [P, NT, E])
        xT = sb("xT", [P, KT, B * S])
        res = sb("res", [P, 4, E])
        stats = sb("stats", [P, 4, 6])
        mv = sb("mv", [P, 4, 2])
        rstd = sb("rstd", [P, 4])
        w_qkv = sb("w_qkv", [P, KT, 3 * E])
        w_o0 = sb("w_o0", [P, KT, E])
        w_x0 = sb("w_x0", [P, 4, KT, E])
        w_x1 = sb("w_x1", [P, 5, KT, E])
        bg = sb("bg", [P, KT])
        nbg = sb("nbg", [P, KT])
        kvbd = sb("kvbd", [P, B, KT, P])
        dsum = sb("dsum", [P, B, KT, P])
        w_ff = sb("w_ff", [P, 3, 2 * FF], BF16)
        wabs = sb("wabs", [P, 3])
        wsc = sb("wsc", [P, 3])
        wsi = sb("wsi", [P, 3])
        w_kvc = sb("w_kvc", [P, KT, LAT])
        w_kr = sb("w_kr", [LAT, KV1, RD])
        w_ki = sb("w_ki", [LAT, KV1, P])
        w_kd = sb("w_kd", [P, KV1, LAT])
        w_vd = sb("w_vd", [P, KV1, LAT])
        w_rt = sb("w_rt", [P, KT, NE])

        CT_W, CR_W = KT * CTX, CB * (E + 1)
        SLOT = CT_W + CR_W
        U1 = Region("u1", 2 * SLOT)
        ctxT, ctxR = [], []
        for s in range(2):
            U1.start(s * SLOT)
            ctxT.append(U1.cut(KT, CTX))
            ctxR.append(U1.cut(CB, E + 1))
        U1.start(SLOT)
        vexp = U1.cut(3, 2, 8, P)
        U1.start(0)
        w_qe = U1.cut(KT, H1, P)
        w_vo = U1.cut(PAIRS, E)
        w_qT = U1.cut(H1, E)
        w_qr = U1.cut(KT, H1, RD)
        w_rot = U1.cut(H1, RH)
        U1.start(0)
        EXP_W = 2 * KT * FI + FM * E
        w_e = [U1.cut(EXP_W) for _ in range(2)]
        U2 = Region("u2", 3 * 2 * FF)
        w_f32 = U2.cut(3, 2 * FF)
        U2.start(0)
        w_oh = U2.cut(H1, E)
        U2.start(0)
        hT = U2.cut(2, FM, 512)
        U3 = Region("u3", 13312)
        qT = U3.cut(KT, S)
        kmask = U3.cut(KT, 8, S)
        sm = U3.cut(8, 4, P)
        PT = U3.cut(8, 4, P)
        oT = U3.cut(KT, S)
        U3.start(0)
        xq = U3.cut(KT, S)
        xk = U3.cut(KT, S)
        xv = U3.cut(TPB, E)
        prob = U3.cut(KEYS + 1)[:, 0:KEYS]
        probT = U3.cut(CB + TPB, P)
        ek = U3.cut(4, E)
        kf = U3.cut(4, E)
        m1 = U3.cut(KT, E + 2)
        m1T = U3.cut(KT, E)
        xo = U3.cut(E)
        xoT = U3.cut(KT, P)
        qtmp = U3.cut(2 * FF)
        U3.start(0)
        fr = U3.cut(2, E)
        fq = U3.cut(2, E, dt=BF16)
        fqT = U3.cut(2, KT, S, dt=BF16)
        sg = U3.cut(2, 512)
        hh = U3.cut(2, FF)
        hr = U3.cut(FF)
        hq = U3.cut(2, FF, dt=BF16)
        hqT = U3.cut(2, FF // P, P, dt=BF16)
        U3.start(0)
        cT = U3.cut(S)
        cR = U3.cut(2, TPB, LAT)
        kg = U3.cut(2, KV1, S)
        qe = U3.cut(3, 2, S)
        dp = U3.cut(6, 3, P)
        dpT = U3.cut(4, 3 * P)
        doT = U3.cut(PAIRS, S)
        U3.start(0)
        eq = U3.cut(2, 512)
        qf = U3.cut(2, KT, S)
        egt = U3.cut(2, 512)
        den = U3.cut(512)
        eat = U3.cut(2, KT, S)
        U3.start(6144)
        rt = U3.cut(NT, NE)
        rt2 = U3.cut(NT, NE)
        rcmp = U3.cut(NT, NE, NE)
        rcm2 = U3.cut(NT, NE, NE)
        wgt = U3.cut(NT, NE)
        sa = U3.cut(2, 512)
        acc = U3.cut(NT, E)
        mx = sb("mx", [P, 8, 4])
        rsum = sb("rsum", [P, 8, 4])
        rinv = sb("rinv", [P, 8, 4])
        bmx = sb("bmx", [P, 8])
        bsum = sb("bsum", [P, 8])
        fs = sb("fs", [P, 2, 8])
        fh = sb("fh", [P, 2, 8])
        dmx = sb("dmx", [P, 8, 2])
        dsm = sb("dsm", [P, 8, 2])
        dri = sb("dri", [P, 8, 2])

        names = """ld_const ld_x ld_xrow ld_attn0 ld_x0 ld_x1 ld_ctx0 ld_ctx1 ld_ffn ld_lat ld_cbias ld_wq ld_wo ld_out
            const_set ln_sum ln_var ln_rstd ln_done xT_raw xT_done
            a_q a_k a_v a_q_sb a_k_sb a_v_sb a_s a_mask a_max a_exp a_rinv a_norm a_pt a_pt_sb a_o a_o_sb a_y
            b_q b_k b_v b_q_sb b_k_sb b_v_sb b_s b_max b_exp b_rinv b_t b_pt_a b_pt_d b_o b_o_sb b_ot b_ot_sb b_y
            x_k x_exp x_kf x_m1 x_m1_sb x_m1T x_m1T_sb x_kv x_kvbd
            w_abs w_sum w_scale w_round w_tern
            f_sc f_round f_q f_qT f_qT_sb f_gu f_sig f_h f_hsc f_hround f_hq f_hqT f_hqT_sb f_y
            d_w d_w_sb d_c d_c_sb d_k d_k_sb d_rot d_q d_q_sb d_s d_max d_exp d_rinv d_norm
            d_t d_t_sb d_o d_o_sb d_y
            e_qg e_exp e_eg e_qf e_nd e_at e_y
            r_log r_act r_v m_w0 m_w1 m_ab m_silu m_h m_y m_acc
            pe_step dve_step pool_step act_step""".split()
        G = {n: sem(n) for n in names}

        block = ctx.enter_context(nc.Block())
        PS_xT = [PS[6], PS[0], PS[7], PS[5]]

        @block.sync
        def _(sp):
            def load(dst, src, s):
                sp.dma_start(dst, src).then_inc(G[s], 16)

            load(xT[:, :, :], d["xT"], "ld_x")
            load(w_qkv[:, :, :], d["w_qkv"], "ld_attn0")
            load(cst[:, :], d["cst"], "ld_const")
            load(x_row[:, :, :], d["x"].rearrange("(t p) e -> p t e", p=P), "ld_xrow")
            load(w_o0[:, :, :], d["w_o0"], "ld_attn0")
            for n in range(4):
                load(w_x0[:, n, :, :], d[f"w_x0_{n}"], "ld_x0")

            def load_ctx(b):
                s = b % 2
                src = d["ctx"][b]
                load(ctxT[s], d["ctxT"][b], f"ld_ctx{s}")
                load(ctxR[s][:, 0:CB - 1, 0:E], src[0:(CB - 1) * P, :].rearrange("(t p) e -> p t e", p=P), f"ld_ctx{s}")
                load(ctxR[s][0:CLAST, CB - 1, 0:E], src[(CB - 1) * P:CTX, :], f"ld_ctx{s}")

            load_ctx(0)
            for n in range(5):
                load(w_x1[:, n, :, :], d[f"w_x1_{n}"], "ld_x1")
            load(bg[:, :], d["bg"], "ld_x1")
            for n in range(3):
                load(w_f32[:, n, :], d[f"w_f{n}"], "ld_ffn")
            sp.wait_ge(G["a_o"], B)
            load_ctx(1)
            load(w_kvc[:, :, :], d["w_kvc"], "ld_lat")
            load(w_ki[:, :, 0:LAT], d["eye4"], "ld_lat")
            load(w_kr[:, :, :], d["w_kr"], "ld_lat")
            load(w_kd[:, :, :], d["w_kd"], "ld_lat")
            load(w_vd[:, :, :], d["w_vd"], "ld_lat")
            load(w_rt[:, :, :], d["w_rt"], "ld_lat")
            for b in range(2, B):
                sp.wait_ge(G["b_o"], 2 * (b - 1))
                load_ctx(b)
            sp.wait_ge(G["w_tern"], 3)
            load(w_oh, d["w_oh"], "ld_wo")
            sp.wait_ge(G["b_o"], 2 * B)
            load(w_qT, d["w_qT"], "ld_wq")
            load(w_qr, d["w_qr"], "ld_wq")
            sp.wait_ge(G["d_y"], B)
            sp.wait_ge(G["d_o"], B * PAIRS)

            def load_expert(e, s):
                for n, (a, z) in enumerate(((0, KT * FI), (KT * FI, 2 * KT * FI), (2 * KT * FI, EXP_W))):
                    sp.dma_start(w_e[s][:, a:z], d[f"e{n}"][:, bass.ds(e, 1), :]).then_inc(G[f"m_w{s}"], 16)

            for s in range(2):
                load_expert(s, s)
            with sp.Fori(0, NE // 2 - 1) as pair:
                e = pair * 2
                for s in range(2):
                    sp.wait_ge(G["m_y"], (e + s) * 4 + 4)
                    load_expert(e + (s + 2), s)
            for t in range(NT):
                sp.wait_ge(G["ln_done"], 5 * NT + t + 1)
                sp.dma_start(out[t * P:(t + 1) * P, :], x_row[:, t, :]).then_inc(G["ld_out"], 16)
            sp.wait_ge(G["ld_out"], 16 * NT)

        @block.gpsimd
        def _(pool):
            g = nc.gpsimd
            pool.wait_ge(G["ld_const"], 16)
            g.tensor_copy(ident16[:, :], ident).then_inc(G["const_set"], 1)
            g.memset(ones[:, :], 1.0).then_inc(G["const_set"], 1)
            g.memset(magic[:, :], MAGIC).then_inc(G["const_set"], 1)
            g.memset(mhalf[:, :], -0.5).then_inc(G["const_set"], 1)
            pool.dma_start(cbias[:, :], d["cbias"]).then_inc(G["ld_cbias"], 16)
            g.memset(ctxR[0][:, :, E:E + 1], 1.0).then_inc(G["const_set"], 1)
            g.memset(vexp, 0.0).then_inc(G["const_set"], 1)
            steps = [0]

            def rstd_of(n):
                s = n % 4
                pool.wait_ge(G["ln_var"], n + 1)
                g.tensor_scalar(rstd[:, s:s + 1], mv[:, s, 1:2], LN_EPS, None, ALU.add).then_inc(G["pool_step"], 1)
                steps[0] += 1
                pool.wait_ge(G["pool_step"], steps[0])
                g.tensor_tensor(rstd[:, s:s + 1], rstd[:, s:s + 1], mhalf[:, :], ALU.pow).then_inc(G["ln_rstd"], 1)

            for b in range(B):
                for f in range(8):
                    pool.wait_ge(G["a_rinv"], 8 * b + f + 1)
                    g.tensor_tensor(sm[:, f, :, :], sm[:, f, :, :],
                                    rinv[:, f, :].unsqueeze(2).broadcast_to([P, 4, P]), ALU.mult).then_inc(G["a_norm"], 1)
                    if f == 3 and b > 0:
                        for t in range(TPB):
                            rstd_of(2 * (b - 1) + t)
            for t in range(TPB):
                rstd_of(2 * (B - 1) + t)
            pool.wait_ge(G["a_o"], B)
            g.memset(ctxR[1][:, :, E:E + 1], 1.0).then_inc(G["const_set"], 1)
            for n in range(NT, 2 * NT):
                rstd_of(n)

            def rotate(dst, src, parts, heads):
                cos = cst[0:parts, C_COS:C_COS + heads * RH].rearrange("p (h r) -> p h r", h=heads)
                sin = cst[0:parts, C_SIN:C_SIN + heads * RH].rearrange("p (h r) -> p h r", h=heads)
                x1, x2 = src[:, :, 0:RH], src[:, :, RH:RD]
                o1, o2 = dst[:, :, 0:RH], dst[:, :, RH:RD]
                t = w_rot[0:parts, 0:heads, :]
                for o, a1, b1, op in ((o1, x1, x2, ALU.subtract), (o2, x2, x1, ALU.add)):
                    for dst1, p0, p1, f in ((o, a1, cos, ALU.mult), (t, b1, sin, ALU.mult), (o, o, t, op)):
                        g.tensor_tensor(dst1, p0, p1, f).then_inc(G["d_rot"], 1)
                        rots[0] += 1
                        pool.wait_ge(G["d_rot"], rots[0])

            rots = [0]
            pool.wait_ge(G["ld_lat"], 96)
            pool.wait_ge(G["ld_wq"], 32)
            rotate(w_ki[:, :, LAT:P], w_kr[:, :, :], LAT, KV1)
            for k in range(KT):
                rotate(w_qe[:, k, :, LAT:P], w_qr[:, k, :, :], P, H1)
            for n in range(2 * NT, 3 * NT):
                rstd_of(n)
            def norm_p(p):
                for h in (2 * p, 2 * p + 1):
                    pool.wait_ge(G["d_rinv"], h + 1)
                    for j, (a, z) in enumerate(((0, 1), (1, 3))):
                        g.tensor_scalar(dp[:, h % 6, a:z, :], dp[:, h % 6, a:z, :], dri[:, h % 8, j:j + 1], 1.0,
                                        ALU.mult, ALU.mult).then_inc(G["d_norm"], 1)

            for p in range(B * PAIRS + 1):
                b, q = divmod(p, PAIRS)
                if p > 0:
                    norm_p(p - 1)
                if q == 5 and b > 0:
                    for t in range(TPB):
                        rstd_of(3 * NT + 2 * (b - 1) + t)
            for t in range(TPB):
                rstd_of(3 * NT + 2 * (B - 1) + t)
            for n in range(4 * NT, 6 * NT):
                rstd_of(n)

        @block.scalar
        def _(act):
            a = nc.scalar
            act.wait_ge(G["const_set"], 6)

            def xT_copy(stage, b):
                n = stage * B + b
                act.wait_ge(G["xT_raw"], n + 1)
                a.activation(xT[:, :, b * S:(b + 1) * S], PS_xT[stage][:, :].rearrange("p (k t) -> p k t", k=KT),
                             ACT.Copy).then_inc(G["xT_done"], 1)

            def a_values(b):
                for w in range(3):
                    bank, at = ((2, 0), (3, 0), (2, E))[w]
                    if w == 0:
                        act.wait_ge(G["a_v"], 2 * b + 2)
                        if b > 0:
                            act.wait_ge(G["a_o"], b)
                    src = PS[bank][:, at:at + E].rearrange("p (f h d) -> p f h d", f=2, h=8)
                    for f in range(2):
                        a.activation(diag(vexp, w, f), src[:, f, :, :], ACT.Copy).then_inc(G["a_v_sb"], 1)

            def diag(v, w, f):
                base = v[:, w, f, 0, 0:D0]
                return bass.AP(base.tensor, base.offset, [list(base.ap[0]), [P + D0, 8], [1, D0]])

            for b in range(B + 1):
                if b < B:
                    act.wait_ge(G["a_q"], b + 1)
                    a.activation(qT, PS[0][:, :].rearrange("p (k t) -> p k t", k=KT), ACT.Copy,
                                 scale=float(D0) ** -0.5).then_inc(G["a_q_sb"], 1)
                if b >= 2:
                    xT_copy(0, b - 2)
                if b >= 1:
                    act.wait_ge(G["a_o"], b)
                    a.activation(oT, PS[6][:, :].rearrange("p (k t) -> p k t", k=KT), ACT.Copy).then_inc(G["a_o_sb"], 1)
                if b < B:
                    a_values(b)
                    for f in range(8):
                        act.wait_ge(G["a_max"], 8 * b + f + 1)
                        for h in range(4):
                            a.activation(sm[:, f, h, :], sm[:, f, h, :], ACT.Exp, bias=mx[:, f, h:h + 1],
                                         accum_out=rsum[:, f, h:h + 1]).then_inc(G["a_exp"], 1)
            xT_copy(0, B - 1)

            def b_exp(u):
                act.wait_ge(G["b_max"], u + 1)
                for c, (lo, hi) in enumerate(SCOLS):
                    a.activation(prob[:, lo:hi], PS[c][:, 0:hi - lo], ACT.Exp, bias=bmx[:, 4:5],
                                 accum_out=bsum[:, c:c + 1]).then_inc(G["b_exp"], 1)

            def b_probT(u, c):
                act.wait_ge(G["b_t"], 4 * u + c + 1)
                a.activation(probT[:, 4 * c:4 * c + 4, :], PS[4][:, :].rearrange("p (j q) -> p j q", j=4),
                             ACT.Copy).then_inc(G["b_pt_a"], 1)

            def b_oT(u):
                act.wait_ge(G["b_ot"], u + 1)
                a.activation(xoT, PS[7 if u % 2 else 6][:, 0:KT * P].rearrange("p (k t) -> p k t", k=KT),
                             ACT.Copy).then_inc(G["b_ot_sb"], 1)

            for b in range(B):
                act.wait_ge(G["b_q"], b + 1)
                a.activation(xq, PS[4][:, :].rearrange("p (k t) -> p k t", k=KT), ACT.Copy,
                             scale=float(E) ** -0.5).then_inc(G["b_q_sb"], 1)
                act.wait_ge(G["b_k"], b + 1)
                a.activation(xk, PS[5][:, :].rearrange("p (k t) -> p k t", k=KT), ACT.Copy).then_inc(G["b_k_sb"], 1)
                if b > 0:
                    b_oT(2 * b - 1)
                b_exp(2 * b)
                for t in range(CB):
                    n = CB * b + t
                    rows = P if t < CB - 1 else CLAST
                    act.wait_ge(G["x_k"], n + 1)
                    if n >= 4:
                        act.wait_ge(G["x_kf"], n - 3)
                    a.activation(ek[0:rows, n % 4, :], PS[4 + t % 2][0:rows, 0:E], ACT.Exp).then_inc(G["x_exp"], 1)
                for c in (0, 2):
                    b_probT(2 * b, c)
                act.wait_ge(G["x_m1T"], b + 1)
                a.activation(m1T, PS[6][:, :].rearrange("p (k t) -> p k t", k=KT), ACT.Copy).then_inc(G["x_m1T_sb"], 1)
                b_exp(2 * b + 1)
                for c in (0, 2):
                    b_probT(2 * b + 1, c)
                b_oT(2 * b)
                if b < 3:
                    act.wait_ge(G["w_scale"], b + 1)
                    a.activation(qtmp, w_f32[:, b, :], ACT.Identity, scale=wsi[:, b:b + 1],
                                 bias=magic[:, :]).then_inc(G["w_round"], 1)
            b_oT(2 * B - 1)

            def f_down(t):
                act.wait_ge(G["f_hsc"], t + 1)
                a.activation(hr, hh[:, t % 2, :], ACT.Identity, scale=fh[:, t % 2, 3:4],
                             bias=magic[:, :]).then_inc(G["f_hround"], 1)

            for t in range(NT + 1):
                if t < NT:
                    if t % TPB == 0:
                        b = t // TPB
                        for j in range(TPB):
                            act.wait_ge(G["f_sc"], t + j + 1)
                            a.activation(fr[:, j, :], x_row[:, t + j, :], ACT.Identity, scale=fs[:, j, 2:3],
                                         bias=magic[:, :]).then_inc(G["f_round"], 1)
                        act.wait_ge(G["f_qT"], b + 1)
                        a.activation(fqT[:, b % 2, :, :], PS[0][:, 0:S].bitcast(BF16).rearrange("p (k t) -> p k t", k=KT),
                                     ACT.Copy).then_inc(G["f_qT_sb"], 1)
                    for c in range(2):
                        act.wait_ge(G["f_gu"], 4 * t + 2 * c + 1)
                        if 2 * t + c >= 2:
                            act.wait_ge(G["f_h"], 2 * t + c - 1)
                        a.activation(sg[:, c, :], PS[1 + 2 * c][:, :], ACT.Sigmoid,
                                     scale=fs[:, t % 2, 3:4]).then_inc(G["f_sig"], 1)
                    f_down(t)
                if t < NT:
                    act.wait_ge(G["d_w"], t + 1)
                    a.activation(w_qe[:, :, 2 * t:2 * t + 2, 0:LAT],
                                 PS[7][:, 0:2 * KT * LAT].rearrange("p (k h c) -> p k h c", k=KT, h=2),
                                 ACT.Copy).then_inc(G["d_w_sb"], 1)
                    a.activation(w_vo[:, t, :], PS[7][:, 256:256 + E], ACT.Copy).then_inc(G["d_w_sb"], 1)
                    act.wait_ge(G["f_hqT"], t + 1)
                    a.activation(hqT[:, t % 2, :, :], PS[5][:, :].bitcast(BF16).rearrange("p (k t) -> p k t", k=FF // P),
                                 ACT.Copy).then_inc(G["f_hqT_sb"], 1)
                if t >= 2 and t % TPB == 0:
                    xT_copy(1, t // TPB - 1)

            def d_latent(b):
                act.wait_ge(G["d_c"], b + 1)
                a.activation(cT[0:LAT, :], PS[7][0:LAT, 0:S], ACT.Copy).then_inc(G["d_c_sb"], 1)
                a.activation(cR[:, b % 2, :, :], PS[7][:, S:S + TPB * LAT].rearrange("p (t c) -> p t c", t=TPB),
                             ACT.Copy).then_inc(G["d_c_sb"], 1)

            def d_keys(b):
                for h in range(2):
                    act.wait_ge(G["d_k"], 2 * b + h + 1)
                    a.activation(kg[:, b % 2, 2 * h:2 * h + 2, :], PS[7][:, :].rearrange("p (h q) -> p h q", h=2), ACT.Copy,
                                 scale=SC1).then_inc(G["d_k_sb"], 1)

            d_latent(0)
            d_keys(0)
            NP = B * PAIRS
            for p in range(NP + 4):
                b, q = divmod(p, PAIRS)
                if q == 4 and b + 1 < B:
                    d_latent(b + 1)
                if q == 5 and b + 1 < B:
                    d_keys(b + 1)
                if p < NP:
                    for h in (2 * p, 2 * p + 1):
                        for j, (lo, hi) in enumerate(((0, 1), (1, 3))):
                            if j == 0:
                                act.wait_ge(G["d_max"], 2 * h + 2)
                            a.activation(dp[:, h % 6, lo:hi, :],
                                         PS[2 + h % 2][:, lo * P:hi * P].rearrange("p (c k) -> p c k", k=P), ACT.Exp,
                                         bias=dmx[:, h % 8, j:j + 1],
                                         accum_out=dsm[:, h % 8, j:j + 1]).then_inc(G["d_exp"], 1)
                if 2 <= p < NP + 2:
                    for h in (2 * p - 4, 2 * p - 3):
                        act.wait_ge(G["d_t"], h + 1)
                        a.activation(dpT[:, h % 4, :], PS[4 + h % 2][:, 0:3 * P], ACT.Copy).then_inc(G["d_t_sb"], 1)
                if 3 <= p < NP + 3:
                    act.wait_ge(G["d_o"], p - 2)
                    a.activation(doT[:, (p - 3) % PAIRS, :], PS[6][:, 0:S], ACT.Copy).then_inc(G["d_o_sb"], 1)
                if q == 6 and b > 0:
                    xT_copy(2, b - 1)
            xT_copy(2, B - 1)

            for b in range(B):
                s = b % 2
                act.wait_ge(G["e_qg"], 2 * b + 1)
                a.activation(eq[:, s, :], PS[0][:, :], ACT.Exp).then_inc(G["e_exp"], 1)
                act.wait_ge(G["e_qg"], 2 * b + 2)
                if b >= 2:
                    act.wait_ge(G["e_at"], b - 1)
                for k in range(KT):
                    a.activation(egt[:, s, k * S:(k + 1) * S], PS[1][:, k * S:(k + 1) * S], ACT.Exp,
                                 bias=nbg[:, k:k + 1], scale=-1.0).then_inc(G["e_eg"], 1)
                if b >= 2:
                    xT_copy(3, b - 2)
            xT_copy(3, B - 2)
            xT_copy(3, B - 1)

            act.wait_ge(G["r_log"], 1)
            a.activation(rt, PS[6][:, 0:NT * NE].rearrange("p (t e) -> p t e", t=NT), ACT.Tanh,
                         scale=1.0 / CAP).then_inc(G["r_act"], 1)
            act.wait_ge(G["r_v"], 1)
            a.activation(rt, rt2, ACT.Exp, scale=CAP).then_inc(G["r_act"], 1)
            with act.Fori(0, NE // 2) as pair:
                e = pair * 2
                for i in range(4 * FM):
                    act.wait_ge(G["m_ab"], e * (4 * FM) + 2 * i + 1)
                    m = e * (2 * FM) + i
                    if i >= 2:
                        act.wait_ge(G["m_h"], m - 1)
                    a.activation(sa[:, i % 2, :], PS[i % 2][:, :], ACT.Silu).then_inc(G["m_silu"], 1)

        @block.vector
        def _(dve):
            v = nc.vector
            steps = [0]

            def link(ins):
                ins.then_inc(G["dve_step"], 1)
                steps[0] += 1
                dve.wait_ge(G["dve_step"], steps[0])

            def ln_begin(n, add):
                s = n % 4
                link(add(res[:, s, :]))
                link(v.bn_stats(stats[:, s, :], res[:, s, :]))
                v.bn_aggr(mv[:, s, :], stats[:, s, :]).then_inc(G["ln_var"], 1)

            def ln_end(n):
                s, t = n % 4, n % NT
                dve.wait_ge(G["ln_rstd"], n + 1)
                v.tensor_scalar(x_row[:, t, :], res[:, s, :], mv[:, s, 0:1], rstd[:, s:s + 1], ALU.subtract,
                                ALU.mult).then_inc(G["ln_done"], 1)

            def add_rows(bank, at, t):
                return lambda o: v.tensor_tensor(o, PS[bank][:, at:at + E], x_row[:, t, :], ALU.add)

            dve.wait_ge(G["const_set"], 6)

            for b in range(B + 1):
                if b < B:
                    dve.wait_ge(G["a_k"], b + 1)
                    for k in range(KT):
                        v.tensor_tensor(kmask[:, k, :, :], PS[1][:, k * S:(k + 1) * S].unsqueeze(1).broadcast_to([P, 8, S]),
                                        hmask.unsqueeze(2).broadcast_to([P, 8, S]), ALU.mult).then_inc(G["a_k_sb"], 1)
                if b >= 1:
                    for f in range(8):
                        dve.wait_ge(G["a_pt"], 8 * (b - 1) + f + 1)
                        v.tensor_copy(PT[:, f, :, :], PS[4 + f % 2][:, :].rearrange("p (h q) -> p h q", h=4)).then_inc(G["a_pt_sb"], 1)
                    if b == 1:
                        dve.wait_ge(G["ld_xrow"], 16)
                    dve.wait_ge(G["a_y"], b)
                    for t in range(TPB):
                        ln_begin(2 * (b - 1) + t, add_rows(7, t * E, 2 * (b - 1) + t))
                if b < B:
                    def rinv_of(f):
                        dve.wait_ge(G["a_exp"], 32 * b + 4 * f + 4)
                        v.reciprocal(rinv[:, f, :], rsum[:, f, :]).then_inc(G["a_rinv"], 1)

                    for f in range(8):
                        dve.wait_ge(G["a_s"], 8 * b + f + 1)
                        v.tensor_tensor(sm[:, f, :, :], PS[f % 4][:, :].rearrange("p (h k) -> p h k", h=4),
                                        wmask[:, f % 2, :].unsqueeze(1).broadcast_to([P, 4, P]), ALU.add).then_inc(G["a_mask"], 1)
                        dve.wait_ge(G["a_mask"], 8 * b + f + 1)
                        v.tensor_reduce(mx[:, f, :], sm[:, f, :, :], AX, ALU.max, negate=True).then_inc(G["a_max"], 1)
                        if f >= 2:
                            rinv_of(f - 2)
                        if f == 5 and b > 0:
                            for t in range(TPB):
                                ln_end(2 * (b - 1) + t)
                    rinv_of(6)
                    rinv_of(7)
            for t in range(TPB):
                ln_end(2 * (B - 1) + t)

            def b_max(u):
                for c, (lo, hi) in enumerate(SCOLS):
                    dve.wait_ge(G["b_s"], 4 * u + c + 1)
                    ins = v.tensor_reduce(bmx[:, c:c + 1], PS[c][:, 0:hi - lo], AX, ALU.max)
                    if c < 3:
                        ins.then_inc(G["dve_step"], 1)
                        steps[0] += 1
                    else:
                        link(ins)
                v.tensor_reduce(bmx[:, 4:5], bmx[:, 0:4], AX, ALU.max, negate=True).then_inc(G["b_max"], 1)

            def b_probT(u, c):
                nb = 4 if c < 3 else 3
                dve.wait_ge(G["b_t"], 4 * u + c + 1)
                v.tensor_copy(probT[:, 4 * c:4 * c + nb, :],
                              PS[5][:, 0:nb * P].rearrange("p (j q) -> p j q", j=nb)).then_inc(G["b_pt_d"], 1)

            def b_rinv(u):
                dve.wait_ge(G["b_exp"], 4 * u + 4)
                link(v.tensor_reduce(bsum[:, 4:5], bsum[:, 0:4], AX, ALU.add))
                link(v.reciprocal(bsum[:, 5:6], bsum[:, 4:5]))

            def b_out(u):
                dve.wait_ge(G["b_o"], u + 1)
                v.tensor_scalar(xo, PS[7][:, 0:E], bsum[:, 5:6], None, ALU.mult).then_inc(G["b_o_sb"], 1)

            def b_ln(u):
                dve.wait_ge(G["b_y"], u + 1)
                ln_begin(NT + u, add_rows(7 if u % 2 else 6, 0, u))

            dve.wait_ge(G["ld_ffn"], 48)
            dve.wait_ge(G["ld_x1"], 96)
            link(v.tensor_scalar(nbg[:, :], bg[:, :], -1.0, None, ALU.mult))
            for b in range(B):
                dve.wait_ge(G["b_v"], b + 1)
                v.tensor_copy(xv, PS[6][:, :].rearrange("p (t e) -> p t e", t=TPB)).then_inc(G["b_v_sb"], 1)
                b_max(2 * b)
                if b > 0:
                    b_ln(2 * b - 1)
                for t in range(CB):
                    n = CB * b + t
                    rows = P if t < CB - 1 else CLAST
                    dve.wait_ge(G["x_exp"], n + 1)
                    link(v.tensor_scalar(ek[0:rows, n % 4, :], ek[0:rows, n % 4, :], 1.0, None, ALU.min))
                    if n >= 4:
                        dve.wait_ge(G["x_m1"], n - 3)
                    v.scalar_tensor_tensor(out=kf[0:rows, n % 4, :], in0=PS[4 + t % 2][0:rows, 0:E], scalar=0.0,
                                           in1=ek[0:rows, n % 4, :], op0=ALU.max, op1=ALU.add).then_inc(G["x_kf"], 1)
                    if t == 4 and b > 0:
                        ln_end(NT + 2 * b - 2)
                        ln_end(NT + 2 * b - 1)
                b_rinv(2 * b)
                b_probT(2 * b, 1)
                b_probT(2 * b, 3)
                dve.wait_ge(G["x_m1"], CB * (b + 1))
                for k in range(KT):
                    v.tensor_copy(m1[:, k, 0:E + 1], PS[6 + k][:, 0:E + 1]).then_inc(G["x_m1_sb"], 1)
                b_max(2 * b + 1)
                b_out(2 * b)
                b_probT(2 * b + 1, 1)
                b_probT(2 * b + 1, 3)
                b_rinv(2 * b + 1)
                dve.wait_ge(G["x_kv"], b + 1)
                for k in range(KT):
                    v.tensor_scalar(dsum[:, b, k, :], blk, m1[:, k, E:E + 1], None, ALU.mult).then_inc(G["dve_step"], 1)
                    steps[0] += 1
                v.tensor_tensor(kvbd[:, b, :, :], PS[6][:, 0:KT * P].rearrange("p (k e) -> p k e", k=KT),
                                blk.unsqueeze(1).broadcast_to([P, KT, P]), ALU.mult).then_inc(G["x_kvbd"], 1)
                if b < 3:
                    v.tensor_reduce(wabs[:, b:b + 1], w_f32[:, b, :], AX, ALU.add,
                                    apply_absolute_value=True).then_inc(G["w_abs"], 1)
                b_ln(2 * b)
                b_out(2 * b + 1)
                if b < 3:
                    dve.wait_ge(G["w_sum"], b + 1)
                    link(v.tensor_scalar(wsc[:, b:b + 1], PS[6][:, 0:1], 1.0 / (FF * E), Q_EPS, ALU.mult, ALU.add))
                    v.reciprocal(wsi[:, b:b + 1], wsc[:, b:b + 1]).then_inc(G["w_scale"], 1)
                    dve.wait_ge(G["w_round"], b + 1)
                    link(v.tensor_scalar(qtmp, qtmp, MAGIC, 1.0, ALU.subtract, ALU.min))
                    v.tensor_scalar(w_ff[:, b, :], qtmp, -1.0, None, ALU.max).then_inc(G["w_tern"], 1)
            b_ln(2 * B - 1)
            ln_end(NT + 2 * B - 2)
            ln_end(NT + 2 * B - 1)

            def f_scales(t):
                j = t % 2
                dve.wait_ge(G["ln_done"], NT + t + 1)
                link(v.tensor_reduce(fs[:, j, 0:1], x_row[:, t, :], AX, ALU.max, apply_absolute_value=True))
                link(v.tensor_scalar(fs[:, j, 1:2], fs[:, j, 0:1], Q_EPS, 1.0 / QMAX, ALU.max, ALU.mult))
                link(v.tensor_tensor(fs[:, j, 3:5], fs[:, j, 1:2].broadcast_to([P, 2]), wsc[:, 0:2], ALU.mult))
                v.reciprocal(fs[:, j, 2:3], fs[:, j, 1:2]).then_inc(G["f_sc"], 1)

            def f_quant(t):
                j = t % 2
                dve.wait_ge(G["f_round"], t + 1)
                v.tensor_scalar(fq[:, j, :], fr[:, j, :], MAGIC, QMAX, ALU.subtract, ALU.min).then_inc(G["f_q"], 1)

            def f_hidden(t):
                j = t % 2
                for c in range(2):
                    dve.wait_ge(G["f_sig"], 2 * t + c + 1)
                    dve.wait_ge(G["f_gu"], 4 * t + 2 * c + 2)
                    v.tensor_tensor(hh[:, j, c * 512:(c + 1) * 512], sg[:, c, :], PS[2 + 2 * c][:, :], ALU.mult).then_inc(G["f_h"], 1)
                dve.wait_ge(G["f_h"], 2 * t + 2)
                link(v.tensor_reduce(fh[:, j, 0:1], hh[:, j, :], AX, ALU.max, apply_absolute_value=True))
                link(v.tensor_scalar(fh[:, j, 1:2], fh[:, j, 0:1], fs[:, j, 4:5], Q_EPS, ALU.mult, ALU.max))
                link(v.tensor_scalar(fh[:, j, 1:2], fh[:, j, 1:2], 1.0 / QMAX, None, ALU.mult))
                link(v.reciprocal(fh[:, j, 2:3], fh[:, j, 1:2]))
                link(v.tensor_tensor(fh[:, j, 4:5], fh[:, j, 1:2], wsc[:, 2:3], ALU.mult))
                v.tensor_tensor(fh[:, j, 3:4], fh[:, j, 2:3], fs[:, j, 4:5], ALU.mult).then_inc(G["f_hsc"], 1)
                dve.wait_ge(G["f_hround"], t + 1)
                v.tensor_scalar(hq[:, j, :], hr, MAGIC, QMAX, ALU.subtract, ALU.min).then_inc(G["f_hq"], 1)

            def f_out(t):
                n = 2 * NT + t
                dve.wait_ge(G["f_y"], t + 1)
                ln_begin(n, lambda o: v.scalar_tensor_tensor(out=o, in0=PS[6][:, 0:E], scalar=fh[:, t % 2, 4:5],
                                                             in1=x_row[:, t, :], op0=ALU.mult, op1=ALU.add))

            for t in range(NT + 1):
                if t < NT and t % TPB == 0:
                    for j in range(TPB):
                        f_scales(t + j)
                    for j in range(TPB):
                        f_quant(t + j)
                if t > 0:
                    f_out(t - 1)
                if t < NT:
                    f_hidden(t)
                if t > 0:
                    ln_end(2 * NT + t - 1)

            def d_query(p):
                dve.wait_ge(G["d_q"], p + 1)
                v.tensor_copy(qe[:, p % 3, :, :], PS[p % 2][:, :].rearrange("p (h q) -> p h q", h=2)).then_inc(G["d_q_sb"], 1)

            def d_rinv(p):
                for h in (2 * p, 2 * p + 1):
                    dve.wait_ge(G["d_exp"], 2 * h + 2)
                    v.reciprocal(dri[:, h % 8, :], dsm[:, h % 8, :]).then_inc(G["d_rinv"], 1)

            def d_ln(b):
                dve.wait_ge(G["d_y"], b + 1)
                for t in range(TPB):
                    ln_begin(3 * NT + 2 * b + t, add_rows(7, t * E, 2 * b + t))

            NP = B * PAIRS
            d_query(0)
            for p in range(NP + 1):
                b, q = divmod(p, PAIRS)
                if p + 1 < NP:
                    d_query(p + 1)
                if p < NP:
                    for h in (2 * p, 2 * p + 1):
                        dve.wait_ge(G["d_s"], h + 1)
                        bank = PS[2 + h % 2]
                        v.tensor_reduce(dmx[:, h % 8, 0:1], bank[:, 0:P], AX, ALU.max, negate=True).then_inc(G["d_max"], 1)
                        v.tensor_reduce(dmx[:, h % 8, 1:2], bank[:, P:3 * P], AX, ALU.max, negate=True).then_inc(G["d_max"], 1)
                if p > 0:
                    d_rinv(p - 1)
                if q == 3 and b > 0:
                    d_ln(b - 1)
                if q == 5 and b > 0:
                    for t in range(TPB):
                        ln_end(3 * NT + 2 * (b - 1) + t)
            d_ln(B - 1)
            for t in range(TPB):
                ln_end(3 * NT + 2 * (B - 1) + t)

            def e_ln(b):
                dve.wait_ge(G["e_y"], b + 1)
                for t in range(TPB):
                    ln_begin(4 * NT + 2 * b + t, add_rows(4, t * E, 2 * b + t))

            for b in range(B):
                s = b % 2
                dve.wait_ge(G["e_exp"], b + 1)
                link(v.tensor_scalar(eq[:, s, :], eq[:, s, :], 1.0, None, ALU.min))
                v.scalar_tensor_tensor(out=qf[:, s, :, :].rearrange("p k t -> p (k t)"), in0=PS[0][:, :], scalar=0.0,
                                       in1=eq[:, s, :], op0=ALU.max, op1=ALU.add).then_inc(G["e_qf"], 1)
                dve.wait_ge(G["e_eg"], 2 * b + 2)
                link(v.tensor_scalar(egt[:, s, :], egt[:, s, :], 1.0, None, ALU.add))
                dve.wait_ge(G["e_nd"], 2 * b + 2)
                link(v.scalar_tensor_tensor(out=den, in0=PS[3][:, :], scalar=Z_EPS, in1=egt[:, s, :], op0=ALU.add, op1=ALU.mult))
                link(v.reciprocal(den, den))
                v.tensor_tensor(eat[:, s, :, :].rearrange("p k t -> p (k t)"), PS[2][:, :], den, ALU.mult).then_inc(G["e_at"], 1)
                if b > 0:
                    e_ln(b - 1)
                    for t in range(TPB):
                        ln_end(4 * NT + 2 * (b - 1) + t)
            e_ln(B - 1)
            for t in range(TPB):
                ln_end(4 * NT + 2 * (B - 1) + t)

            dve.wait_ge(G["r_act"], 1)
            top = rcmp[:, :, 0, 0:1]
            link(v.tensor_reduce(rcmp[:, :, 0, 0], rt, AX, ALU.max))
            v.tensor_tensor(rt2, rt, top.broadcast_to([P, NT, NE]), ALU.subtract).then_inc(G["r_v"], 1)
            dve.wait_ge(G["r_act"], 2)
            link(v.tensor_reduce(rcm2[:, :, 0, 0], rt, AX, ALU.add))
            link(v.reciprocal(rcm2[:, :, 1, 0], rcm2[:, :, 0, 0]))
            link(v.tensor_tensor(wgt, rt, rcm2[:, :, 1, 0:1].broadcast_to([P, NT, NE]), ALU.mult))
            for t in range(NT):
                link(v.tensor_tensor(rcmp[:, t, :, :], wgt[:, t, :].unsqueeze(1).broadcast_to([P, NE, NE]),
                                     wgt[:, t, :].unsqueeze(2).broadcast_to([P, NE, NE]), ALU.is_gt))
                link(v.tensor_tensor(rcm2[:, t, :, :], wgt[:, t, :].unsqueeze(1).broadcast_to([P, NE, NE]),
                                     wgt[:, t, :].unsqueeze(2).broadcast_to([P, NE, NE]), ALU.is_equal))
                link(v.tensor_tensor(rcm2[:, t, :, :], rcm2[:, t, :, :], tri, ALU.mult))
            link(v.tensor_tensor(rcmp, rcmp, rcm2, ALU.add))
            link(v.tensor_reduce(rt2, rcmp, AX, ALU.add))
            link(v.tensor_scalar(rt2, rt2, float(TOPK), None, ALU.is_lt))
            link(v.tensor_tensor(wgt, wgt, rt2, ALU.mult))
            link(v.tensor_copy(acc, x_row[:, :, :]))

            def m_hidden(e, i):
                dve.wait_ge(G["m_silu"], e * (2 * FM) + i + 1)
                dve.wait_ge(G["m_ab"], e * (4 * FM) + 2 * i + 2)
                v.tensor_tensor(hT[:, (i // FM) % 2, i % FM, :], sa[:, i % 2, :], PS[2 + i % 2][:, :], ALU.mult).then_inc(G["m_h"], 1)

            def m_add(e, s, c, count):
                for j in range(2):
                    dve.wait_ge(G["m_y"], count + j)
                    for q in range(2):
                        t = 4 * c + 2 * j + q
                        v.scalar_tensor_tensor(out=acc[:, t, :], in0=PS[4 + j][:, q * E:(q + 1) * E],
                                               scalar=wgt[:, t, bass.ds(e + s, 1)], in1=acc[:, t, :],
                                               op0=ALU.mult, op1=ALU.add).then_inc(G["m_acc"], 1)

            with dve.Fori(0, NE // 2) as pair:
                e = pair * 2
                for k in range(5):
                    if k < 4:
                        for m in range(FM):
                            m_hidden(e, FM * k + m)
                    if k:
                        m_add(e, (k - 1) // 2, (k - 1) % 2, e * 4 + 2 * k - 1)
            dve.wait_ge(G["m_acc"], NE * NT)
            for t in range(0, NT, 2):
                for n in (t, t + 1):
                    ln_begin(5 * NT + n, lambda o: v.tensor_copy(o, acc[:, n, :]))
                for n in (t, t + 1):
                    ln_end(5 * NT + n)

        @block.tensor
        def _(pe):
            def mm(o, w, x, start=True, stop=True, **k):
                return nc.tensor.matmul(o, w, x, start=start, stop=stop, **k)

            def project(o, w, x):
                for k in range(KT):
                    ins = mm(o, w(k), x(k), start=k == 0, stop=k == KT - 1)
                return ins

            def to_xT(stage, b):
                pe.wait_ge(G["ln_done"], (0, 2, 3, 4)[stage] * NT + 2 * b + 2)
                for k in range(KT):
                    for t in range(TPB):
                        ins = mm(PS_xT[stage][:, k * S + t * P:k * S + (t + 1) * P], x_row[:, 2 * b + t, k * P:(k + 1) * P],
                                 ident, is_transpose=True)
                ins.then_inc(G["xT_raw"], 1)

            pe.wait_ge(G["const_set"], 6)

            def a_project(b):
                seq = lambda k: xT[:, k, b * S:(b + 1) * S]
                for n, (bank, s, freed) in enumerate(((0, "a_q", 5), (1, "a_k", 6))):
                    if b > 0:
                        pe.wait_ge(G["a_mask"], 8 * (b - 1) + freed)
                    for f in range(KT):
                        at = n * E + f * P
                        ins = project(PS[bank][:, f * S:(f + 1) * S], lambda k: w_qkv[:, k, at:at + P], seq)
                    ins.then_inc(G[s], 1)
                for bank, starts, freed in ((2, (0, P), 7), (3, (WIN,), 8)):
                    if b > 0:
                        pe.wait_ge(G["a_mask"], 8 * (b - 1) + freed)
                    for i, w in enumerate(starts):
                        ins = project(PS[bank][:, i * E:(i + 1) * E], lambda k: xT[:, k, b * S + w:b * S + w + P],
                                      lambda k: w_qkv[:, k, 2 * E:3 * E])
                    ins.then_inc(G["a_v"], 1)

            def a_scores(b):
                for i in range(8):
                    f, g, t = i // 4, (i // 2) % 2, i % 2
                    o = PS[i % 4]
                    if i == 0:
                        pe.wait_ge(G["a_q_sb"], b + 1)
                        pe.wait_ge(G["a_k_sb"], 2 * b + 2)
                    if i == 2:
                        pe.wait_ge(G["a_v_sb"], 6 * b + 6)
                    if i >= 4:
                        pe.wait_ge(G["a_mask"], 8 * b + i - 3)
                    if t == 0:
                        ins = mm(o[:, :], qT[:, f, 0:P], kmask[:, f, 4 * g:4 * g + 4, 0:P])
                    else:
                        for c in range(2):
                            ins = mm(o[c * WIN:(c + 1) * WIN, :], qT[:, f, P + c * WIN:P + (c + 1) * WIN],
                                     kmask[:, f, 4 * g:4 * g + 4, (c + 1) * WIN:(c + 1) * WIN + P])
                    ins.then_inc(G["a_s"], 1)

            def a_tail(b):
                for i in range(8):
                    pe.wait_ge(G["a_norm"], 8 * b + i + 1)
                    if 8 * b + i >= 2:
                        pe.wait_ge(G["a_pt_sb"], 8 * b + i - 1)
                    for h in range(4):
                        ins = mm(PS[4 + i % 2][:, h * P:(h + 1) * P], sm[:, i, h, :], ident, is_transpose=True)
                    ins.then_inc(G["a_pt"], 1)
                pe.wait_ge(G["a_pt_sb"], 8 * b + 8)
                pe.wait_ge(G["a_v_sb"], 6 * b + 6)
                if b >= 1:
                    pe.wait_ge(G["xT_done"], b)
                for f in range(KT):
                    for lo, hi, w in ((0, P, 0), (P, P + WIN, 1), (P + WIN, S, 2)):
                        for h in range(8):
                            i = 4 * f + 2 * (h // 4) + (w > 0)
                            a, z = (0, P) if w == 0 else ((w - 1) * WIN, w * WIN)
                            ins = mm(PS[6][:, f * S + lo:f * S + hi], vexp[:, w, f, h, :], PT[:, i, h % 4, a:z],
                                     start=h == 0, stop=h == 7)
                ins.then_inc(G["a_o"], 1)
                pe.wait_ge(G["a_o_sb"], b + 1)
                if b > 0:
                    pe.wait_ge(G["ln_var"], 2 * b)
                for t in range(TPB):
                    ins = project(PS[7][:, t * E:(t + 1) * E], lambda k: oT[:, k, t * P:(t + 1) * P], lambda k: w_o0[:, k, :])
                ins.then_inc(G["a_y"], 1)

            pe.wait_ge(G["ld_x"], 16)
            pe.wait_ge(G["ld_attn0"], 32)
            for b in range(B + 1):
                if b < B:
                    a_project(b)
                if b >= 2:
                    pe.wait_ge(G["a_o_sb"], b - 1)
                    to_xT(0, b - 2)
                if b >= 1:
                    a_tail(b - 1)
                if b < B:
                    a_scores(b)
            to_xT(0, B - 1)

            pe.wait_ge(G["ld_x0"], 64)
            pe.wait_ge(G["ld_x1"], 96)

            def b_project(b):
                seq = lambda k: xT[:, k, b * S:(b + 1) * S]
                pe.wait_ge(G["xT_done"], b + 1)
                for n, (bank, s, freed) in enumerate(((4, "b_q", "b_pt_a"), (5, "b_k", "b_pt_d"))):
                    if b > 0:
                        pe.wait_ge(G[freed], 4 * b)
                    else:
                        pe.wait_ge(G["a_pt_sb"], 8 * B)
                    for f in range(KT):
                        ins = project(PS[bank][:, f * S:(f + 1) * S], lambda k: w_x0[:, n, k, f * P:(f + 1) * P], seq)
                    ins.then_inc(G[s], 1)
                if b == 0:
                    pe.wait_ge(G["xT_done"], B)
                elif b <= 3:
                    pe.wait_ge(G["w_scale"], b)
                for t in range(TPB):
                    ins = project(PS[6][:, t * E:(t + 1) * E], lambda k: xT[:, k, b * S + t * P:b * S + (t + 1) * P],
                                  lambda k: w_x0[:, 2, k, :])
                ins.then_inc(G["b_v"], 1)

            def b_score(u, c):
                b, t = divmod(u, TPB)
                lo, hi = SCOLS[c]
                if u == 0:
                    pe.wait_ge(G["a_mask"], 8 * B)
                else:
                    pe.wait_ge(G["b_exp"], 4 * (u - 1) + c + 1)
                q = lambda k: xq[:, k, t * P:(t + 1) * P]
                n = min(hi, CTX) - lo
                ins = project(PS[c][:, 0:n], q, lambda k: ctxT[b % 2][:, k, lo:lo + n])
                if c == 3:
                    ins = project(PS[c][:, n:n + S], q, lambda k: xk[:, k, :])
                ins.then_inc(G["b_s"], 1)

            def b_transpose(u, c):
                if c == 0:
                    pe.wait_ge(G["b_exp"], 4 * u + 4)
                if c >= 2:
                    pe.wait_ge(G["b_pt_d" if c % 2 else "b_pt_a"], 2 * u + 1)
                elif u % 2:
                    pe.wait_ge(G["b_pt_d" if c % 2 else "b_pt_a"], 2 * u)
                else:
                    pe.wait_ge(G["x_kf"], CB * (u // 2 + 1))
                for j in range(4 if c < 3 else 3):
                    n = 4 * c + j
                    lo, hi = key_block(n)
                    ins = mm(PS[4 + c % 2][0:hi - lo, j * P:(j + 1) * P], prob[:, lo:hi], ident, is_transpose=True)
                ins.then_inc(G["b_t"], 1)

            def key_block(n):
                if n < CB:
                    return n * P, min((n + 1) * P, CTX)
                return CTX + (n - CB) * P, CTX + (n - CB + 1) * P

            def b_values(u):
                b = u // TPB
                pe.wait_ge(G["b_pt_a"], 2 * u + 2)
                pe.wait_ge(G["b_pt_d"], 2 * u + 2)
                if u % 2:
                    pe.wait_ge(G["b_o_sb"], u)
                else:
                    pe.wait_ge(G["x_m1_sb"], 2 * b + 2)
                for n in range(CB + TPB):
                    lo, hi = key_block(n)
                    rhs = ctxR[b % 2][0:hi - lo, n, 0:E] if n < CB else xv[:, n - CB, :]
                    ins = mm(PS[7][:, 0:E], probT[0:hi - lo, n, :], rhs, start=n == 0, stop=n == CB + TPB - 1)
                ins.then_inc(G["b_o"], 1)

            def b_outT(u):
                pe.wait_ge(G["b_o_sb"], u + 1)
                if u % 2 == 0:
                    pe.wait_ge(G["x_kvbd"], u // 2 + 1)
                for k in range(KT):
                    ins = mm(PS[7 if u % 2 else 6][:, k * P:(k + 1) * P], xo[:, k * P:(k + 1) * P], ident, is_transpose=True)
                ins.then_inc(G["b_ot"], 1)

            def b_project_out(u):
                pe.wait_ge(G["b_ot_sb"], u + 1)
                ins = project(PS[7 if u % 2 else 6][:, 0:E], lambda k: xoT[:, k, :], lambda k: w_x0[:, 3, k, :])
                ins.then_inc(G["b_y"], 1)

            def x_keys(b):
                s = b % 2

                def key_fill(t):
                    rows = P if t < CB - 1 else CLAST
                    if t == 0:
                        pe.wait_ge(G["b_q_sb"], b + 1)
                    elif t == 1:
                        pe.wait_ge(G["b_k_sb"], b + 1)
                    else:
                        pe.wait_ge(G["x_kf"], CB * b + t - 1)
                    ins = project(PS[4 + t % 2][0:rows, 0:E], lambda k: ctxT[s][:, k, t * P:t * P + rows],
                                  lambda k: w_x1[:, 0, k, :])
                    ins.then_inc(G["x_k"], 1)

                key_fill(0)
                key_fill(1)
                pe.wait_ge(G["b_v_sb"], b + 1)
                if b > 0:
                    pe.wait_ge(G["ln_var"], NT + 2 * b)
                else:
                    pe.wait_ge(G["ln_var"], NT)
                for t in range(CB):
                    rows = P if t < CB - 1 else CLAST
                    n = CB * b + t
                    pe.wait_ge(G["x_kf"], n + 1)
                    for h in range(KT):
                        ins = mm(PS[6 + h][:, 0:E + 1], kf[0:rows, n % 4, h * P:(h + 1) * P], ctxR[s][0:rows, t, :],
                                 start=t == 0, stop=t == CB - 1)
                    ins.then_inc(G["x_m1"], 1)
                    if t + 2 < CB:
                        key_fill(t + 2)

            def x_transpose(b):
                pe.wait_ge(G["x_m1_sb"], 2 * b + 2)
                for k in range(KT):
                    for h in range(KT):
                        ins = mm(PS[6][:, k * S + h * P:k * S + (h + 1) * P], m1[:, h, k * P:(k + 1) * P], ident, is_transpose=True)
                ins.then_inc(G["x_m1T"], 1)

            def x_values(b):
                pe.wait_ge(G["x_m1T_sb"], b + 1)
                for h in range(KT):
                    ins = project(PS[6][:, h * P:(h + 1) * P], lambda k: m1T[:, k, h * P:(h + 1) * P],
                                  lambda k: w_x1[:, 1, k, h * P:(h + 1) * P])
                ins.then_inc(G["x_kv"], 1)

            for b in range(B):
                b_project(b)
                if b > 0:
                    b_outT(2 * b - 1)
                pe.wait_ge(G[f"ld_ctx{b % 2}"], 48 * (b // 2 + 1))
                if b == 1:
                    pe.wait_ge(G["const_set"], 7)
                for c in range(4):
                    if c == 0:
                        pe.wait_ge(G["b_q_sb"], b + 1)
                    if c == 3:
                        pe.wait_ge(G["b_k_sb"], b + 1)
                    b_score(2 * b, c)
                if b > 0:
                    b_project_out(2 * b - 1)
                x_keys(b)
                for c in range(4):
                    b_transpose(2 * b, c)
                    b_score(2 * b + 1, c)
                x_transpose(b)
                b_values(2 * b)
                for c in range(4):
                    b_transpose(2 * b + 1, c)
                x_values(b)
                b_outT(2 * b)
                b_values(2 * b + 1)
                b_project_out(2 * b)
                if b < 3:
                    pe.wait_ge(G["w_abs"], b + 1)
                    pe.wait_ge(G["ln_var"], NT + 2 * b + 1)
                    mm(PS[6][:, 0:1], ones[:, :], wabs[:, b:b + 1]).then_inc(G["w_sum"], 1)
            b_outT(2 * B - 1)
            b_project_out(2 * B - 1)

            def f_transpose(b):
                pe.wait_ge(G["f_q"], 2 * b + 2)
                if b == 0:
                    pe.wait_ge(G["b_exp"], 8 * NT // 2)
                elif b >= 2:
                    pe.wait_ge(G["xT_done"], B + b - 1)
                o = PS[0][:, 0:S].bitcast(BF16)
                for k in range(KT):
                    for t in range(TPB):
                        ins = mm(o[:, k * S + t * P:k * S + (t + 1) * P], fq[:, t, k * P:(k + 1) * P], ident16[:, :], is_transpose=True)
                ins.then_inc(G["f_qT"], 1)

            def f_gate_up(t):
                b, j = divmod(t, TPB)
                pe.wait_ge(G["f_qT_sb"], b + 1)
                for c in range(2):
                    for n in range(2):
                        if t > 0:
                            pe.wait_ge(*((G["f_sig"], 2 * t + c - 1) if n == 0 else (G["f_h"], 2 * t + c - 1)))
                        if t == 0 and (n, c) == (1, 1):
                            pe.wait_ge(G["b_pt_a"], 2 * NT)
                        ins = project(PS[1 + 2 * c + n][:, :], lambda k: fqT[:, b % 2, k, j * P:(j + 1) * P],
                                      lambda k: w_ff[:, n, k * FF + c * 512:k * FF + (c + 1) * 512])
                        ins.then_inc(G["f_gu"], 1)

            def f_hiddenT(t):
                pe.wait_ge(G["f_hq"], t + 1)
                if t == 0:
                    pe.wait_ge(G["b_pt_d"], 2 * NT)
                else:
                    pe.wait_ge(G["f_hqT_sb"], t)
                o = PS[5][:, :].bitcast(BF16)
                for k in range(FF // P):
                    ins = mm(o[:, k * P:(k + 1) * P], hq[:, t % 2, k * P:(k + 1) * P], ident16[:, :], is_transpose=True)
                ins.then_inc(G["f_hqT"], 1)

            def f_down(t):
                pe.wait_ge(G["f_hqT_sb"], t + 1)
                pe.wait_ge(G["ln_var"], 2 * NT - 1 if t == 0 else 2 * NT + t)
                for k in range(FF // P):
                    ins = mm(PS[6][:, 0:E], hqT[:, t % 2, k, :], w_ff[:, 2, k * E:(k + 1) * E], start=k == 0, stop=k == FF // P - 1)
                ins.then_inc(G["f_y"], 1)

            def d_fold(t):
                if t == 0:
                    pe.wait_ge(G["ld_lat"], 96)
                    pe.wait_ge(G["ld_wq"], 32)
                    pe.wait_ge(G["ld_wo"], 16)
                    pe.wait_ge(G["ln_var"], 2 * NT)
                else:
                    pe.wait_ge(G["d_w_sb"], 2 * t)
                g = 2 * t // (H1 // KV1)
                for k in range(KT):
                    for i in range(2):
                        at = (2 * k + i) * LAT
                        mm(PS[7][:, at:at + LAT], w_qT[:, 2 * t + i, k * P:(k + 1) * P], w_kd[:, g, :])
                for i in range(2):
                    ins = mm(PS[7][i * LAT:(i + 1) * LAT, 256:256 + E], w_vd[:, g, :], w_oh[:, 2 * t + i, :])
                ins.then_inc(G["d_w"], 1)

            pe.wait_ge(G["w_tern"], 3)
            for t in range(NT + 1):
                if t < NT:
                    if t % TPB == 0:
                        f_transpose(t // TPB)
                    f_gate_up(t)
                if t > 0:
                    f_down(t - 1)
                if t < NT:
                    d_fold(t)
                    f_hiddenT(t)
                if t >= 2 and t % TPB == 0:
                    pe.wait_ge(G["f_qT_sb"], t // TPB)
                    to_xT(1, t // TPB - 1)

            def d_latent(b):
                seq = lambda k: xT[:, k, b * S:(b + 1) * S]
                pe.wait_ge(G["xT_done"], B + b + 1)
                if b == 0:
                    pe.wait_ge(G["d_w_sb"], 2 * PAIRS)
                elif b == 1:
                    pe.wait_ge(G["d_k_sb"], 2)
                else:
                    pe.wait_ge(G["ln_var"], 3 * NT + 2 * (b - 1))
                project(PS[7][0:LAT, 0:S], lambda k: w_kvc[:, k, :], seq)
                for t in range(TPB):
                    ins = project(PS[7][:, S + t * LAT:S + (t + 1) * LAT], lambda k: xT[:, k, b * S + t * P:b * S + (t + 1) * P],
                                  lambda k: w_kvc[:, k, :])
                ins.then_inc(G["d_c"], 1)

            def d_keys(b, h):
                pe.wait_ge(G["d_c_sb"], 2 * b + 2)
                if h == 1:
                    pe.wait_ge(G["d_k_sb"], 2 * b + 1)
                for i in range(2):
                    ins = mm(PS[7][:, i * S:(i + 1) * S], w_ki[:, 2 * h + i, :], cT[0:LAT, :])
                ins.then_inc(G["d_k"], 1)

            def d_query(p):
                b, q = divmod(p, PAIRS)
                pe.wait_ge(G["xT_done"], B + b + 1)
                if p == 0:
                    pe.wait_ge(G["xT_done"], 2 * B)
                elif p == 1:
                    pe.wait_ge(G["f_sig"], 2 * NT)
                else:
                    pe.wait_ge(G["d_q_sb"], p - 1)
                for i in range(2):
                    ins = project(PS[p % 2][:, i * S:(i + 1) * S], lambda k: w_qe[:, k, 2 * q + i, :],
                                  lambda k: xT[:, k, b * S:(b + 1) * S])
                ins.then_inc(G["d_q"], 1)

            def d_scores(h):
                p, b, g = h // 2, h // H1, (h % H1) // (H1 // KV1)
                pe.wait_ge(G["d_q_sb"], p + 1)
                pe.wait_ge(G["d_k_sb"], 2 * b + 2)
                o = PS[2 + h % 2]
                if h < 2:
                    pe.wait_ge(*((G["f_h"], 2 * NT) if h == 0 else (G["f_sig"], 2 * NT)))
                else:
                    pe.wait_ge(G["d_exp"], 2 * (h - 2) + 2)
                q = qe[:, p % 3, h % 2, :]
                k = kg[:, b % 2, g, :]
                mm(o[:, 0:3 * P], ident16[:, :], cbias[:, :], stop=False)
                mm(o[:, 0:P], q[:, 0:P], k[:, 0:P], start=False, stop=False)
                mm(o[:, P:3 * P], q[:, P:S], k, start=False, stop=True).then_inc(G["d_s"], 1)

            def d_transpose(h):
                pe.wait_ge(G["d_norm"], 2 * h + 2)
                if h < 2:
                    pe.wait_ge(*((G["f_h"], 2 * NT) if h == 0 else (G["f_hqT_sb"], NT)))
                else:
                    pe.wait_ge(G["d_t_sb"], h - 1)
                for c in range(3):
                    ins = mm(PS[4 + h % 2][:, c * P:(c + 1) * P], dp[:, h % 6, c, :], ident, is_transpose=True)
                ins.then_inc(G["d_t"], 1)

            def d_values(p):
                b = p // PAIRS
                pe.wait_ge(G["d_t_sb"], 2 * p + 2)
                if p == 0:
                    pe.wait_ge(G["ln_var"], 3 * NT)
                else:
                    pe.wait_ge(G["d_o_sb"], p)
                for h in (2 * p, 2 * p + 1):
                    o = PS[6][(h % 2) * LAT:(h % 2 + 1) * LAT, :]
                    mm(o[:, 0:S], cR[:, b % 2, 0, :], dpT[:, h % 4, 0:S], stop=False)
                    ins = mm(o[:, P:S], cR[:, b % 2, 1, :], dpT[:, h % 4, S:3 * P], start=False)
                ins.then_inc(G["d_o"], 1)

            def d_out(b):
                pe.wait_ge(G["d_o_sb"], PAIRS * (b + 1))
                if b > 0:
                    pe.wait_ge(G["xT_done"], 2 * B + b)
                for t in range(TPB):
                    for i in range(PAIRS):
                        ins = mm(PS[7][:, t * E:(t + 1) * E], doT[:, i, t * P:(t + 1) * P], w_vo[:, i, :], start=i == 0, stop=i == PAIRS - 1)
                ins.then_inc(G["d_y"], 1)

            pe.wait_ge(G["ld_cbias"], 16)
            pe.wait_ge(G["d_rot"], 6 * (1 + KT))
            d_latent(0)
            d_keys(0, 0)
            d_keys(0, 1)
            d_query(0)
            NP = B * PAIRS
            for p in range(NP + 4):
                b, q = divmod(p, PAIRS)
                if q == 3 and b > 0:
                    d_out(b - 1)
                if q == 4 and b + 1 < B:
                    d_latent(b + 1)
                if p + 1 < NP:
                    if q == 5 and b + 1 < B:
                        d_keys(b + 1, 0)
                        d_keys(b + 1, 1)
                    d_query(p + 1)
                if q == 6 and b > 0:
                    pe.wait_ge(*((G["d_k_sb"], 2 * b + 4) if b + 1 < B else (G["ln_var"], 3 * NT + 2 * b)))
                    to_xT(2, b - 1)
                if p < NP:
                    d_scores(2 * p)
                    d_scores(2 * p + 1)
                if 2 <= p < NP + 2:
                    d_transpose(2 * p - 4)
                    d_transpose(2 * p - 3)
                if 3 <= p < NP + 3:
                    d_values(p - 3)
            pe.wait_ge(G["ln_var"], 4 * NT)
            to_xT(2, B - 1)

            def e_project(b):
                seq = lambda k: xT[:, k, b * S:(b + 1) * S]
                pe.wait_ge(G["xT_done"], 2 * B + b + 1)
                for n in range(2):
                    if b > 0:
                        pe.wait_ge(*((G["e_qf"], b) if n == 0 else (G["e_eg"], 2 * b)))
                    else:
                        pe.wait_ge(G["d_q_sb"], NP)
                    for f in range(KT):
                        ins = project(PS[n][:, f * S:(f + 1) * S], lambda k: w_x1[:, 2 + n, k, f * P:(f + 1) * P], seq)
                    ins.then_inc(G["e_qg"], 1)

            def e_attend(b):
                pe.wait_ge(G["e_qf"], b + 1)
                pe.wait_ge(*((G["e_at"], b) if b else (G["d_exp"], 4 * NP)))
                for bank, w in ((2, kvbd), (3, dsum)):
                    for f in range(KT):
                        ins = mm(PS[bank][:, f * S:(f + 1) * S], w[:, b, f, :], qf[:, b % 2, f, :])
                    ins.then_inc(G["e_nd"], 1)

            def e_out(b):
                pe.wait_ge(G["e_at"], b + 1)
                pe.wait_ge(*((G["ln_var"], 4 * NT + 2 * b) if b else (G["d_t_sb"], 2 * NP)))
                for t in range(TPB):
                    ins = project(PS[4][:, t * E:(t + 1) * E], lambda k: eat[:, b % 2, k, t * P:(t + 1) * P], lambda k: w_x1[:, 4, k, :])
                ins.then_inc(G["e_y"], 1)

            for b in range(B + 2):
                if b < B:
                    e_project(b)
                    e_attend(b)
                if 1 <= b <= B:
                    e_out(b - 1)
                if b >= 2:
                    pe.wait_ge(*((G["xT_done"], 3 * B + b - 2) if b > 2 else (G["d_t_sb"], 2 * NP)))
                    to_xT(3, b - 2)

            pe.wait_ge(G["xT_done"], 4 * B)
            pe.wait_ge(G["d_o_sb"], NP)
            for t in range(NT):
                ins = project(PS[6][:, t * NE:(t + 1) * NE], lambda k: xT[:, k, t * P:(t + 1) * P], lambda k: w_rt[:, k, :])
            ins.then_inc(G["r_log"], 1)

            w13 = lambda s, n, k, m: w_e[s][:, (n * KT + k) * FI + m * P:(n * KT + k) * FI + (m + 1) * P]
            w2 = lambda s, m: w_e[s][:, 2 * KT * FI + m * E:2 * KT * FI + (m + 1) * E]

            def m_gate_up(e, k):
                s, c = divmod(k, 2)
                for m in range(FM):
                    i = FM * k + m
                    for n in range(2):
                        if i >= 2:
                            pe.wait_ge(G["m_silu" if n == 0 else "m_h"], e * (2 * FM) + i - 1)
                        ins = project(PS[2 * n + m % 2][:, :], lambda q: w13(s, n, q, m), lambda q: xT[:, q, c * 512:(c + 1) * 512])
                        ins.then_inc(G["m_ab"], 1)

            def m_down(e, k):
                s, c = divmod(k, 2)
                pe.wait_ge(G["m_h"], e * (2 * FM) + FM * (k + 1))
                for j in range(2):
                    if k:
                        pe.wait_ge(G["m_acc"], e * 8 + 4 * (k - 1) + 2 * (j + 1))
                    for q in range(2):
                        t = 2 * j + q
                        for m in range(FM):
                            ins = mm(PS[4 + j][:, q * E:(q + 1) * E], hT[:, k % 2, m, t * P:(t + 1) * P], w2(s, m),
                                     start=m == 0, stop=m == FM - 1)
                    ins.then_inc(G["m_y"], 1)

            pe.wait_ge(G["e_at"], B)
            pe.wait_ge(G["ln_var"], 5 * NT)
            with pe.Fori(0, NE // 2) as pair:
                e = pair * 2
                for k in range(4):
                    if k % 2 == 0:
                        pe.wait_ge(G[f"m_w{k // 2}"], e * 24 + 48)
                    m_gate_up(e, k)
                    if k:
                        m_down(e, k - 1)
                m_down(e, 3)
                pe.wait_ge(G["m_acc"], e * 8 + 16)


def pack(w):
    return np.ascontiguousarray(w.reshape(-1, P, w.shape[1]).transpose(1, 0, 2))


def kernel(**inputs):
    import concourse.bacc as bacc
    from concourse.bass_utils import run_bass_kernel_spmd as run

    i = {k: np.asarray(v) for k, v in inputs.items() if k != "mask_BxSx4224_bf0"}
    x = i["x"].reshape(B * S, E)
    a = {"x": x, "xT": pack(x.T), "cst": constants(), "cbias": causal_bias()}
    a["w_qkv"] = pack(i["L0_attn_w_qkv"].T)
    a["w_o0"] = pack(i["L0_attn_w_out"].T)
    for n, k in enumerate("qkvo"):
        a[f"w_x0_{n}"] = pack(i[f"L0_xattn_w{k}"].T)
    a["ctx"] = i["ctx_2048"]
    a["ctxT"] = np.ascontiguousarray(i["ctx_2048"].transpose(0, 2, 1).reshape(B, KT, P, CTX).transpose(0, 2, 1, 3))
    wkv = i["L1_xattn_Wkv"]
    for n, w in enumerate((wkv[:E], wkv[E:], i["L1_xattn_Wq"], i["L1_xattn_Wg"], i["L1_xattn_Wo"])):
        a[f"w_x1_{n}"] = pack(w.T)
    a["bg"] = np.ascontiguousarray(i["L1_xattn_bg"].reshape(KT, P).T)
    for n, k in enumerate(("gate", "up", "down")):
        a[f"w_f{n}"] = pack(i[f"L0_ffn_w_{k}"].T).reshape(P, 2 * FF)
    a["w_kvc"] = pack(i["L1_attn_Wkvc"])
    a["eye4"] = np.ascontiguousarray(np.broadcast_to(np.eye(LAT, dtype=np.float32)[:, None], (LAT, KV1, LAT)))
    halves = lambda w, h: w.reshape(-1, h, RH, 2).transpose(0, 1, 3, 2).reshape(-1, h, RD)
    a["w_kr"] = np.ascontiguousarray(halves(i["L1_attn_Wkrope"], KV1))
    a["w_kd"] = np.ascontiguousarray(i["L1_attn_Wkdec"].reshape(LAT, KV1, HD).transpose(2, 1, 0))
    a["w_vd"] = np.ascontiguousarray(i["L1_attn_Wvdec"].reshape(LAT, KV1, HD).transpose(2, 1, 0))
    a["w_rt"] = pack(i["L1_ffn_w_gate"])
    a["w_qT"] = np.ascontiguousarray(i["L1_attn_Wq"].reshape(E, H1, HD).transpose(2, 1, 0))
    a["w_qr"] = np.ascontiguousarray(halves(i["L1_attn_Wqrope"], H1).reshape(KT, P, H1, RD).transpose(1, 0, 2, 3))
    a["w_oh"] = np.ascontiguousarray(i["L1_attn_Wo"].reshape(H1, HD + RD, E)[:, :HD].transpose(1, 0, 2))
    per = lambda w: np.ascontiguousarray(w.reshape(NE, -1, P, w.shape[2]).transpose(2, 0, 1, 3).reshape(P, NE, -1))
    a["e0"], a["e1"], a["e2"] = per(i["L1_ffn_w1"]), per(i["L1_ffn_w3"]), per(i["L1_ffn_w2"])

    nc = bacc.Bacc("TRN2", target_bir_lowering=False, num_devices=1)
    dr = {k: nc.dram_tensor(f"in_{k}", v.shape, F32, kind="ExternalInput").ap() for k, v in a.items()}
    out = nc.dram_tensor("out", (B * S, E), F32, kind="ExternalOutput").ap()
    build(nc, dr, out)
    r = run(nc, [{f"in_{k}": v for k, v in a.items()}], core_ids=[0])
    return r.results[0]["out"].reshape(B, S, E)
```

```python
import numpy as np
import concourse.bass as bass
from concourse import mybir
from contextlib import ExitStack

F32 = mybir.dt.float32
BF16 = mybir.dt.bfloat16
U32 = mybir.dt.uint32
I32 = mybir.dt.int32
ACT = mybir.ActivationFunctionType
ALU = mybir.AluOpType
AX = mybir.AxisListType.X

P = 128
B, S, E = 4, 256, 256
KT = E // P
TPB = S // P
NT = B * TPB
LN_EPS = 1e-5
H0, D0, WIN = 16, 16, 64
FILLS = 8
D0P = 32
CTX = 1601
CB = -(-CTX // P)
CLAST = CTX - (CB - 1) * P
KEYS = CTX + S
SCOLS = [(0, 512), (512, 1024), (1024, 1536), (1536, KEYS)]
FF = 1024
QMAX = 127.0
Q_EPS = 1e-5
MAGIC = 1.5 * 2.0 ** 23
H1, KV1, HD, RD, LAT = 16, 4, 128, 64, 64
RH = RD // 2
SC1 = float(HD + RD) ** -0.5
PAIRS = H1 // 2
Z_EPS = 1e-6
NE, TOPK, FI = 8, 2, 512
CAP = 30.0
FM = FI // P
TOKENS = B * S
TILES = TOKENS * TOPK // P + NE - 1
ROWS = NE * TOKENS + (TILES - TOKENS * TOPK // P) * P
EXP_W = 2 * KT * FI + FM * E

C_ID, C_WMASK, C_BLK, C_HM, C_TRI, C_COS, C_SIN, C_THR, C_EROW, C_TILE, C_N = (
    int(n) for n in np.cumsum([0, P, 2 * P, P, 8, NE * NE, H1 * RH, H1 * RH, NE, NE, TILES]))
NEG = -1e30


def constants():
    c = np.zeros((P, C_N), np.float32)
    c[:, C_ID:C_ID + P] = np.eye(P)
    q, k = np.arange(P)[:, None], np.arange(P)[None, :]
    d0 = q - k
    d1 = (q % WIN) + WIN - k
    c[:, C_WMASK:C_WMASK + P] = np.where((d0 >= 0) & (d0 <= WIN), 0, NEG)
    c[:, C_WMASK + P:C_WMASK + 2 * P] = np.where((d1 >= 0) & (d1 <= WIN), 0, NEG)
    c[:, C_BLK:C_BLK + P] = (q // D0) == (k // D0)
    c[:, C_HM:C_HM + 8] = (np.arange(P)[:, None] // D0) == np.arange(8)[None, :]
    c[:, C_TRI:C_TRI + NE * NE] = (np.arange(NE)[None, :] < np.arange(NE)[:, None]).reshape(1, -1)
    c[:, C_THR:C_THR + NE] = P * np.arange(NE)
    c[:, C_EROW:C_EROW + NE] = TOKENS * np.arange(NE) + 1
    c[:, C_TILE:C_TILE + TILES] = np.arange(TILES)
    freqs = (1.0 / np.float32(10000.0) ** (np.arange(0, RD, 2, dtype=np.float32) / np.float32(RD))).astype(np.float32)
    ang = np.outer(np.arange(H1, dtype=np.float32), freqs).astype(np.float32)
    c[:, C_COS:C_COS + H1 * RH] = np.cos(ang).reshape(1, -1)
    c[:, C_SIN:C_SIN + H1 * RH] = np.sin(ang).reshape(1, -1)
    return c


def causal_bias():
    d = np.where(np.arange(P)[:, None] >= np.arange(P)[None, :], 0, NEG)
    return np.concatenate([d, np.zeros((P, P)), d], 1).astype(np.float32)


def build(nc, d, xs, ys, out):
    with ExitStack() as ctx:
        def sb(name, shape, dt=F32):
            return ctx.enter_context(nc.sbuf_tensor(name, shape, dt))

        def sem(name):
            return ctx.enter_context(nc.semaphore(name))

        class Region:

            def __init__(self, base, words):
                self.base, self.words = base, words
                self.at = 0

            def start(self, at=0):
                self.at = at

            def cut(self, *shape, dt=F32):
                n = int(np.prod(shape))
                words = -(-n // 2) if dt == BF16 else n
                assert self.at + words <= self.words, (self.at, words, self.words)
                v = arena[:, self.base + self.at:self.base + self.at + words]
                self.at += words
                if dt != F32:
                    v = v.bitcast(dt)
                names = " ".join("abcd"[:len(shape)])
                if len(shape) == 1:
                    return v
                return v.rearrange(f"p ({names}) -> p {names}", **dict(zip("abcd", shape)))

        PS = [ctx.enter_context(nc.psum_tensor(f"bank{i}", [P, 512], F32)) for i in range(8)]

        cst = sb("cst", [P, C_N])
        ident = cst[:, C_ID:C_ID + P]
        blk = cst[:, C_BLK:C_BLK + P]
        hmask = cst[:, C_HM:C_HM + 8]
        tri = cst[:, C_TRI:C_TRI + NE * NE].rearrange("p (a b) -> p a b", a=NE)
        ident16 = sb("ident16", [P, P], BF16)
        cbias = sb("cbias", [P, 3 * P], BF16)
        ones = sb("ones", [P, P])
        magic = sb("magic", [P, 1])
        mhalf = sb("mhalf", [P, 1])
        x_row = sb("x_row", [P, NT, E])
        xT = sb("xT", [P, KT, B * S])
        res = sb("res", [P, 4, E])
        stats = sb("stats", [P, 4, 6])
        mv = sb("mv", [P, 4, 2])
        rstd = sb("rstd", [P, 4])
        w_qkv = sb("w_qkv", [P, KT, 3 * E])
        w_x0 = sb("w_x0", [P, 4, KT, E])
        w_x1 = sb("w_x1", [P, 5, KT, E])
        bg = sb("bg", [P, KT])
        nbg = sb("nbg", [P, KT])
        kvbd = sb("kvbd", [P, B, KT, P])
        dsum = sb("dsum", [P, B, KT, P])
        w_ff = sb("w_ff", [P, 3, 2 * FF], BF16)
        wabs = sb("wabs", [P, 3])
        wsc = sb("wsc", [P, 3])
        wsi = sb("wsi", [P, 3])
        w_kvc = sb("w_kvc", [P, KT, LAT])
        w_kr = sb("w_kr", [LAT, KV1, RD])
        w_ki = sb("w_ki", [LAT, KV1, P])
        w_kd = sb("w_kd", [P, KV1, LAT])
        w_vd = sb("w_vd", [P, KV1, LAT])
        w_rt = sb("w_rt", [P, KT, NE])

        CT_W, CR_W = KT * CTX, CB * (E + 1)
        SLOT = CT_W + CR_W
        N2, N1, N3 = 3 * 2 * FF, 2 * SLOT, 13312
        arena = sb("arena", [P, N2 + N1 + N3])
        U2, U1, U3 = Region(0, N2), Region(N2, N1), Region(N2 + N1, N3)
        ctxT, ctxR = [], []
        for s in range(2):
            U1.start(s * SLOT)
            ctxT.append(U1.cut(KT, CTX))
            ctxR.append(U1.cut(CB, E + 1))
        U1.start(SLOT)
        vpad = U1.cut(2, 3, H0 * D0P)
        w_o0 = U1.cut(H0 * D0P // P, E)
        oT = U1.cut(H0 * D0P // P, S)
        wmask16 = U1.cut(2, P, dt=BF16)
        zeros = U1.cut(E)
        U1.start(0)
        w_qe = U1.cut(KT, H1, P)
        w_vo = U1.cut(PAIRS, E)
        w_qT = U1.cut(H1, E)
        w_qr = U1.cut(KT, H1, RD)
        w_rot = U1.cut(H1, RH)
        w_f32 = U2.cut(3, 2 * FF)
        U2.start(0)
        w_oh = U2.cut(H1, E)
        qT = U3.cut(2, KT, S)
        kmask = U3.cut(2, KT, 8, S)
        sm = U3.cut(4, 4, P)
        PT = U3.cut(4, 4, P)
        U3.start(0)
        xq = U3.cut(KT, S)
        xk = U3.cut(KT, S)
        xv = U3.cut(TPB, E)
        prob = U3.cut(KEYS + 1)[:, 0:KEYS]
        probT = U3.cut(CB + TPB, P)
        ek = U3.cut(4, E)
        kf = U3.cut(4, E)
        m1 = U3.cut(KT, E + 2)
        m1T = U3.cut(KT, E)
        xo = U3.cut(E)
        xoT = U3.cut(KT, P)
        qtmp = U3.cut(2 * FF)
        U3.start(0)
        fr = U3.cut(2, E)
        fq = U3.cut(2, E, dt=BF16)
        fqT = U3.cut(2, KT, S, dt=BF16)
        sg = U3.cut(2, 512)
        hh = U3.cut(2, FF)
        hr = U3.cut(FF)
        hq = U3.cut(2, FF, dt=BF16)
        hqT = U3.cut(2, FF // P, P, dt=BF16)
        U3.start(0)
        cT = U3.cut(S)
        cR = U3.cut(2, TPB, LAT)
        kg = U3.cut(2, KV1, S)
        qe = U3.cut(3, 2, S)
        dp = U3.cut(6, 3, P)
        dpT = U3.cut(4, 3 * P)
        doT = U3.cut(PAIRS, S)
        w_all = arena[:, 0:NE * EXP_W].rearrange("p (e w) -> p e w", e=NE)
        late = Region(NE * EXP_W, N2 + N1 + N3 - NE * EXP_W)
        eq = late.cut(2, 512)
        qf = late.cut(2, KT, S)
        egt = late.cut(2, 512)
        den = late.cut(512)
        eat = late.cut(2, KT, S)
        router_at = late.at
        late.start(0)
        xg = late.cut(2, E)
        xgT = late.cut(2, KT, P)
        sa = late.cut(FI)
        hs = late.cut(FI)
        hT = late.cut(FM, P)
        yt = late.cut(2, E)
        late.start(router_at)
        rt = late.cut(NT, NE)
        rt2 = late.cut(NT, NE)
        wgt = late.cut(NT, NE)
        slots = late.cut(NT, NE)
        rtop = late.cut(NT)
        rsm = late.cut(NT)
        rsi = late.cut(NT)
        shi = late.cut(NT)
        ssm = late.cut(NT)
        w_lo, w_hi = late.cut(NT), late.cut(NT)
        rcmp = late.cut(NE, NE)
        rcm2 = late.cut(NE, NE)
        kept16 = late.cut(NT, NE, dt=BF16)
        before16 = late.cut(P, dt=BF16)
        ones16 = late.cut(P, dt=BF16)
        tok_rows = late.cut(2, NT, dt=U32)
        out_rows = late.cut(2, NT, dt=U32)
        chosen = late.cut(NT, NE)
        etiles = late.cut(NE)
        eends = late.cut(NE)
        eskip = late.cut(NE)
        tcmp = late.cut(TILES, NE)
        tab = late.cut(2, TILES)
        table = late.cut(2, TILES, dt=I32)
        y_lo = arena[:, 0:NT * E].rearrange("p (t e) -> p t e", t=NT)
        y_hi = arena[:, NT * E:2 * NT * E].rearrange("p (t e) -> p t e", t=NT)
        mx = sb("mx", [P, 8, 4])
        rsum = sb("rsum", [P, 8, 4])
        rinv = sb("rinv", [P, 8, 4])
        bmx = sb("bmx", [P, 8])
        bsum = sb("bsum", [P, 8])
        fs = sb("fs", [P, 4, 8])
        fh = sb("fh", [P, 2, 8])
        dmx = sb("dmx", [P, 8, 2])
        dsm = sb("dsm", [P, 8, 2])
        dri = sb("dri", [P, 8, 2])

        names = """ld_const ld_x ld_xrow ld_attn0 ld_x0 ld_x1 ld_ctx0 ld_ctx1 ld_ffn ld_lat ld_cbias ld_wq ld_wo ld_out
            const_set ln_sum ln_var ln_rstd ln_done xT_raw xT_done
            a_q a_k0 a_k1v0 a_v12 a_q_sb a_k0_sb a_k1_sb a_v_sb a_s a_max a_exp a_rinv a_norm
            a_pt a_pt_even a_pt_odd a_o a_o_sb a_y ld_rest ld_wo0
            b_q b_k b_v b_q_sb b_k_sb b_v_sb b_s b_max b_exp b_rinv b_t b_pt_a b_pt_d b_o b_o_sb b_ot b_ot_sb b_y
            x_k x_exp x_kf x_m1 x_m1_sb x_m1T x_m1T_sb x_kv x_kvbd
            w_abs w_sum w_scale w_round w_tern
            f_sc f_round f_q f_qT f_qT_sb f_gu f_sig f_h f_hsc f_hround f_hq f_hqT f_hqT_sb f_y
            d_w d_w_sb d_c d_c_sb d_k d_k_sb d_rot d_q d_q_sb d_s d_max d_exp d_rinv d_norm
            d_t d_t_sb d_o d_o_sb d_y
            e_qg e_exp e_eg e_qf e_nd e_at e_y
            ld_zero ld_exp r_set r_log r_act r_v r_kept r_count r_rows r_out_rows r_scat r_table
            m_x0 m_x1 m_xT m_xT_sb m_g m_u m_silu m_h m_hT m_hT_sb m_y m_y_sb m_st0 m_st1
            y_got0 y_got1 y_got2 y_got3 y_got4 y_got5 y_got6 y_got7
            pe_step dve_step pool_step act_step""".split()
        G = {n: sem(n) for n in names}

        block = ctx.enter_context(nc.Block())
        PS_xT = [PS[5], PS[0], PS[7], PS[5]]

        @block.sync
        def _(sp):
            def load(dst, src, s):
                sp.dma_start(dst, src).then_inc(G[s], 16)

            load(xT[:, :, 0:S], d["xT"][:, :, 0:S], "ld_x")
            load(w_qkv[:, :, :], d["w_qkv"], "ld_attn0")
            load(cst[:, :], d["cst"], "ld_const")
            load(xT[:, :, S:B * S], d["xT"][:, :, S:B * S], "ld_rest")
            load(w_o0, d["w_o0"], "ld_wo0")
            load(x_row[:, :, :], d["x"].rearrange("(t p) e -> p t e", p=P), "ld_xrow")
            for n in range(4):
                load(w_x0[:, n, :, :], d[f"w_x0_{n}"], "ld_x0")

            def load_ctx(b):
                s = b % 2
                src = d["ctx"][b]
                load(ctxT[s], d["ctxT"][b], f"ld_ctx{s}")
                load(ctxR[s][:, 0:CB - 1, 0:E], src[0:(CB - 1) * P, :].rearrange("(t p) e -> p t e", p=P), f"ld_ctx{s}")
                load(ctxR[s][0:CLAST, CB - 1, 0:E], src[(CB - 1) * P:CTX, :], f"ld_ctx{s}")

            load_ctx(0)
            for n in range(5):
                load(w_x1[:, n, :, :], d[f"w_x1_{n}"], "ld_x1")
            load(bg[:, :], d["bg"], "ld_x1")
            for n in range(3):
                load(w_f32[:, n, :], d[f"w_f{n}"], "ld_ffn")
            sp.wait_ge(G["const_set"], 6)
            xs_tiles = xs.rearrange("(t p) e -> p t e", p=P)
            for at in range(0, ROWS // P, NT):
                n = min(NT, ROWS // P - at)
                load(xs_tiles[:, at:at + n, :], zeros.unsqueeze(1).broadcast_to([P, n, E]), "ld_zero")
            sp.wait_ge(G["a_y"], B)
            sp.wait_ge(G["ld_zero"], 16 * (NE + 1))
            load_ctx(1)
            load(w_kvc[:, :, :], d["w_kvc"], "ld_lat")
            load(w_ki[:, :, 0:LAT], d["eye4"], "ld_lat")
            load(w_kr[:, :, :], d["w_kr"], "ld_lat")
            load(w_kd[:, :, :], d["w_kd"], "ld_lat")
            load(w_vd[:, :, :], d["w_vd"], "ld_lat")
            load(w_rt[:, :, :], d["w_rt"], "ld_lat")
            for b in range(2, B):
                sp.wait_ge(G["b_o"], 2 * (b - 1))
                load_ctx(b)
            sp.wait_ge(G["w_tern"], 3)
            load(w_oh, d["w_oh"], "ld_wo")
            sp.wait_ge(G["b_o"], 2 * B)
            load(w_qT, d["w_qT"], "ld_wq")
            load(w_qr, d["w_qr"], "ld_wq")
            for n in range(NE):
                if n == 0:
                    sp.wait_ge(G["d_w"], NT)
                if (n + 1) * EXP_W > N2 >= n * EXP_W:
                    sp.wait_ge(G["d_y"], B)
                    sp.wait_ge(G["d_o"], B * PAIRS)
                load(w_all[:, n, :], d["w_exp"][:, n, :], "ld_exp")

            def load_rows(i, slot):
                row = sp.value_load(table[0:1, 1, bass.ds(i, 1)], min_val=0, max_val=ROWS - P)
                sp.dma_start(xg[:, slot, :], xs[bass.ds(row, P), :]).then_inc(G[f"m_x{slot}"], 16)

            def store_rows(i, slot):
                sp.wait_ge(G["m_y_sb"], i + 1)
                sp.dma_start(ys[bass.ds(i * P, P), :], yt[:, slot, :]).then_inc(G[f"m_st{slot}"], 16)

            def m_step(i, slot, first=False, last=False):
                if not last:
                    sp.wait_ge(G["m_xT"], i + 1)
                    load_rows(i + 2, slot)
                if not first:
                    store_rows(i - 1, 1 - slot)

            sp.wait_ge(G["r_table"], 2)
            sp.wait_ge(G["r_scat"], 16 * TOPK * NT)
            load_rows(0, 0)
            load_rows(1, 1)
            m_step(0, 0, first=True)
            m_step(1, 1)
            m_step(2, 0)
            with sp.Fori(1, TILES // 2 - 1) as h:
                m_step(h * 2 + 1, 1)
                m_step(h * 2 + 2, 0)
            m_step(TILES - 2, 1, last=True)
            m_step(TILES - 1, 0, last=True)
            store_rows(TILES - 1, 0)
            sp.wait_ge(G["m_st0"], 16 * (TILES // 2 + 1))
            sp.wait_ge(G["m_st1"], 16 * (TILES // 2))
            for t in range(NT):
                sp.wait_ge(G["ln_done"], 5 * NT + t + 1)
                sp.dma_start(out[t * P:(t + 1) * P, :], x_row[:, t, :]).then_inc(G["ld_out"], 16)
            sp.wait_ge(G["ld_out"], 16 * NT)

        @block.gpsimd
        def _(pool):
            g = nc.gpsimd
            g.memset(vpad, 0.0).then_inc(G["const_set"], 1)
            g.memset(ones[:, :], 1.0).then_inc(G["const_set"], 1)
            g.memset(magic[:, :], MAGIC).then_inc(G["const_set"], 1)
            g.memset(mhalf[:, :], -0.5).then_inc(G["const_set"], 1)
            g.memset(ctxR[0][:, :, E:E + 1], 1.0).then_inc(G["const_set"], 1)
            g.memset(zeros, 0.0).then_inc(G["const_set"], 1)
            pool.wait_ge(G["ld_const"], 16)
            g.tensor_copy(ident16[:, :], ident).then_inc(G["const_set"], 1)
            g.tensor_copy(wmask16, cst[:, C_WMASK:C_WMASK + 2 * P].rearrange("p (t k) -> p t k", t=2)).then_inc(G["const_set"], 1)
            pool.dma_start(cbias[:, :], d["cbias"]).then_inc(G["ld_cbias"], 16)
            steps = [0]

            def rstd_of(n):
                s = n % 4
                pool.wait_ge(G["ln_var"], n + 1)
                g.tensor_scalar(rstd[:, s:s + 1], mv[:, s, 1:2], LN_EPS, None, ALU.add).then_inc(G["pool_step"], 1)
                steps[0] += 1
                pool.wait_ge(G["pool_step"], steps[0])
                g.tensor_tensor(rstd[:, s:s + 1], rstd[:, s:s + 1], mhalf[:, :], ALU.pow).then_inc(G["ln_rstd"], 1)

            for n in range(FILLS * B + 8):
                b, i = divmod(n, FILLS)
                if n < FILLS * B:
                    pool.wait_ge(G["a_rinv"], n + 1)
                    g.tensor_tensor(sm[:, n % 4, :, :], sm[:, n % 4, :, :],
                                    rinv[:, n % 8, :].unsqueeze(2).broadcast_to([P, 4, P]), ALU.mult).then_inc(G["a_norm"], 1)
                if i == 5 and b > 0:
                    for t in range(TPB):
                        rstd_of(2 * (b - 1) + t)
            pool.wait_ge(G["a_y"], B)
            pool.wait_ge(G["ld_zero"], 16 * (NE + 1))
            g.memset(ctxR[1][:, :, E:E + 1], 1.0).then_inc(G["const_set"], 1)
            for n in range(NT, 2 * NT):
                rstd_of(n)

            def rotate(dst, src, parts, heads):
                cos = cst[0:parts, C_COS:C_COS + heads * RH].rearrange("p (h r) -> p h r", h=heads)
                sin = cst[0:parts, C_SIN:C_SIN + heads * RH].rearrange("p (h r) -> p h r", h=heads)
                x1, x2 = src[:, :, 0:RH], src[:, :, RH:RD]
                o1, o2 = dst[:, :, 0:RH], dst[:, :, RH:RD]
                t = w_rot[0:parts, 0:heads, :]
                for o, a1, b1, op in ((o1, x1, x2, ALU.subtract), (o2, x2, x1, ALU.add)):
                    for dst1, p0, p1, f in ((o, a1, cos, ALU.mult), (t, b1, sin, ALU.mult), (o, o, t, op)):
                        g.tensor_tensor(dst1, p0, p1, f).then_inc(G["d_rot"], 1)
                        rots[0] += 1
                        pool.wait_ge(G["d_rot"], rots[0])

            rots = [0]
            pool.wait_ge(G["ld_lat"], 96)
            pool.wait_ge(G["ld_wq"], 32)
            rotate(w_ki[:, :, LAT:P], w_kr[:, :, :], LAT, KV1)
            for k in range(KT):
                rotate(w_qe[:, k, :, LAT:P], w_qr[:, k, :, :], P, H1)
            for n in range(2 * NT, 3 * NT):
                rstd_of(n)
            def norm_p(p):
                for h in (2 * p, 2 * p + 1):
                    pool.wait_ge(G["d_rinv"], h + 1)
                    for j, (a, z) in enumerate(((0, 1), (1, 3))):
                        g.tensor_scalar(dp[:, h % 6, a:z, :], dp[:, h % 6, a:z, :], dri[:, h % 8, j:j + 1], 1.0,
                                        ALU.mult, ALU.mult).then_inc(G["d_norm"], 1)

            for p in range(B * PAIRS + 1):
                b, q = divmod(p, PAIRS)
                if p > 0:
                    norm_p(p - 1)
                if q == 5 and b > 0:
                    for t in range(TPB):
                        rstd_of(3 * NT + 2 * (b - 1) + t)
            for t in range(TPB):
                rstd_of(3 * NT + 2 * (B - 1) + t)
            for b in range(B + 1):
                if b < B:
                    for t in range(TPB):
                        rstd_of(4 * NT + 2 * b + t)
                if b > 0:
                    pool.wait_ge(G["r_rows"], 2 * b)
                for t in range(2 * b - 2, 2 * b) if b else ():
                    for c in range(TOPK):
                        g.indirect_dma_start(xs, bass.IndirectOffsetOnAxis(ap=tok_rows[:, c, t:t + 1], axis=0),
                                             x_row[:, t, :], None).then_inc(G["r_scat"], 16)
            pool.wait_ge(G["r_out_rows"], 2)
            pool.wait_ge(G["m_st0"], 16 * (TILES // 2 + 1))
            pool.wait_ge(G["m_st1"], 16 * (TILES // 2))
            for t in range(NT):
                for c, o in enumerate((y_lo, y_hi)):
                    g.indirect_dma_start(o[:, t, :], None, ys,
                                         bass.IndirectOffsetOnAxis(ap=out_rows[:, c, t:t + 1], axis=0)).then_inc(G[f"y_got{t}"], 16)
            for n in range(5 * NT, 6 * NT):
                rstd_of(n)

        @block.scalar
        def _(act):
            a = nc.scalar
            act.wait_ge(G["const_set"], 8)

            def xT_copy(stage, b):
                n = stage * B + b
                act.wait_ge(G["xT_raw"], n + 1)
                a.activation(xT[:, :, b * S:(b + 1) * S], PS_xT[stage][:, :].rearrange("p (k t) -> p k t", k=KT),
                             ACT.Copy).then_inc(G["xT_done"], 1)

            def a_query(b):
                act.wait_ge(G["a_q"], b + 1)
                a.activation(qT[:, b % 2, :, :], PS[5][:, :].rearrange("p (k t) -> p k t", k=KT), ACT.Copy,
                             scale=float(D0) ** -0.5).then_inc(G["a_q_sb"], 1)

            def a_values(b, bank, at, w):
                a.activation(vpad[:, b % 2, w, :].rearrange("p (h c) -> p h c", c=D0P)[:, :, 0:D0],
                             PS[bank][:, at:at + E].rearrange("p (h c) -> p h c", c=D0), ACT.Copy).then_inc(G["a_v_sb"], 1)

            def a_keys1(b, g):
                act.wait_ge(G["a_k1v0"], b + 1)
                for h in range(4 * g, 4 * g + 4):
                    a.activation(kmask[:, b % 2, 1, h, :], PS[5][:, 0:S], ACT.Copy, scale=hmask[:, h:h + 1]).then_inc(G["a_k1_sb"], 1)

            def a_outT(b, f):
                act.wait_ge(G["a_o"], 2 * b + f + 1)
                if b > 0 and f == 0:
                    act.wait_ge(G["a_y"], b)
                a.activation(oT[:, 2 * f:2 * f + 2, :], PS[7][:, :].rearrange("p (k t) -> p k t", k=2), ACT.Copy).then_inc(G["a_o_sb"], 1)

            a_query(0)
            a_keys1(0, 0)
            a_values(0, 5, S, 0)
            a_keys1(0, 1)
            for n in range(FILLS * B + 8):
                b, i = divmod(n, FILLS)
                if i == 0 and 0 < b < B:
                    a_keys1(b, 1)
                if n < FILLS * B:
                    act.wait_ge(G["a_max"], n + 1)
                    if n >= 4:
                        act.wait_ge(G["a_pt"], n - 3)
                    for h in range(4):
                        a.activation(sm[:, n % 4, h, :], PS[n % 3][:, h * P:(h + 1) * P], ACT.Exp, bias=mx[:, n % 8, h:h + 1],
                                     accum_out=rsum[:, n % 8, h:h + 1]).then_inc(G["a_exp"], 1)
                if 3 <= n < FILLS * B + 3 and n % 2 == 0:
                    act.wait_ge(G["a_pt"], n - 2)
                    a.activation(PT[:, (n - 3) % 4, :, :], PS[4][:, :].rearrange("p (h q) -> p h q", h=4),
                                 ACT.Copy).then_inc(G["a_pt_odd"], 1)
                if i in (0, 4) and b > 0:
                    a_outT(b - 1, i // 4)
                if i == 3 and b < B:
                    act.wait_ge(G["a_v12"], b + 1)
                    a_values(b, 6, 0, 1)
                    a_values(b, 6, E, 2)
                if i == 3 and b >= 2:
                    xT_copy(0, b - 2)
                if i == 6 and b + 1 < B:
                    a_query(b + 1)
                if i == 7 and b + 1 < B:
                    a_keys1(b + 1, 0)
                    a_values(b + 1, 5, S, 0)
            xT_copy(0, B - 1)

            def b_exp(u):
                act.wait_ge(G["b_max"], u + 1)
                for c, (lo, hi) in enumerate(SCOLS):
                    a.activation(prob[:, lo:hi], PS[c][:, 0:hi - lo], ACT.Exp, bias=bmx[:, 4:5],
                                 accum_out=bsum[:, c:c + 1]).then_inc(G["b_exp"], 1)

            def b_probT(u, c):
                act.wait_ge(G["b_t"], 4 * u + c + 1)
                a.activation(probT[:, 4 * c:4 * c + 4, :], PS[4][:, :].rearrange("p (j q) -> p j q", j=4),
                             ACT.Copy).then_inc(G["b_pt_a"], 1)

            def b_oT(u):
                act.wait_ge(G["b_ot"], u + 1)
                a.activation(xoT, PS[7 if u % 2 else 6][:, 0:KT * P].rearrange("p (k t) -> p k t", k=KT),
                             ACT.Copy).then_inc(G["b_ot_sb"], 1)

            for b in range(B):
                act.wait_ge(G["b_q"], b + 1)
                a.activation(xq, PS[4][:, :].rearrange("p (k t) -> p k t", k=KT), ACT.Copy,
                             scale=float(E) ** -0.5).then_inc(G["b_q_sb"], 1)
                act.wait_ge(G["b_k"], b + 1)
                a.activation(xk, PS[5][:, :].rearrange("p (k t) -> p k t", k=KT), ACT.Copy).then_inc(G["b_k_sb"], 1)
                if b > 0:
                    b_oT(2 * b - 1)
                b_exp(2 * b)
                for t in range(CB):
                    n = CB * b + t
                    rows = P if t < CB - 1 else CLAST
                    act.wait_ge(G["x_k"], n + 1)
                    if n >= 4:
                        act.wait_ge(G["x_kf"], n - 3)
                    a.activation(ek[0:rows, n % 4, :], PS[4 + t % 2][0:rows, 0:E], ACT.Exp).then_inc(G["x_exp"], 1)
                for c in (0, 2):
                    b_probT(2 * b, c)
                act.wait_ge(G["x_m1T"], b + 1)
                a.activation(m1T, PS[6][:, :].rearrange("p (k t) -> p k t", k=KT), ACT.Copy).then_inc(G["x_m1T_sb"], 1)
                b_exp(2 * b + 1)
                for c in (0, 2):
                    b_probT(2 * b + 1, c)
                b_oT(2 * b)
                if b < 3:
                    act.wait_ge(G["w_scale"], b + 1)
                    a.activation(qtmp, w_f32[:, b, :], ACT.Identity, scale=wsi[:, b:b + 1],
                                 bias=magic[:, :]).then_inc(G["w_round"], 1)
            b_oT(2 * B - 1)

            def f_round(t):
                act.wait_ge(G["f_sc"], t + 1)
                a.activation(fr[:, t % 2, :], x_row[:, t, :], ACT.Identity, scale=fs[:, t % 4, 2:3],
                             bias=magic[:, :]).then_inc(G["f_round"], 1)

            f_round(0)
            f_round(1)
            for t in range(NT + 1):
                if t < NT:
                    if t % TPB == 0:
                        b = t // TPB
                        act.wait_ge(G["f_qT"], b + 1)
                        a.activation(fqT[:, b % 2, :, :], PS[0][:, 0:S].bitcast(BF16).rearrange("p (k t) -> p k t", k=KT),
                                     ACT.Copy).then_inc(G["f_qT_sb"], 1)
                    for c in range(2):
                        act.wait_ge(G["f_gu"], 4 * t + 2 * c + 1)
                        if 2 * t + c >= 2:
                            act.wait_ge(G["f_h"], 2 * t + c - 1)
                        a.activation(sg[:, c, :], PS[1 + 2 * c][:, :], ACT.Sigmoid,
                                     scale=fs[:, t % 4, 3:4]).then_inc(G["f_sig"], 1)
                if t > 0:
                    act.wait_ge(G["f_hqT"], t)
                    a.activation(hqT[:, (t - 1) % 2, :, :], PS[5][:, :].bitcast(BF16).rearrange("p (k t) -> p k t", k=FF // P),
                                 ACT.Copy).then_inc(G["f_hqT_sb"], 1)
                if t < NT:
                    act.wait_ge(G["f_hsc"], t + 1)
                    a.activation(hr, hh[:, t % 2, :], ACT.Identity, scale=fh[:, t % 2, 3:4],
                                 bias=magic[:, :]).then_inc(G["f_hround"], 1)
                if t % TPB and t + 1 < NT:
                    f_round(t + 1)
                    f_round(t + 2)
                if t > 0:
                    act.wait_ge(G["d_w"], t)
                    a.activation(w_qe[:, :, 2 * t - 2:2 * t, 0:LAT],
                                 PS[7][:, 0:2 * KT * LAT].rearrange("p (k h c) -> p k h c", k=KT, h=2),
                                 ACT.Copy).then_inc(G["d_w_sb"], 1)
                    a.activation(w_vo[:, t - 1, :], PS[7][:, 256:256 + E], ACT.Copy).then_inc(G["d_w_sb"], 1)
                if t >= 3 and t % TPB:
                    xT_copy(1, t // TPB - 1)
            xT_copy(1, B - 1)

            def d_latent(b):
                act.wait_ge(G["d_c"], b + 1)
                a.activation(cT[0:LAT, :], PS[7][0:LAT, 0:S], ACT.Copy).then_inc(G["d_c_sb"], 1)
                a.activation(cR[:, b % 2, :, :], PS[7][:, S:S + TPB * LAT].rearrange("p (t c) -> p t c", t=TPB),
                             ACT.Copy).then_inc(G["d_c_sb"], 1)

            def d_keys(b):
                for h in range(2):
                    act.wait_ge(G["d_k"], 2 * b + h + 1)
                    a.activation(kg[:, b % 2, 2 * h:2 * h + 2, :], PS[7][:, :].rearrange("p (h q) -> p h q", h=2), ACT.Copy,
                                 scale=SC1).then_inc(G["d_k_sb"], 1)

            d_latent(0)
            d_keys(0)
            NP = B * PAIRS
            for p in range(NP + 4):
                b, q = divmod(p, PAIRS)
                if q == 4 and b + 1 < B:
                    d_latent(b + 1)
                if q == 5 and b + 1 < B:
                    d_keys(b + 1)
                if p < NP:
                    for h in (2 * p, 2 * p + 1):
                        for j, (lo, hi) in enumerate(((0, 1), (1, 3))):
                            if j == 0:
                                act.wait_ge(G["d_max"], 2 * h + 2)
                            a.activation(dp[:, h % 6, lo:hi, :],
                                         PS[2 + h % 2][:, lo * P:hi * P].rearrange("p (c k) -> p c k", k=P), ACT.Exp,
                                         bias=dmx[:, h % 8, j:j + 1],
                                         accum_out=dsm[:, h % 8, j:j + 1]).then_inc(G["d_exp"], 1)
                if 2 <= p < NP + 2:
                    for h in (2 * p - 4, 2 * p - 3):
                        act.wait_ge(G["d_t"], h + 1)
                        a.activation(dpT[:, h % 4, :], PS[4 + h % 2][:, 0:3 * P], ACT.Copy).then_inc(G["d_t_sb"], 1)
                if 3 <= p < NP + 3:
                    act.wait_ge(G["d_o"], p - 2)
                    a.activation(doT[:, (p - 3) % PAIRS, :], PS[6][:, 0:S], ACT.Copy).then_inc(G["d_o_sb"], 1)
                if q == 6 and b > 0:
                    xT_copy(2, b - 1)
            xT_copy(2, B - 1)

            def r_softmax(b):
                act.wait_ge(G["r_log"], b + 1)
                a.activation(rt[:, 2 * b:2 * b + 2, :], PS[6][:, 0:TPB * NE].rearrange("p (t e) -> p t e", t=TPB), ACT.Tanh,
                             scale=1.0 / CAP).then_inc(G["r_act"], 1)
                act.wait_ge(G["r_v"], b + 1)
                a.activation(rt[:, 2 * b:2 * b + 2, :], rt2[:, 2 * b:2 * b + 2, :], ACT.Exp, scale=CAP).then_inc(G["r_act"], 1)

            for b in range(B):
                s = b % 2
                act.wait_ge(G["e_qg"], 2 * b + 1)
                a.activation(eq[:, s, :], PS[0][:, :], ACT.Exp).then_inc(G["e_exp"], 1)
                act.wait_ge(G["e_qg"], 2 * b + 2)
                if b >= 2:
                    act.wait_ge(G["e_at"], b - 1)
                for k in range(KT):
                    a.activation(egt[:, s, k * S:(k + 1) * S], PS[1][:, k * S:(k + 1) * S], ACT.Exp,
                                 bias=nbg[:, k:k + 1], scale=-1.0).then_inc(G["e_eg"], 1)
                if b >= 2:
                    xT_copy(3, b - 2)
                    r_softmax(b - 2)
            for b in (B - 2, B - 1):
                xT_copy(3, b)
                r_softmax(b)

            def m_rows(i, slot, used=None):
                act.wait_ge(G["m_y"], i + 1)
                if used is not None:
                    act.wait_ge(G[f"m_st{slot}"], used)
                a.activation(yt[:, slot, :], PS[4][:, 0:E], ACT.Copy).then_inc(G["m_y_sb"], 1)

            def m_tokens(i, slot):
                act.wait_ge(G["m_xT"], i + 1)
                a.activation(xgT[:, slot, :, :], PS[5][:, 0:KT * P].rearrange("p (k t) -> p k t", k=KT),
                             ACT.Copy).then_inc(G["m_xT_sb"], 1)

            def m_step(i, h, slot, first=False, last=False, used=True):
                act.wait_ge(G["m_g"], i + 1)
                if not first:
                    act.wait_ge(G["m_h"], i)
                a.activation(sa, PS[0][:, :], ACT.Silu).then_inc(G["m_silu"], 1)
                if not last:
                    m_tokens(i + 1, 1 - slot)
                if not first:
                    m_rows(i - 1, 1 - slot, (h if slot else h - 1) * 16 if used else None)

            m_tokens(0, 0)
            m_step(0, 0, 0, first=True)
            m_step(1, 0, 1, used=False)
            m_step(2, 1, 0, used=False)
            with act.Fori(1, TILES // 2 - 1) as h:
                m_step(h * 2 + 1, h, 1)
                m_step(h * 2 + 2, h + 1, 0)
            m_step(TILES - 2, TILES // 2 - 1, 1)
            m_step(TILES - 1, TILES // 2, 0, last=True)
            m_rows(TILES - 1, 0, TILES // 2 * 16)

        @block.vector
        def _(dve):
            v = nc.vector
            steps = [0]

            def link(ins):
                ins.then_inc(G["dve_step"], 1)
                steps[0] += 1
                dve.wait_ge(G["dve_step"], steps[0])

            def ln_begin(n, add):
                s = n % 4
                link(add(res[:, s, :]))
                link(v.bn_stats(stats[:, s, :], res[:, s, :]))
                v.bn_aggr(mv[:, s, :], stats[:, s, :]).then_inc(G["ln_var"], 1)

            def ln_end(n):
                s, t = n % 4, n % NT
                dve.wait_ge(G["ln_rstd"], n + 1)
                v.tensor_scalar(x_row[:, t, :], res[:, s, :], mv[:, s, 0:1], rstd[:, s:s + 1], ALU.subtract,
                                ALU.mult).then_inc(G["ln_done"], 1)

            def add_rows(bank, at, t):
                return lambda o: v.tensor_tensor(o, PS[bank][:, at:at + E], x_row[:, t, :], ALU.add)

            dve.wait_ge(G["const_set"], 8)

            def a_keys0(b, g):
                dve.wait_ge(G["a_k0"], b + 1)
                v.tensor_tensor(kmask[:, b % 2, 0, 4 * g:4 * g + 4, :], PS[6][:, 0:S].unsqueeze(1).broadcast_to([P, 4, S]),
                                hmask[:, 4 * g:4 * g + 4].unsqueeze(2).broadcast_to([P, 4, S]), ALU.mult).then_inc(G["a_k0_sb"], 1)

            a_keys0(0, 0)
            a_keys0(0, 1)
            for n in range(FILLS * B + 8):
                b, i = divmod(n, FILLS)
                if n < FILLS * B:
                    dve.wait_ge(G["a_s"], n + 1)
                    v.tensor_reduce(mx[:, n % 8, :], PS[n % 3][:, :].rearrange("p (h k) -> p h k", h=4), AX, ALU.max,
                                    negate=True).then_inc(G["a_max"], 1)
                if 1 <= n <= FILLS * B:
                    dve.wait_ge(G["a_exp"], 4 * n)
                    v.reciprocal(rinv[:, (n - 1) % 8, :], rsum[:, (n - 1) % 8, :]).then_inc(G["a_rinv"], 1)
                if 3 <= n < FILLS * B + 3 and n % 2:
                    dve.wait_ge(G["a_pt"], n - 2)
                    v.tensor_copy(PT[:, (n - 3) % 4, :, :], PS[3][:, :].rearrange("p (h q) -> p h q", h=4)).then_inc(G["a_pt_even"], 1)
                if i == 6 and b > 0:
                    if b == 1:
                        dve.wait_ge(G["ld_xrow"], 16)
                    dve.wait_ge(G["a_y"], b)
                    for t in range(TPB):
                        ln_begin(2 * (b - 1) + t, add_rows(5, t * E, 2 * (b - 1) + t))
                if i in (6, 7) and b + 1 < B:
                    a_keys0(b + 1, i - 6)
                if i == 7 and b > 0:
                    for t in range(TPB):
                        ln_end(2 * (b - 1) + t)

            def b_max(u):
                for c, (lo, hi) in enumerate(SCOLS):
                    dve.wait_ge(G["b_s"], 4 * u + c + 1)
                    ins = v.tensor_reduce(bmx[:, c:c + 1], PS[c][:, 0:hi - lo], AX, ALU.max)
                    if c < 3:
                        ins.then_inc(G["dve_step"], 1)
                        steps[0] += 1
                    else:
                        link(ins)
                v.tensor_reduce(bmx[:, 4:5], bmx[:, 0:4], AX, ALU.max, negate=True).then_inc(G["b_max"], 1)

            def b_probT(u, c):
                nb = 4 if c < 3 else 3
                dve.wait_ge(G["b_t"], 4 * u + c + 1)
                v.tensor_copy(probT[:, 4 * c:4 * c + nb, :],
                              PS[5][:, 0:nb * P].rearrange("p (j q) -> p j q", j=nb)).then_inc(G["b_pt_d"], 1)

            def b_rinv(u):
                dve.wait_ge(G["b_exp"], 4 * u + 4)
                link(v.tensor_reduce(bsum[:, 4:5], bsum[:, 0:4], AX, ALU.add))
                link(v.reciprocal(bsum[:, 5:6], bsum[:, 4:5]))

            def b_out(u):
                dve.wait_ge(G["b_o"], u + 1)
                v.tensor_scalar(xo, PS[7][:, 0:E], bsum[:, 5:6], None, ALU.mult).then_inc(G["b_o_sb"], 1)

            def b_ln(u):
                dve.wait_ge(G["b_y"], u + 1)
                ln_begin(NT + u, add_rows(7 if u % 2 else 6, 0, u))

            dve.wait_ge(G["ld_ffn"], 48)
            dve.wait_ge(G["ld_x1"], 96)
            link(v.tensor_scalar(nbg[:, :], bg[:, :], -1.0, None, ALU.mult))
            for b in range(B):
                dve.wait_ge(G["b_v"], b + 1)
                v.tensor_copy(xv, PS[6][:, :].rearrange("p (t e) -> p t e", t=TPB)).then_inc(G["b_v_sb"], 1)
                b_max(2 * b)
                if b > 0:
                    b_ln(2 * b - 1)
                for t in range(CB):
                    n = CB * b + t
                    rows = P if t < CB - 1 else CLAST
                    dve.wait_ge(G["x_exp"], n + 1)
                    link(v.tensor_scalar(ek[0:rows, n % 4, :], ek[0:rows, n % 4, :], 1.0, None, ALU.min))
                    if n >= 4:
                        dve.wait_ge(G["x_m1"], n - 3)
                    v.scalar_tensor_tensor(out=kf[0:rows, n % 4, :], in0=PS[4 + t % 2][0:rows, 0:E], scalar=0.0,
                                           in1=ek[0:rows, n % 4, :], op0=ALU.max, op1=ALU.add).then_inc(G["x_kf"], 1)
                    if t == 4 and b > 0:
                        ln_end(NT + 2 * b - 2)
                        ln_end(NT + 2 * b - 1)
                b_rinv(2 * b)
                b_probT(2 * b, 1)
                b_probT(2 * b, 3)
                dve.wait_ge(G["x_m1"], CB * (b + 1))
                for k in range(KT):
                    v.tensor_copy(m1[:, k, 0:E + 1], PS[6 + k][:, 0:E + 1]).then_inc(G["x_m1_sb"], 1)
                b_max(2 * b + 1)
                b_out(2 * b)
                b_probT(2 * b + 1, 1)
                b_probT(2 * b + 1, 3)
                b_rinv(2 * b + 1)
                dve.wait_ge(G["x_kv"], b + 1)
                for k in range(KT):
                    v.tensor_scalar(dsum[:, b, k, :], blk, m1[:, k, E:E + 1], None, ALU.mult).then_inc(G["dve_step"], 1)
                    steps[0] += 1
                v.tensor_tensor(kvbd[:, b, :, :], PS[6][:, 0:KT * P].rearrange("p (k e) -> p k e", k=KT),
                                blk.unsqueeze(1).broadcast_to([P, KT, P]), ALU.mult).then_inc(G["x_kvbd"], 1)
                if b < 3:
                    v.tensor_reduce(wabs[:, b:b + 1], w_f32[:, b, :], AX, ALU.add,
                                    apply_absolute_value=True).then_inc(G["w_abs"], 1)
                b_ln(2 * b)
                b_out(2 * b + 1)
                if b < 3:
                    dve.wait_ge(G["w_sum"], b + 1)
                    link(v.tensor_scalar(wsc[:, b:b + 1], PS[6][:, 0:1], 1.0 / (FF * E), Q_EPS, ALU.mult, ALU.add))
                    v.reciprocal(wsi[:, b:b + 1], wsc[:, b:b + 1]).then_inc(G["w_scale"], 1)
                    dve.wait_ge(G["w_round"], b + 1)
                    link(v.tensor_scalar(qtmp, qtmp, MAGIC, 1.0, ALU.subtract, ALU.min))
                    v.tensor_scalar(w_ff[:, b, :], qtmp, -1.0, None, ALU.max).then_inc(G["w_tern"], 1)
            b_ln(2 * B - 1)
            ln_end(NT + 2 * B - 2)
            ln_end(NT + 2 * B - 1)

            def f_scales(t):
                j = t % 4
                dve.wait_ge(G["ln_done"], NT + t + 1)
                link(v.tensor_reduce(fs[:, j, 0:1], x_row[:, t, :], AX, ALU.max, apply_absolute_value=True))
                link(v.tensor_scalar(fs[:, j, 1:2], fs[:, j, 0:1], Q_EPS, 1.0 / QMAX, ALU.max, ALU.mult))
                link(v.tensor_tensor(fs[:, j, 3:5], fs[:, j, 1:2].broadcast_to([P, 2]), wsc[:, 0:2], ALU.mult))
                v.reciprocal(fs[:, j, 2:3], fs[:, j, 1:2]).then_inc(G["f_sc"], 1)

            def f_quant(t):
                j = t % 2
                dve.wait_ge(G["f_round"], t + 1)
                v.tensor_scalar(fq[:, j, :], fr[:, j, :], MAGIC, QMAX, ALU.subtract, ALU.min).then_inc(G["f_q"], 1)

            def f_hidden(t):
                j, i = t % 2, t % 4
                for c in range(2):
                    dve.wait_ge(G["f_sig"], 2 * t + c + 1)
                    dve.wait_ge(G["f_gu"], 4 * t + 2 * c + 2)
                    v.tensor_tensor(hh[:, j, c * 512:(c + 1) * 512], sg[:, c, :], PS[2 + 2 * c][:, :], ALU.mult).then_inc(G["f_h"], 1)
                dve.wait_ge(G["f_h"], 2 * t + 2)
                link(v.tensor_reduce(fh[:, j, 0:1], hh[:, j, :], AX, ALU.max, apply_absolute_value=True))
                link(v.tensor_scalar(fh[:, j, 1:2], fh[:, j, 0:1], fs[:, i, 4:5], Q_EPS, ALU.mult, ALU.max))
                link(v.tensor_scalar(fh[:, j, 1:2], fh[:, j, 1:2], 1.0 / QMAX, None, ALU.mult))
                link(v.reciprocal(fh[:, j, 2:3], fh[:, j, 1:2]))
                link(v.tensor_tensor(fh[:, j, 4:5], fh[:, j, 1:2], wsc[:, 2:3], ALU.mult))
                v.tensor_tensor(fh[:, j, 3:4], fh[:, j, 2:3], fs[:, i, 4:5], ALU.mult).then_inc(G["f_hsc"], 1)

            def f_hidden_quant(t):
                j = t % 2
                dve.wait_ge(G["f_hround"], t + 1)
                v.tensor_scalar(hq[:, j, :], hr, MAGIC, QMAX, ALU.subtract, ALU.min).then_inc(G["f_hq"], 1)

            def f_out(t):
                n = 2 * NT + t
                dve.wait_ge(G["f_y"], t + 1)
                ln_begin(n, lambda o: v.scalar_tensor_tensor(out=o, in0=PS[6][:, 0:E], scalar=fh[:, t % 2, 4:5],
                                                             in1=x_row[:, t, :], op0=ALU.mult, op1=ALU.add))

            for f in (f_scales, f_quant):
                for t in range(TPB):
                    f(t)
            for t in range(NT + 1):
                following = range(t + 1, t + 1 + TPB) if t % TPB and t + 1 < NT else ()
                if t < NT:
                    f_hidden(t)
                for n in following:
                    f_scales(n)
                if t > 0:
                    f_out(t - 1)
                if t < NT:
                    f_hidden_quant(t)
                for n in following:
                    f_quant(n)
                if t > 0:
                    ln_end(2 * NT + t - 1)

            def d_query(p):
                dve.wait_ge(G["d_q"], p + 1)
                v.tensor_copy(qe[:, p % 3, :, :], PS[p % 2][:, :].rearrange("p (h q) -> p h q", h=2)).then_inc(G["d_q_sb"], 1)

            def d_rinv(p):
                for h in (2 * p, 2 * p + 1):
                    dve.wait_ge(G["d_exp"], 2 * h + 2)
                    v.reciprocal(dri[:, h % 8, :], dsm[:, h % 8, :]).then_inc(G["d_rinv"], 1)

            def d_ln(b):
                dve.wait_ge(G["d_y"], b + 1)
                for t in range(TPB):
                    ln_begin(3 * NT + 2 * b + t, add_rows(7, t * E, 2 * b + t))

            NP = B * PAIRS
            d_query(0)
            for p in range(NP + 1):
                b, q = divmod(p, PAIRS)
                if p + 1 < NP:
                    d_query(p + 1)
                if p < NP:
                    for h in (2 * p, 2 * p + 1):
                        dve.wait_ge(G["d_s"], h + 1)
                        bank = PS[2 + h % 2]
                        v.tensor_reduce(dmx[:, h % 8, 0:1], bank[:, 0:P], AX, ALU.max, negate=True).then_inc(G["d_max"], 1)
                        v.tensor_reduce(dmx[:, h % 8, 1:2], bank[:, P:3 * P], AX, ALU.max, negate=True).then_inc(G["d_max"], 1)
                if p > 0:
                    d_rinv(p - 1)
                if q == 3 and b > 0:
                    d_ln(b - 1)
                if q == 5 and b > 0:
                    for t in range(TPB):
                        ln_end(3 * NT + 2 * (b - 1) + t)
            d_ln(B - 1)
            for t in range(TPB):
                ln_end(3 * NT + 2 * (B - 1) + t)

            def pair_rows(o, at, s):
                link(v.tensor_reduce(shi[:, at], slots[:, at, :], AX, ALU.max))
                link(v.tensor_reduce(ssm[:, at], slots[:, at, :], AX, ALU.add))
                v.tensor_scalar(o[:, 1, at], shi[:, at], -1.0, None, ALU.add).then_inc(G[s], 1)
                v.scalar_tensor_tensor(out=o[:, 0, at], in0=ssm[:, at], scalar=-1.0, in1=shi[:, at],
                                       op0=ALU.add, op1=ALU.subtract).then_inc(G[s], 1)

            def r_route(b):
                at = slice(2 * b, 2 * b + 2)
                over = lambda x: x[:, at].unsqueeze(2).broadcast_to([P, TPB, NE])
                dve.wait_ge(G["r_act"], 2 * b + 1)
                link(v.tensor_reduce(rtop[:, at], rt[:, at, :], AX, ALU.max))
                v.tensor_tensor(rt2[:, at, :], rt[:, at, :], over(rtop), ALU.subtract).then_inc(G["r_v"], 1)
                dve.wait_ge(G["r_act"], 2 * b + 2)
                link(v.tensor_reduce(rsm[:, at], rt[:, at, :], AX, ALU.add))
                link(v.reciprocal(rsi[:, at], rsm[:, at]))
                link(v.tensor_tensor(wgt[:, at, :], rt[:, at, :], over(rsi), ALU.mult))
                for t in range(2 * b, 2 * b + 2):
                    other = wgt[:, t, :].unsqueeze(1).broadcast_to([P, NE, NE])
                    own = wgt[:, t, :].unsqueeze(2).broadcast_to([P, NE, NE])
                    link(v.tensor_tensor(rcmp, other, own, ALU.is_gt))
                    link(v.tensor_tensor(rcm2, other, own, ALU.is_equal))
                    link(v.tensor_tensor(rcm2, rcm2, tri, ALU.mult))
                    link(v.tensor_tensor(rcmp, rcmp, rcm2, ALU.add))
                    link(v.tensor_reduce(rt2[:, t, :], rcmp, AX, ALU.add))
                link(v.tensor_scalar(rt2[:, at, :], rt2[:, at, :], float(TOPK), None, ALU.is_lt))
                v.tensor_copy(kept16[:, at, :], rt2[:, at, :]).then_inc(G["r_kept"], 1)
                link(v.tensor_tensor(wgt[:, at, :], wgt[:, at, :], rt2[:, at, :], ALU.mult))
                dve.wait_ge(G["r_count"], b + 1)
                first = cst[:, C_EROW:C_EROW + NE].unsqueeze(1).broadcast_to([P, TPB, NE])
                link(v.tensor_tensor(slots[:, at, :], PS[7][:, 0:TPB * NE].rearrange("p (t e) -> p t e", t=TPB), first, ALU.add))
                link(v.tensor_tensor(slots[:, at, :], slots[:, at, :], rt2[:, at, :], ALU.mult))
                pair_rows(tok_rows, at, "r_rows")
                link(v.tensor_tensor(chosen[:, at, :], slots[:, at, :], over(shi), ALU.is_equal))
                link(v.tensor_tensor(chosen[:, at, :], chosen[:, at, :], wgt[:, at, :], ALU.mult))
                link(v.tensor_reduce(w_hi[:, at], chosen[:, at, :], AX, ALU.add))
                link(v.tensor_reduce(w_lo[:, at], wgt[:, at, :], AX, ALU.add))
                link(v.tensor_tensor(w_lo[:, at], w_lo[:, at], w_hi[:, at], ALU.subtract))

            dve.wait_ge(G["ld_cbias"], 16)
            v.tensor_scalar(before16, cbias[:, 0:P], 0.0, None, ALU.is_lt).then_inc(G["r_set"], 1)
            v.tensor_copy(ones16, ones[:, :]).then_inc(G["r_set"], 1)

            def e_ln(b):
                dve.wait_ge(G["e_y"], b + 1)
                for t in range(TPB):
                    ln_begin(4 * NT + 2 * b + t, add_rows(4, t * E, 2 * b + t))

            for b in range(B):
                s = b % 2
                dve.wait_ge(G["e_exp"], b + 1)
                link(v.tensor_scalar(eq[:, s, :], eq[:, s, :], 1.0, None, ALU.min))
                v.scalar_tensor_tensor(out=qf[:, s, :, :].rearrange("p k t -> p (k t)"), in0=PS[0][:, :], scalar=0.0,
                                       in1=eq[:, s, :], op0=ALU.max, op1=ALU.add).then_inc(G["e_qf"], 1)
                dve.wait_ge(G["e_eg"], 2 * b + 2)
                link(v.tensor_scalar(egt[:, s, :], egt[:, s, :], 1.0, None, ALU.add))
                dve.wait_ge(G["e_nd"], 2 * b + 2)
                link(v.scalar_tensor_tensor(out=den, in0=PS[3][:, :], scalar=Z_EPS, in1=egt[:, s, :], op0=ALU.add, op1=ALU.mult))
                link(v.reciprocal(den, den))
                v.tensor_tensor(eat[:, s, :, :].rearrange("p k t -> p (k t)"), PS[2][:, :], den, ALU.mult).then_inc(G["e_at"], 1)
                if b > 0:
                    e_ln(b - 1)
                    for t in range(TPB):
                        ln_end(4 * NT + 2 * (b - 1) + t)
                if b > 1:
                    r_route(b - 2)
            e_ln(B - 1)
            for t in range(TPB):
                ln_end(4 * NT + 2 * (B - 1) + t)
            r_route(B - 2)
            r_route(B - 1)

            count = PS[7][:, TPB * NE:TPB * NE + NE]
            thr, tile_no = cst[:, C_THR:C_THR + NE], cst[:, C_TILE:C_TILE + TILES]
            link(v.tensor_tensor(rcmp, count.unsqueeze(2).broadcast_to([P, NE, NE]),
                                 thr.unsqueeze(1).broadcast_to([P, NE, NE]), ALU.is_gt))
            link(v.tensor_reduce(etiles, rcmp, AX, ALU.add))
            link(v.tensor_tensor(rcm2, tri, etiles.unsqueeze(1).broadcast_to([P, NE, NE]), ALU.mult))
            link(v.tensor_reduce(eends, rcm2, AX, ALU.add))
            link(v.tensor_tensor(eends, eends, etiles, ALU.add))
            link(v.tensor_scalar(eskip, etiles, -float(P), float(TOKENS), ALU.mult, ALU.add))
            link(v.tensor_tensor(tcmp, tile_no.unsqueeze(2).broadcast_to([P, TILES, NE]),
                                 eends.unsqueeze(1).broadcast_to([P, TILES, NE]), ALU.is_ge))
            link(v.tensor_reduce(tab[:, 0, :], tcmp, AX, ALU.add))
            link(v.tensor_tensor(tcmp, tcmp, eskip.unsqueeze(1).broadcast_to([P, TILES, NE]), ALU.mult))
            link(v.tensor_reduce(tab[:, 1, :], tcmp, AX, ALU.add))
            link(v.scalar_tensor_tensor(out=tab[:, 1, :], in0=tile_no, scalar=float(P), in1=tab[:, 1, :], op0=ALU.mult, op1=ALU.add))
            v.tensor_scalar(table[:, 0, :], tab[:, 0, :], float(NE - 1), None, ALU.min).then_inc(G["r_table"], 1)
            v.tensor_copy(table[:, 1, :], tab[:, 1, :]).then_inc(G["r_table"], 1)

            link(v.tensor_tensor(eends, eends, etiles, ALU.subtract))
            link(v.tensor_scalar(eends, eends, float(P), 1.0, ALU.mult, ALU.add))
            link(v.tensor_tensor(eends, eends, cst[:, C_EROW:C_EROW + NE], ALU.subtract))
            link(v.tensor_tensor(slots, slots, eends.unsqueeze(1).broadcast_to([P, NT, NE]), ALU.add))
            link(v.tensor_tensor(slots, slots, rt2, ALU.mult))
            pair_rows(out_rows, slice(0, NT), "r_out_rows")

            def m_hidden(i):
                dve.wait_ge(G["m_silu"], i + 1)
                dve.wait_ge(G["m_u"], i + 1)
                v.tensor_tensor(hs, sa, PS[1][:, :], ALU.mult).then_inc(G["m_h"], 1)

            def m_hiddenT(i):
                dve.wait_ge(G["m_hT"], i + 1)
                v.tensor_copy(hT, PS[2][:, :].rearrange("p (m t) -> p m t", m=FM)).then_inc(G["m_hT_sb"], 1)

            m_hidden(0)
            with dve.Fori(0, TILES - 1) as i:
                m_hiddenT(i)
                m_hidden(i + 1)
            m_hiddenT(TILES - 1)

            def add_experts(t):
                def add(o):
                    dve.wait_ge(G[f"y_got{t}"], 16 * TOPK)
                    link(v.scalar_tensor_tensor(out=o, in0=y_lo[:, t, :], scalar=w_lo[:, t:t + 1], in1=x_row[:, t, :],
                                                op0=ALU.mult, op1=ALU.add))
                    return v.scalar_tensor_tensor(out=o, in0=y_hi[:, t, :], scalar=w_hi[:, t:t + 1], in1=o,
                                                  op0=ALU.mult, op1=ALU.add)
                return add

            for t in range(NT + 1):
                if t < NT:
                    ln_begin(5 * NT + t, add_experts(t))
                if t > 0:
                    ln_end(5 * NT + t - 1)

        @block.tensor
        def _(pe):
            def mm(o, w, x, start=True, stop=True, **k):
                return nc.tensor.matmul(o, w, x, start=start, stop=stop, **k)

            def project(o, w, x):
                for k in range(KT):
                    ins = mm(o, w(k), x(k), start=k == 0, stop=k == KT - 1)
                return ins

            def to_xT(stage, b):
                pe.wait_ge(G["ln_done"], (0, 2, 3, 4)[stage] * NT + 2 * b + 2)
                for k in range(KT):
                    for t in range(TPB):
                        ins = mm(PS_xT[stage][:, k * S + t * P:k * S + (t + 1) * P], x_row[:, 2 * b + t, k * P:(k + 1) * P],
                                 ident, is_transpose=True)
                ins.then_inc(G["xT_raw"], 1)

            pe.wait_ge(G["const_set"], 8)

            def a_query_key(b):
                seq = lambda k: xT[:, k, b * S:(b + 1) * S]
                if b == 1:
                    pe.wait_ge(G["a_k1_sb"], 8)
                    pe.wait_ge(G["a_v_sb"], 1)
                elif b > 1:
                    pe.wait_ge(G["ln_var"], 2 * (b - 1))
                for f in range(KT):
                    ins = project(PS[5][:, f * S:(f + 1) * S], lambda k: w_qkv[:, k, f * P:(f + 1) * P], seq)
                ins.then_inc(G["a_q"], 1)
                if b > 0:
                    pe.wait_ge(G["a_v_sb"], 3 * b)
                project(PS[6][:, 0:S], lambda k: w_qkv[:, k, E:E + P], seq).then_inc(G["a_k0"], 1)

            def a_value(o, b, w):
                return project(o, lambda k: xT[:, k, b * S + w:b * S + w + P], lambda k: w_qkv[:, k, 2 * E:3 * E])

            def a_key_value(b):
                pe.wait_ge(G["a_q_sb"], b + 1)
                project(PS[5][:, 0:S], lambda k: w_qkv[:, k, E + P:2 * E], lambda k: xT[:, k, b * S:(b + 1) * S])
                a_value(PS[5][:, S:S + E], b, 0).then_inc(G["a_k1v0"], 1)

            def a_scores(n):
                b, i = divmod(n, FILLS)
                f, g, t = i // 4, (i // 2) % 2, i % 2
                if i == 0:
                    pe.wait_ge(G["a_q_sb"], b + 1)
                if t == 0:
                    pe.wait_ge(*((G["a_k0_sb"], 2 * b + g + 1) if f == 0 else (G["a_k1_sb"], 8 * b + 4 * g + 4)))
                if n >= 3:
                    pe.wait_ge(G["a_exp"], 4 * (n - 2))
                mask = wmask16[:, t, :].unsqueeze(1).broadcast_to([P, 4, P])
                q = qT[:, b % 2, f, :]
                k = kmask[:, b % 2, f, 4 * g:4 * g + 4, :]
                o = PS[n % 3]
                if t == 0:
                    mm(o[:, :], ident16[:, :], mask, stop=False)
                    ins = mm(o[:, :], q[:, 0:P], k[:, :, 0:P], start=False)
                else:
                    for c in range(2):
                        mm(o[c * WIN:(c + 1) * WIN, :], ident16[:, c * WIN:(c + 1) * WIN], mask, stop=False)
                    for c in range(2):
                        ins = mm(o[c * WIN:(c + 1) * WIN, :], q[:, P + c * WIN:P + (c + 1) * WIN],
                                 k[:, :, (c + 1) * WIN:(c + 1) * WIN + P], start=False)
                ins.then_inc(G["a_s"], 1)

            def a_transpose(n):
                pe.wait_ge(G["a_norm"], n + 1)
                if n >= 2:
                    pe.wait_ge(G["a_pt_odd" if n % 2 else "a_pt_even"], n // 2)
                for h in range(4):
                    ins = mm(PS[3 + n % 2][:, h * P:(h + 1) * P], sm[:, n % 4, h, :], ident, is_transpose=True)
                ins.then_inc(G["a_pt"], 1)

            def a_output(n):
                b, i = divmod(n, FILLS)
                f, g, t = i // 4, (i // 2) % 2, i % 2
                pe.wait_ge(G["a_pt_odd" if n % 2 else "a_pt_even"], n // 2 + 1)
                pe.wait_ge(G["a_v_sb"], 3 * b + (3 if t else 1))
                if i % 4 == 0 and n > 0:
                    pe.wait_ge(G["a_o_sb"], 2 * b + f)
                for h in range(4):
                    for w, lo, hi in ((0, 0, P),) if t == 0 else ((1, P, P + WIN), (2, P + WIN, S)):
                        head = (8 * f + 4 * g + h) * D0P
                        ins = mm(PS[7][h * D0P:(h + 1) * D0P, g * S + lo:g * S + hi], vpad[:, b % 2, w, head:head + D0P],
                                 PT[:, n % 4, h, lo - t * P:hi - t * P], tile_position=(0, h * D0P))
                if i % 4 == 3:
                    ins.then_inc(G["a_o"], 1)

            def a_project_out(b):
                pe.wait_ge(G["a_o_sb"], 2 * b + 2)
                if b == 0:
                    pe.wait_ge(G["a_k1_sb"], 16)
                    pe.wait_ge(G["a_v_sb"], 4)
                else:
                    pe.wait_ge(G["xT_done"], b)
                last = H0 * D0P // P - 1
                for t in range(TPB):
                    for k in range(last + 1):
                        ins = mm(PS[5][:, t * E:(t + 1) * E], oT[:, k, t * P:(t + 1) * P], w_o0[:, k, :], start=k == 0, stop=k == last)
                ins.then_inc(G["a_y"], 1)

            pe.wait_ge(G["ld_x"], 16)
            pe.wait_ge(G["ld_attn0"], 16)
            a_query_key(0)
            a_key_value(0)
            for n in range(FILLS * B + 8):
                b, i = divmod(n, FILLS)
                if n < FILLS * B:
                    a_scores(n)
                if 3 <= n < FILLS * B + 3:
                    a_transpose(n - 3)
                if 5 <= n < FILLS * B + 5:
                    a_output(n - 5)
                if i == 2 and b < B:
                    pe.wait_ge(G["a_k0_sb"], 2 * b + 2)
                    a_value(PS[6][:, 0:E], b, WIN)
                    a_value(PS[6][:, E:2 * E], b, P).then_inc(G["a_v12"], 1)
                if i == 2 and b >= 2:
                    if b < B:
                        pe.wait_ge(G["a_k1_sb"], 8 * b + 8)
                        pe.wait_ge(G["a_v_sb"], 3 * b + 1)
                    to_xT(0, b - 2)
                if i == 5 and b > 0:
                    if b == 1:
                        pe.wait_ge(G["ld_wo0"], 16)
                    a_project_out(b - 1)
                if i == 6 and b + 1 < B:
                    if b == 0:
                        pe.wait_ge(G["ld_rest"], 16)
                    a_query_key(b + 1)
                if i == 7 and b + 1 < B:
                    a_key_value(b + 1)
            to_xT(0, B - 1)

            pe.wait_ge(G["ld_x0"], 64)
            pe.wait_ge(G["ld_x1"], 96)

            def b_project(b):
                seq = lambda k: xT[:, k, b * S:(b + 1) * S]
                pe.wait_ge(G["xT_done"], b + 1)
                for n, (bank, s, freed) in enumerate(((4, "b_q", "b_pt_a"), (5, "b_k", "b_pt_d"))):
                    if b > 0:
                        pe.wait_ge(G[freed], 4 * b)
                    elif n == 0:
                        pe.wait_ge(G["a_pt_odd"], FILLS * B // 2)
                    else:
                        pe.wait_ge(G["xT_done"], B)
                    for f in range(KT):
                        ins = project(PS[bank][:, f * S:(f + 1) * S], lambda k: w_x0[:, n, k, f * P:(f + 1) * P], seq)
                    ins.then_inc(G[s], 1)
                if b == 0:
                    pe.wait_ge(G["a_v_sb"], 3 * B)
                elif b <= 3:
                    pe.wait_ge(G["w_scale"], b)
                for t in range(TPB):
                    ins = project(PS[6][:, t * E:(t + 1) * E], lambda k: xT[:, k, b * S + t * P:b * S + (t + 1) * P],
                                  lambda k: w_x0[:, 2, k, :])
                ins.then_inc(G["b_v"], 1)

            def b_score(u, c):
                b, t = divmod(u, TPB)
                lo, hi = SCOLS[c]
                if u == 0:
                    pe.wait_ge(*((G["a_exp"], 4 * FILLS * B) if c < 3 else (G["a_pt_even"], FILLS * B // 2)))
                else:
                    pe.wait_ge(G["b_exp"], 4 * (u - 1) + c + 1)
                q = lambda k: xq[:, k, t * P:(t + 1) * P]
                n = min(hi, CTX) - lo
                ins = project(PS[c][:, 0:n], q, lambda k: ctxT[b % 2][:, k, lo:lo + n])
                if c == 3:
                    ins = project(PS[c][:, n:n + S], q, lambda k: xk[:, k, :])
                ins.then_inc(G["b_s"], 1)

            def b_transpose(u, c):
                if c == 0:
                    pe.wait_ge(G["b_exp"], 4 * u + 4)
                if c >= 2:
                    pe.wait_ge(G["b_pt_d" if c % 2 else "b_pt_a"], 2 * u + 1)
                elif u % 2:
                    pe.wait_ge(G["b_pt_d" if c % 2 else "b_pt_a"], 2 * u)
                else:
                    pe.wait_ge(G["x_kf"], CB * (u // 2 + 1))
                for j in range(4 if c < 3 else 3):
                    n = 4 * c + j
                    lo, hi = key_block(n)
                    ins = mm(PS[4 + c % 2][0:hi - lo, j * P:(j + 1) * P], prob[:, lo:hi], ident, is_transpose=True)
                ins.then_inc(G["b_t"], 1)

            def key_block(n):
                if n < CB:
                    return n * P, min((n + 1) * P, CTX)
                return CTX + (n - CB) * P, CTX + (n - CB + 1) * P

            def b_values(u):
                b = u // TPB
                pe.wait_ge(G["b_pt_a"], 2 * u + 2)
                pe.wait_ge(G["b_pt_d"], 2 * u + 2)
                if u % 2:
                    pe.wait_ge(G["b_o_sb"], u)
                else:
                    pe.wait_ge(G["x_m1_sb"], 2 * b + 2)
                for n in range(CB + TPB):
                    lo, hi = key_block(n)
                    rhs = ctxR[b % 2][0:hi - lo, n, 0:E] if n < CB else xv[:, n - CB, :]
                    ins = mm(PS[7][:, 0:E], probT[0:hi - lo, n, :], rhs, start=n == 0, stop=n == CB + TPB - 1)
                ins.then_inc(G["b_o"], 1)

            def b_outT(u):
                pe.wait_ge(G["b_o_sb"], u + 1)
                if u % 2 == 0:
                    pe.wait_ge(G["x_kvbd"], u // 2 + 1)
                for k in range(KT):
                    ins = mm(PS[7 if u % 2 else 6][:, k * P:(k + 1) * P], xo[:, k * P:(k + 1) * P], ident, is_transpose=True)
                ins.then_inc(G["b_ot"], 1)

            def b_project_out(u):
                pe.wait_ge(G["b_ot_sb"], u + 1)
                ins = project(PS[7 if u % 2 else 6][:, 0:E], lambda k: xoT[:, k, :], lambda k: w_x0[:, 3, k, :])
                ins.then_inc(G["b_y"], 1)

            def x_keys(b):
                s = b % 2

                def key_fill(t):
                    rows = P if t < CB - 1 else CLAST
                    if t == 0:
                        pe.wait_ge(G["b_q_sb"], b + 1)
                    elif t == 1:
                        pe.wait_ge(G["b_k_sb"], b + 1)
                    else:
                        pe.wait_ge(G["x_kf"], CB * b + t - 1)
                    ins = project(PS[4 + t % 2][0:rows, 0:E], lambda k: ctxT[s][:, k, t * P:t * P + rows],
                                  lambda k: w_x1[:, 0, k, :])
                    ins.then_inc(G["x_k"], 1)

                key_fill(0)
                key_fill(1)
                pe.wait_ge(G["b_v_sb"], b + 1)
                if b > 0:
                    pe.wait_ge(G["ln_var"], NT + 2 * b)
                else:
                    pe.wait_ge(G["ln_var"], NT)
                for t in range(CB):
                    rows = P if t < CB - 1 else CLAST
                    n = CB * b + t
                    pe.wait_ge(G["x_kf"], n + 1)
                    for h in range(KT):
                        ins = mm(PS[6 + h][:, 0:E + 1], kf[0:rows, n % 4, h * P:(h + 1) * P], ctxR[s][0:rows, t, :],
                                 start=t == 0, stop=t == CB - 1)
                    ins.then_inc(G["x_m1"], 1)
                    if t + 2 < CB:
                        key_fill(t + 2)

            def x_transpose(b):
                pe.wait_ge(G["x_m1_sb"], 2 * b + 2)
                for k in range(KT):
                    for h in range(KT):
                        ins = mm(PS[6][:, k * S + h * P:k * S + (h + 1) * P], m1[:, h, k * P:(k + 1) * P], ident, is_transpose=True)
                ins.then_inc(G["x_m1T"], 1)

            def x_values(b):
                pe.wait_ge(G["x_m1T_sb"], b + 1)
                for h in range(KT):
                    ins = project(PS[6][:, h * P:(h + 1) * P], lambda k: m1T[:, k, h * P:(h + 1) * P],
                                  lambda k: w_x1[:, 1, k, h * P:(h + 1) * P])
                ins.then_inc(G["x_kv"], 1)

            for b in range(B):
                b_project(b)
                if b > 0:
                    b_outT(2 * b - 1)
                pe.wait_ge(G[f"ld_ctx{b % 2}"], 48 * (b // 2 + 1))
                if b == 1:
                    pe.wait_ge(G["const_set"], 9)
                for c in range(4):
                    if c == 0:
                        pe.wait_ge(G["b_q_sb"], b + 1)
                    if c == 3:
                        pe.wait_ge(G["b_k_sb"], b + 1)
                    b_score(2 * b, c)
                if b > 0:
                    b_project_out(2 * b - 1)
                x_keys(b)
                for c in range(4):
                    b_transpose(2 * b, c)
                    b_score(2 * b + 1, c)
                x_transpose(b)
                b_values(2 * b)
                for c in range(4):
                    b_transpose(2 * b + 1, c)
                x_values(b)
                b_outT(2 * b)
                b_values(2 * b + 1)
                b_project_out(2 * b)
                if b < 3:
                    pe.wait_ge(G["w_abs"], b + 1)
                    pe.wait_ge(G["ln_var"], NT + 2 * b + 1)
                    mm(PS[6][:, 0:1], ones[:, :], wabs[:, b:b + 1]).then_inc(G["w_sum"], 1)
            b_outT(2 * B - 1)
            b_project_out(2 * B - 1)

            def f_transpose(b):
                pe.wait_ge(G["f_q"], 2 * b + 2)
                if b == 0:
                    pe.wait_ge(G["b_exp"], 8 * NT // 2)
                elif b >= 2:
                    pe.wait_ge(G["xT_done"], B + b - 1)
                o = PS[0][:, 0:S].bitcast(BF16)
                for k in range(KT):
                    for t in range(TPB):
                        ins = mm(o[:, k * S + t * P:k * S + (t + 1) * P], fq[:, t, k * P:(k + 1) * P], ident16[:, :], is_transpose=True)
                ins.then_inc(G["f_qT"], 1)

            def f_gate_up(t):
                b, j = divmod(t, TPB)
                pe.wait_ge(G["f_qT_sb"], b + 1)
                for c in range(2):
                    for n in range(2):
                        if t > 0:
                            pe.wait_ge(*((G["f_sig"], 2 * t + c - 1) if n == 0 else (G["f_h"], 2 * t + c - 1)))
                        if t == 0 and (n, c) == (1, 1):
                            pe.wait_ge(G["b_pt_a"], 2 * NT)
                        ins = project(PS[1 + 2 * c + n][:, :], lambda k: fqT[:, b % 2, k, j * P:(j + 1) * P],
                                      lambda k: w_ff[:, n, k * FF + c * 512:k * FF + (c + 1) * 512])
                        ins.then_inc(G["f_gu"], 1)

            def f_hiddenT(t):
                pe.wait_ge(G["f_hq"], t + 1)
                if t == 0:
                    pe.wait_ge(G["b_pt_d"], 2 * NT)
                else:
                    pe.wait_ge(G["f_hqT_sb"], t)
                o = PS[5][:, :].bitcast(BF16)
                for k in range(FF // P):
                    ins = mm(o[:, k * P:(k + 1) * P], hq[:, t % 2, k * P:(k + 1) * P], ident16[:, :], is_transpose=True)
                ins.then_inc(G["f_hqT"], 1)

            def f_down(t):
                pe.wait_ge(G["f_hqT_sb"], t + 1)
                pe.wait_ge(G["ln_var"], 2 * NT - 1 if t == 0 else 2 * NT + t)
                for k in range(FF // P):
                    ins = mm(PS[6][:, 0:E], hqT[:, t % 2, k, :], w_ff[:, 2, k * E:(k + 1) * E], start=k == 0, stop=k == FF // P - 1)
                ins.then_inc(G["f_y"], 1)

            def d_fold(t):
                if t == 0:
                    pe.wait_ge(G["ld_lat"], 96)
                    pe.wait_ge(G["ld_wq"], 32)
                    pe.wait_ge(G["ld_wo"], 16)
                    pe.wait_ge(G["ln_var"], 2 * NT)
                else:
                    pe.wait_ge(G["d_w_sb"], 2 * t)
                g = 2 * t // (H1 // KV1)
                for k in range(KT):
                    for i in range(2):
                        at = (2 * k + i) * LAT
                        mm(PS[7][:, at:at + LAT], w_qT[:, 2 * t + i, k * P:(k + 1) * P], w_kd[:, g, :])
                for i in range(2):
                    ins = mm(PS[7][i * LAT:(i + 1) * LAT, 256:256 + E], w_vd[:, g, :], w_oh[:, 2 * t + i, :])
                ins.then_inc(G["d_w"], 1)

            pe.wait_ge(G["w_tern"], 3)
            for t in range(NT + 1):
                if t < NT:
                    if t % TPB == 0:
                        f_transpose(t // TPB)
                    f_gate_up(t)
                if t > 0:
                    f_hiddenT(t - 1)
                    d_fold(t - 1)
                    f_down(t - 1)
                if t >= 3 and t % TPB:
                    pe.wait_ge(G["f_qT_sb"], t // TPB + 1)
                    to_xT(1, t // TPB - 1)
            to_xT(1, B - 1)

            def d_latent(b):
                seq = lambda k: xT[:, k, b * S:(b + 1) * S]
                pe.wait_ge(G["xT_done"], B + b + 1)
                if b == 0:
                    pe.wait_ge(G["d_w_sb"], 2 * PAIRS)
                elif b == 1:
                    pe.wait_ge(G["d_k_sb"], 2)
                else:
                    pe.wait_ge(G["ln_var"], 3 * NT + 2 * (b - 1))
                project(PS[7][0:LAT, 0:S], lambda k: w_kvc[:, k, :], seq)
                for t in range(TPB):
                    ins = project(PS[7][:, S + t * LAT:S + (t + 1) * LAT], lambda k: xT[:, k, b * S + t * P:b * S + (t + 1) * P],
                                  lambda k: w_kvc[:, k, :])
                ins.then_inc(G["d_c"], 1)

            def d_keys(b, h):
                pe.wait_ge(G["d_c_sb"], 2 * b + 2)
                if h == 1:
                    pe.wait_ge(G["d_k_sb"], 2 * b + 1)
                for i in range(2):
                    ins = mm(PS[7][:, i * S:(i + 1) * S], w_ki[:, 2 * h + i, :], cT[0:LAT, :])
                ins.then_inc(G["d_k"], 1)

            def d_query(p):
                b, q = divmod(p, PAIRS)
                pe.wait_ge(G["xT_done"], B + b + 1)
                if p == 0:
                    pe.wait_ge(G["xT_done"], 2 * B)
                elif p == 1:
                    pe.wait_ge(G["f_sig"], 2 * NT)
                else:
                    pe.wait_ge(G["d_q_sb"], p - 1)
                for i in range(2):
                    ins = project(PS[p % 2][:, i * S:(i + 1) * S], lambda k: w_qe[:, k, 2 * q + i, :],
                                  lambda k: xT[:, k, b * S:(b + 1) * S])
                ins.then_inc(G["d_q"], 1)

            def d_scores(h):
                p, b, g = h // 2, h // H1, (h % H1) // (H1 // KV1)
                pe.wait_ge(G["d_q_sb"], p + 1)
                pe.wait_ge(G["d_k_sb"], 2 * b + 2)
                o = PS[2 + h % 2]
                if h < 2:
                    pe.wait_ge(*((G["f_h"], 2 * NT) if h == 0 else (G["f_sig"], 2 * NT)))
                else:
                    pe.wait_ge(G["d_exp"], 2 * (h - 2) + 2)
                q = qe[:, p % 3, h % 2, :]
                k = kg[:, b % 2, g, :]
                mm(o[:, 0:3 * P], ident16[:, :], cbias[:, :], stop=False)
                mm(o[:, 0:P], q[:, 0:P], k[:, 0:P], start=False, stop=False)
                mm(o[:, P:3 * P], q[:, P:S], k, start=False, stop=True).then_inc(G["d_s"], 1)

            def d_transpose(h):
                pe.wait_ge(G["d_norm"], 2 * h + 2)
                if h < 2:
                    pe.wait_ge(*((G["f_h"], 2 * NT) if h == 0 else (G["f_hqT_sb"], NT)))
                else:
                    pe.wait_ge(G["d_t_sb"], h - 1)
                for c in range(3):
                    ins = mm(PS[4 + h % 2][:, c * P:(c + 1) * P], dp[:, h % 6, c, :], ident, is_transpose=True)
                ins.then_inc(G["d_t"], 1)

            def d_values(p):
                b = p // PAIRS
                pe.wait_ge(G["d_t_sb"], 2 * p + 2)
                if p == 0:
                    pe.wait_ge(G["ln_var"], 3 * NT)
                else:
                    pe.wait_ge(G["d_o_sb"], p)
                for h in (2 * p, 2 * p + 1):
                    o = PS[6][(h % 2) * LAT:(h % 2 + 1) * LAT, :]
                    mm(o[:, 0:S], cR[:, b % 2, 0, :], dpT[:, h % 4, 0:S], stop=False)
                    ins = mm(o[:, P:S], cR[:, b % 2, 1, :], dpT[:, h % 4, S:3 * P], start=False)
                ins.then_inc(G["d_o"], 1)

            def d_out(b):
                pe.wait_ge(G["d_o_sb"], PAIRS * (b + 1))
                if b > 0:
                    pe.wait_ge(G["xT_done"], 2 * B + b)
                for t in range(TPB):
                    for i in range(PAIRS):
                        ins = mm(PS[7][:, t * E:(t + 1) * E], doT[:, i, t * P:(t + 1) * P], w_vo[:, i, :], start=i == 0, stop=i == PAIRS - 1)
                ins.then_inc(G["d_y"], 1)

            pe.wait_ge(G["ld_cbias"], 16)
            pe.wait_ge(G["d_rot"], 6 * (1 + KT))
            d_latent(0)
            d_keys(0, 0)
            d_keys(0, 1)
            d_query(0)
            NP = B * PAIRS
            for p in range(NP + 4):
                b, q = divmod(p, PAIRS)
                if q == 3 and b > 0:
                    d_out(b - 1)
                if q == 4 and b + 1 < B:
                    d_latent(b + 1)
                if p + 1 < NP:
                    if q == 5 and b + 1 < B:
                        d_keys(b + 1, 0)
                        d_keys(b + 1, 1)
                    d_query(p + 1)
                if q == 6 and b > 0:
                    pe.wait_ge(*((G["d_k_sb"], 2 * b + 4) if b + 1 < B else (G["ln_var"], 3 * NT + 2 * b)))
                    to_xT(2, b - 1)
                if p < NP:
                    d_scores(2 * p)
                    d_scores(2 * p + 1)
                if 2 <= p < NP + 2:
                    d_transpose(2 * p - 4)
                    d_transpose(2 * p - 3)
                if 3 <= p < NP + 3:
                    d_values(p - 3)
            pe.wait_ge(G["ln_var"], 4 * NT)
            to_xT(2, B - 1)

            def e_project(b):
                seq = lambda k: xT[:, k, b * S:(b + 1) * S]
                pe.wait_ge(G["xT_done"], 2 * B + b + 1)
                for n in range(2):
                    if b > 0:
                        pe.wait_ge(*((G["e_qf"], b) if n == 0 else (G["e_eg"], 2 * b)))
                    else:
                        pe.wait_ge(G["d_q_sb"], NP)
                    for f in range(KT):
                        ins = project(PS[n][:, f * S:(f + 1) * S], lambda k: w_x1[:, 2 + n, k, f * P:(f + 1) * P], seq)
                    ins.then_inc(G["e_qg"], 1)

            def e_attend(b):
                pe.wait_ge(G["e_qf"], b + 1)
                pe.wait_ge(*((G["e_at"], b) if b else (G["d_exp"], 4 * NP)))
                for bank, w in ((2, kvbd), (3, dsum)):
                    for f in range(KT):
                        ins = mm(PS[bank][:, f * S:(f + 1) * S], w[:, b, f, :], qf[:, b % 2, f, :])
                    ins.then_inc(G["e_nd"], 1)

            def e_out(b):
                pe.wait_ge(G["e_at"], b + 1)
                pe.wait_ge(*((G["ln_var"], 4 * NT + 2 * b) if b else (G["d_t_sb"], 2 * NP)))
                for t in range(TPB):
                    ins = project(PS[4][:, t * E:(t + 1) * E], lambda k: eat[:, b % 2, k, t * P:(t + 1) * P], lambda k: w_x1[:, 4, k, :])
                ins.then_inc(G["e_y"], 1)

            def r_logits(b):
                pe.wait_ge(G["xT_done"], 3 * B + b + 1)
                if b > 0:
                    pe.wait_ge(G["r_act"], 2 * b - 1)
                else:
                    pe.wait_ge(G["d_o_sb"], NP)
                for t in range(TPB):
                    ins = project(PS[6][:, t * NE:(t + 1) * NE], lambda k: xT[:, k, b * S + t * P:b * S + (t + 1) * P],
                                  lambda k: w_rt[:, k, :])
                ins.then_inc(G["r_log"], 1)

            def r_count(b):
                pe.wait_ge(G["r_kept"], b + 1)
                if b > 0:
                    pe.wait_ge(G["r_rows"], 2 * b)
                else:
                    pe.wait_ge(G["r_set"], 2)
                    pe.wait_ge(G["xT_done"], 3 * B)
                for t in range(2 * b, 2 * b + 2):
                    o = PS[7][:, (t % 2) * NE:(t % 2 + 1) * NE]
                    for u in range(t):
                        mm(o, ones16, kept16[:, u, :], start=u == 0, stop=False)
                    ins = mm(o, before16, kept16[:, t, :], start=t == 0)
                if b == B - 1:
                    for t in range(NT):
                        ins = mm(PS[7][:, TPB * NE:TPB * NE + NE], ones16, kept16[:, t, :], start=t == 0, stop=t == NT - 1)
                ins.then_inc(G["r_count"], 1)

            for b in range(B + 2):
                if b < B:
                    e_project(b)
                    e_attend(b)
                if 1 <= b <= B:
                    e_out(b - 1)
                if b >= 2:
                    pe.wait_ge(*((G["xT_done"], 3 * B + b - 2) if b > 2 else (G["d_t_sb"], 2 * NP)))
                    to_xT(3, b - 2)
                    r_logits(b - 2)
                    r_count(b - 2)

            def expert(i):
                return pe.value_load(table[0:1, 0, bass.ds(i, 1)], min_val=0, max_val=NE - 1)

            def m_tokens(slot, count):
                pe.wait_ge(G[f"m_x{slot}"], count)
                for k in range(KT):
                    ins = mm(PS[5][:, k * P:(k + 1) * P], xg[:, slot, k * P:(k + 1) * P], ident, is_transpose=True)
                ins.then_inc(G["m_xT"], 1)

            def m_half(n, e, slot, s):
                ins = project(PS[n][:, :], lambda k: xgT[:, slot, k, :],
                              lambda k: w_all[:, bass.ds(e, 1), (n * KT + k) * FI:(n * KT + k + 1) * FI])
                ins.then_inc(G[s], 1)

            def m_hiddenT(i):
                pe.wait_ge(G["m_h"], i + 1)
                for m in range(FM):
                    ins = mm(PS[2][:, m * P:(m + 1) * P], hs[:, m * P:(m + 1) * P], ident, is_transpose=True)
                ins.then_inc(G["m_hT"], 1)

            def m_down(i, e, free=True):
                pe.wait_ge(G["m_hT_sb"], i + 1)
                if free:
                    pe.wait_ge(G["m_y_sb"], i)
                for m in range(FM):
                    at = 2 * KT * FI + m * E
                    ins = mm(PS[4][:, 0:E], hT[:, m, :], w_all[:, bass.ds(e, 1), at:at + E], start=m == 0, stop=m == FM - 1)
                ins.then_inc(G["m_y"], 1)

            def m_step(i, h, slot, first=False, last=False, free=True):
                e = expert(i)
                pe.wait_ge(G["m_xT_sb"], i + 1)
                m_half(0, e, slot, "m_g")
                if not first:
                    m_hiddenT(i - 1)
                if not last:
                    m_tokens(1 - slot, (h + (2 if slot else 1)) * 16)
                m_half(1, e, slot, "m_u")
                if not first:
                    m_down(i - 1, expert(i - 1), free)

            pe.wait_ge(G["ld_exp"], 16 * NE)
            pe.wait_ge(G["r_table"], 1)
            m_tokens(0, 16)
            m_step(0, 0, 0, first=True)
            m_step(1, 0, 1, free=False)
            m_step(2, 1, 0)
            with pe.Fori(1, TILES // 2 - 1) as h:
                m_step(h * 2 + 1, h, 1)
                m_step(h * 2 + 2, h + 1, 0)
            m_step(TILES - 2, TILES // 2 - 1, 1)
            m_step(TILES - 1, TILES // 2, 0, last=True)
            m_hiddenT(TILES - 1)
            m_down(TILES - 1, expert(TILES - 1))


def pack(w):
    return np.ascontiguousarray(w.reshape(-1, P, w.shape[1]).transpose(1, 0, 2))


def kernel(**inputs):
    import concourse.bacc as bacc
    from concourse.bass_utils import run_bass_kernel_spmd as run

    i = {k: np.asarray(v) for k, v in inputs.items() if k != "mask_BxSx4224_bf0"}
    x = i["x"].reshape(B * S, E)
    a = {"x": x, "xT": pack(x.T), "cst": constants(), "cbias": causal_bias()}
    a["w_qkv"] = pack(i["L0_attn_w_qkv"].T)
    w_o0 = np.zeros((H0, D0P, E), np.float32)
    w_o0[:, :D0] = i["L0_attn_w_out"].T.reshape(H0, D0, E)
    a["w_o0"] = pack(w_o0.reshape(H0 * D0P, E))
    for n, k in enumerate("qkvo"):
        a[f"w_x0_{n}"] = pack(i[f"L0_xattn_w{k}"].T)
    a["ctx"] = i["ctx_2048"]
    a["ctxT"] = np.ascontiguousarray(i["ctx_2048"].transpose(0, 2, 1).reshape(B, KT, P, CTX).transpose(0, 2, 1, 3))
    wkv = i["L1_xattn_Wkv"]
    for n, w in enumerate((wkv[:E], wkv[E:], i["L1_xattn_Wq"], i["L1_xattn_Wg"], i["L1_xattn_Wo"])):
        a[f"w_x1_{n}"] = pack(w.T)
    a["bg"] = np.ascontiguousarray(i["L1_xattn_bg"].reshape(KT, P).T)
    for n, k in enumerate(("gate", "up", "down")):
        a[f"w_f{n}"] = pack(i[f"L0_ffn_w_{k}"].T).reshape(P, 2 * FF)
    a["w_kvc"] = pack(i["L1_attn_Wkvc"])
    a["eye4"] = np.ascontiguousarray(np.broadcast_to(np.eye(LAT, dtype=np.float32)[:, None], (LAT, KV1, LAT)))
    halves = lambda w, h: w.reshape(-1, h, RH, 2).transpose(0, 1, 3, 2).reshape(-1, h, RD)
    a["w_kr"] = np.ascontiguousarray(halves(i["L1_attn_Wkrope"], KV1))
    a["w_kd"] = np.ascontiguousarray(i["L1_attn_Wkdec"].reshape(LAT, KV1, HD).transpose(2, 1, 0))
    a["w_vd"] = np.ascontiguousarray(i["L1_attn_Wvdec"].reshape(LAT, KV1, HD).transpose(2, 1, 0))
    a["w_rt"] = pack(i["L1_ffn_w_gate"])
    a["w_qT"] = np.ascontiguousarray(i["L1_attn_Wq"].reshape(E, H1, HD).transpose(2, 1, 0))
    a["w_qr"] = np.ascontiguousarray(halves(i["L1_attn_Wqrope"], H1).reshape(KT, P, H1, RD).transpose(1, 0, 2, 3))
    a["w_oh"] = np.ascontiguousarray(i["L1_attn_Wo"].reshape(H1, HD + RD, E)[:, :HD].transpose(1, 0, 2))
    per = lambda w: w.reshape(NE, -1, P, w.shape[2]).transpose(2, 0, 1, 3).reshape(P, NE, -1)
    a["w_exp"] = np.concatenate([per(i[f"L1_ffn_w{n}"]) for n in (1, 3, 2)], axis=2)

    nc = bacc.Bacc("TRN2", target_bir_lowering=False, num_devices=1)
    dr = {k: nc.dram_tensor(f"in_{k}", v.shape, F32, kind="ExternalInput").ap() for k, v in a.items()}
    out = nc.dram_tensor("out", (B * S, E), F32, kind="ExternalOutput").ap()
    xs = nc.dram_tensor("xs", (ROWS, E), F32, kind="Internal").ap()
    ys = nc.dram_tensor("ys", (TILES * P, E), F32, kind="Internal").ap()
    build(nc, dr, xs, ys, out)
    r = run(nc, [{f"in_{k}": v for k, v in a.items()}], core_ids=[0])
    return r.results[0]["out"].reshape(B, S, E)
```

```python
import numpy as np
import concourse.bass as bass
from concourse import mybir
from contextlib import ExitStack

F32 = mybir.dt.float32
F32R = mybir.dt.float32r
BF16 = mybir.dt.bfloat16
U32 = mybir.dt.uint32
I32 = mybir.dt.int32
ACT = mybir.ActivationFunctionType
ALU = mybir.AluOpType
AX = mybir.AxisListType.X

P = 128
B, S, E = 4, 256, 256
KT = E // P
TPB = S // P
NT = B * TPB
LN_EPS = 1e-5
H0, D0, WIN = 16, 16, 64
FILLS = 8
D0P = 32
CTX = 1601
CB = -(-CTX // P)
CLAST = CTX - (CB - 1) * P
CP = -(-CB // 2)
KEYS = CTX + S
CCOLS = [(0, 512), (512, 1024), (1024, KEYS - 511), (KEYS - 512, CTX)]
TCOLS = CCOLS[:3] + [(KEYS - 511, CTX)]
SCOLS = CCOLS[:2] + [(1024, KEYS - 512), (KEYS - 512, KEYS)]
RBLOCKS = [(0, 4), (4, 8), (8, CB)]
RSTEPS = (0, 1, 3)
NR = len(RBLOCKS) + 1
FF = 1024
QMAX = 127.0
Q_EPS = 1e-5
MAGIC = 1.5 * 2.0 ** 23
H1, KV1, HD, RD, LAT = 16, 4, 128, 64, 64
RH = RD // 2
SC1 = float(HD + RD) ** -0.5
PAIRS = H1 // 2
Z_EPS = 1e-6
DX = 16
HT = P // DX
NE, TOPK, FI = 8, 2, 512
CAP = 30.0
FM = FI // P
TOKENS = B * S
TILES = TOKENS * TOPK // P + NE - 1
ROWS = NE * TOKENS + (TILES - TOKENS * TOPK // P) * P
EXP_W = 2 * KT * FI + FM * E

C_ID, C_WMASK, C_BLK, C_HM, C_TRI, C_COS, C_SIN, C_THR, C_EROW, C_TILE, C_TOK, C_N = (
    int(n) for n in np.cumsum([0, P, 2 * P, P, 8, NE * NE, H1 * RH, H1 * RH, NE, NE, TILES, TOPK * NT]))
NEG = -1e30
LO, HI = 0, 1
KBANKS = (4, 5, 0, 1)


def constants():
    c = np.zeros((P, C_N), np.float32)
    c[:, C_ID:C_ID + P] = np.eye(P)
    q, k = np.arange(P)[:, None], np.arange(P)[None, :]
    d0 = q - k
    d1 = (q % WIN) + WIN - k
    c[:, C_WMASK:C_WMASK + P] = np.where((d0 >= 0) & (d0 <= WIN), 0, NEG)
    c[:, C_WMASK + P:C_WMASK + 2 * P] = np.where((d1 >= 0) & (d1 <= WIN), 0, NEG)
    c[:, C_BLK:C_BLK + P] = (q // D0) == (k // D0)
    c[:, C_HM:C_HM + 8] = (np.arange(P)[:, None] // D0) == np.arange(8)[None, :]
    c[:, C_TRI:C_TRI + NE * NE] = (np.arange(NE)[None, :] < np.arange(NE)[:, None]).reshape(1, -1)
    c[:, C_THR:C_THR + NE] = P * np.arange(NE)
    c[:, C_EROW:C_EROW + NE] = TOKENS * np.arange(NE) + 1
    c[:, C_TILE:C_TILE + TILES] = np.arange(TILES)
    c[:, C_TOK:C_TOK + NT] = 1 + P * np.arange(NT)[None, :] + np.arange(P)[:, None]
    c[:, C_TOK + NT:C_TOK + 2 * NT] = TOKENS
    freqs = (1.0 / np.float32(10000.0) ** (np.arange(0, RD, 2, dtype=np.float32) / np.float32(RD))).astype(np.float32)
    ang = np.outer(np.arange(H1, dtype=np.float32), freqs).astype(np.float32)
    c[:, C_COS:C_COS + H1 * RH] = np.cos(ang).reshape(1, -1)
    c[:, C_SIN:C_SIN + H1 * RH] = np.sin(ang).reshape(1, -1)
    return c


def causal_bias():
    d = np.where(np.arange(P)[:, None] >= np.arange(P)[None, :], 0, NEG)
    return np.concatenate([d, np.zeros((P, P)), d], 1).astype(np.float32)


def build(nc, d, xs, ys, out):
    with ExitStack() as ctx:
        def sb(name, shape, dt=F32):
            return ctx.enter_context(nc.sbuf_tensor(name, shape, dt))

        def same_place(**sizes):
            with ExitStack() as names:
                return [names.enter_context(nc.sbuf_tensor(name, [P, n], F32R)) for name, n in sizes.items()]

        def sem(name):
            return ctx.enter_context(nc.semaphore(name))

        class Region:

            def __init__(self, base, words):
                self.base, self.words = base, words
                self.at = 0

            def start(self, at=0):
                self.at = at

            def cut(self, *shape, dt=F32):
                n = int(np.prod(shape))
                words = -(-n // 2) if dt == BF16 else n
                assert self.at + words <= self.words, (self.at, words, self.words)
                v = arena[:, self.base + self.at:self.base + self.at + words]
                self.at += words
                if dt != F32:
                    v = v.bitcast(dt)
                names = " ".join("abcd"[:len(shape)])
                if len(shape) == 1:
                    return v
                return v.rearrange(f"p ({names}) -> p {names}", **dict(zip("abcd", shape)))

        PS = [ctx.enter_context(nc.psum_tensor(f"bank{i}", [P, 512], F32)) for i in range(8)]

        cst = sb("cst", [P, C_N])
        ident = cst[:, C_ID:C_ID + P]
        blk = cst[:, C_BLK:C_BLK + P]
        hmask = cst[:, C_HM:C_HM + 8]
        tri = cst[:, C_TRI:C_TRI + NE * NE].rearrange("p (a b) -> p a b", a=NE)
        ident16 = sb("ident16", [P, P], BF16)
        cbias = sb("cbias", [P, 3 * P], BF16)
        ones = sb("ones", [P, P])
        magic = sb("magic", [P, 1])
        mhalf = sb("mhalf", [P, 1])
        x_ids = sb("x_ids", [P, NT, E + 2])
        x_row = x_ids[:, :, 0:E]
        xT = sb("xT", [P, KT, B * S])
        res = sb("res", [P, 4, E])
        stats = sb("stats", [P, 4, 6])
        mv = sb("mv", [P, 4, 2])
        nmr = sb("nmr", [P, 4])
        rstd = sb("rstd", [P, 4])
        w_qkv = sb("w_qkv", [P, KT, 3 * E])
        w_x0 = sb("w_x0", [P, 4, KT, E])
        w_x1_split, = same_place(w_x1_split=5 * KT * E)
        w_x1 = sb("w_x1", [P, 5, KT, E])
        wk_hi = sb("wk_hi", [P, KT, E], F32R)
        bg = sb("bg", [P, KT])
        kvd = sb("kvd", [P, B, KT, P + HT])
        w_ff = sb("w_ff", [P, 3, 2 * FF], BF16)
        wabs = sb("wabs", [P, 3])
        wsc = sb("wsc", [P, 3])
        wsi = sb("wsi", [P, 3])
        w_kvc = sb("w_kvc", [P, KT, LAT])
        w_kr = sb("w_kr", [LAT, KV1, RD])
        w_ki = sb("w_ki", [LAT, KV1, P])
        w_kd = sb("w_kd", [P, KV1, LAT])
        w_vd = sb("w_vd", [P, KV1, LAT])
        w_rt = sb("w_rt", [P, KT, NE])

        CT_W, CR_W = KT * CTX, CB * (E + 2)
        SLOT = CT_W + CR_W
        N2, N1, N3 = 3 * 2 * FF, -(-2 * SLOT // 8) * 8, 13312
        U2_split, U1_split, U3_split = same_place(U2_split=N2, U1_split=N1, U3_split=N3)
        arena = sb("arena", [P, N2 + N1 + N3])
        U2, U1, U3 = Region(0, N2), Region(N2, N1), Region(N2 + N1, N3)
        ctxT, ctxR = [None, None], [None, None]
        for n in (LO, HI):
            U1.start(n * SLOT)
            ctxT[n] = U1.cut(KT, CTX)
            ctxR[n] = U1.cut(CB, E + 2)
        U1.start(SLOT)
        vpad = U1.cut(2, 3, H0 * D0P)
        w_o0 = U1.cut(H0 * D0P // P, E)
        oT = U1.cut(H0 * D0P // P, S)
        wmask16 = U1.cut(2, P, dt=BF16)
        zeros = U1.cut(E + 2)
        U1.start(0)
        w_qe = U1.cut(KT, H1, P)
        w_vo = U1.cut(PAIRS, E)
        w_qT = U1.cut(H1, E)
        w_qr_at = U1.at
        w_qr = U1.cut(KT, H1, RD)
        w_rot = U1.cut(H1, RH)
        U1.start(KT * H1 * P + PAIRS * E)
        w_qh = U1.cut(KT, H1, P)
        U1.start(w_qr_at)
        dx = [U1.cut(2, KT, S), U1.cut(2, KT, S)]
        w_f32 = U2.cut(3, 2 * FF)
        U2.start(0)
        w_oh = U2.cut(H1, E)
        w_vh = U2.cut(PAIRS, E)
        qT = U3.cut(2, KT, S)
        kmask = U3.cut(2, KT, 8, S)
        sm = U3.cut(4, 4, P)
        PT = U3.cut(4, 4, P)
        U3.start(0)
        pair = lambda *shape: [U3.cut(*shape), U3.cut(*shape)]
        xq = pair(KT, S)
        xk = pair(KT, S)
        xv = pair(TPB, E)
        prob = U3.cut(KEYS + 1)[:, 0:KEYS]
        probT = pair(CB + TPB, P)
        ek_at = U3.at
        kf_lo = U3.cut(3, 2 * E)
        kf_at = U3.at
        kf_hi = U3.cut(2, 2 * E)
        xo = U3.cut(E)
        xoT = U3.cut(KT, P)
        fr = U3.cut(E)
        fq = U3.cut(NT, E, dt=BF16)
        U3.start(ek_at)
        m1 = U3.cut(KT, E + 2)
        U3.start(kf_at)
        m1T = U3.cut(KT, E)
        U3.start(2560)
        fqT = U3.cut(2, KT, S, dt=BF16)
        sg = U3.cut(2, 512)
        hh = U3.cut(2, FF)
        hr = U3.cut(FF)
        hq = U3.cut(2, FF, dt=BF16)
        hqT = U3.cut(2, FF // P, P, dt=BF16)
        U3.start(0)
        cT = U3.cut(S)
        cR = U3.cut(2, TPB, LAT)
        kg = U3.cut(2, KV1, S)
        qe = U3.cut(3, 2, S)
        dp = U3.cut(6, 3, P)
        dpT = U3.cut(4, 3 * P)
        DO_RING = PAIRS + 2
        doT = pair(DO_RING, S)
        w_all = arena[:, 0:NE * EXP_W].rearrange("p (e w) -> p e w", e=NE)
        late = Region(NE * EXP_W, N2 + N1 + N3 - NE * EXP_W)
        eq = late.cut(2, 512)
        qf = late.cut(2, KT, S)
        eat = late.cut(2, KT, S)
        eav = late.cut(2, TPB, E)
        late.start(9984 - (NE * EXP_W - N2 - N1))
        gate = late.cut(B, KT, S)
        router_at = late.at
        late.start(0)
        xg = late.cut(2, E + 2)
        xgT = late.cut(2, KT, P)
        sa = late.cut(FI)
        hs = late.cut(FI)
        hT = late.cut(FM, P)
        yt = late.cut(2, E)
        late.start(router_at)
        rt = late.cut(NT, NE)
        rt2 = late.cut(NT, NE)
        wgt = late.cut(NT, NE)
        slots = late.cut(NT, NE)
        rtop = late.cut(NT)
        rsm = late.cut(NT)
        rsi = late.cut(NT)
        shi = late.cut(NT)
        ssm = late.cut(NT)
        w_lo, w_hi = late.cut(NT), late.cut(NT)
        rcmp = late.cut(TPB, NE, NE)
        rcm2 = late.cut(TPB, NE, NE)
        kept16 = late.cut(NT, NE, dt=BF16)
        before16 = late.cut(P, dt=BF16)
        ones16 = late.cut(P, dt=BF16)
        tok_rows = late.cut(2, NT, dt=U32)
        y_ids = late.cut(2, dt=U32)
        chosen = late.cut(NT, NE)
        etiles = late.cut(NE)
        eends = late.cut(NE)
        eskip = late.cut(NE)
        tcmp = late.cut(TILES, NE)
        tab = late.cut(2, TILES)
        table = late.cut(2, TILES, dt=I32)
        y_lo = arena[:, 0:NT * E].rearrange("p (t e) -> p t e", t=NT)
        y_hi = arena[:, NT * E:2 * NT * E].rearrange("p (t e) -> p t e", t=NT)
        mx = sb("mx", [P, 8, 4])
        rsum = sb("rsum", [P, 8, 4])
        rinv = sb("rinv", [P, 8, 4])
        bmx = sb("bmx", [P, 8])
        bsum = sb("bsum", [P, 8])
        fs = sb("fs", [P, NT, 8])
        fh = sb("fh", [P, 2, 8])
        dmx = sb("dmx", [P, 8, 2])
        dsm = sb("dsm", [P, 8, 2])
        dri = sb("dri", [P, 8, 2])
        eri = sb("eri", [P, TPB, KT * HT])

        names = """ld_const ld_x ld_xrow ld_attn0 ld_x0 ld_x1 ld_ctxT ld_ctxR ld_ffn ld_lat ld_cbias ld_wq ld_wo ld_out
            const_set ln_var ln_rstd ln_done xT_raw xT_done
            a_q a_k0 a_k1v0 a_v12 a_q_sb a_k0_sb a_k1_sb a_v_sb a_s a_max a_exp a_rinv a_norm
            a_pt a_pt_even a_pt_odd a_o a_o_sb a_y ld_rest ld_wo0
            b_q b_k b_v hi_part lo_part c_Thi c_Tlo c_Rhi c_Rlo wk_split b_s b_max b_exp b_t b_pt_hi b_pt b_o b_o_sb b_ot b_ot_sb b_y
            x_k x_exp x_kf x_kf_hi x_kf_lo x_m1 x_m1_sb x_m1T x_m1T_sb x_kv x_kvbd
            w_abs w_sum w_scale w_round w_tern
            f_sc f_fac f_round f_q f_qT f_qT_sb f_gu f_sig f_h f_hsc f_hround f_hq f_hqT f_hqT_sb f_y
            d_w d_w_sb d_c d_c_sb d_k d_k_sb d_rot d_q d_q_sb d_s d_max d_exp d_rinv d_norm
            d_t d_t_sb d_o d_o_sb d_o_lo d_y
            e_g e_sig e_q e_exp e_qf e_nd e_av e_avT e_at e_y
            ld_zero ld_exp r_set r_log r_act r_exp r_v r_kept r_count r_rows m_ids r_scat r_table
            m_x0 m_x1 m_xT m_xT_sb m_g m_u m_silu m_h m_hT m_hT_sb m_y m_y_sb m_st0 m_st1
            y_got01 y_got23 y_got45 y_got67
            dve_step pool_step""".split()
        G = {n: sem(n) for n in names}
        y_got = ("y_got01", "y_got23", "y_got45", "y_got67")

        def split_of(b):
            return (1, PAIRS + 2, 2 * PAIRS + 3, 2 * PAIRS + 4)[b]

        def r32(a):
            if a.dtype == F32R:
                return a
            at = a.offset
            if a.tensor.name == w_x1.name:
                t, rows = w_x1_split, 5 * KT * E
            else:
                t, rows = U2_split, N2
                if at >= N2:
                    t, rows, at = U1_split, N1, at - N2
                if at >= N1 and t is U1_split:
                    t, rows, at = U3_split, N3, at - N1
            assert at < rows
            return bass.AP(t, at, [[rows, a.ap[0][1]]] + list(a.ap[1:]))

        xs_words = xs.rearrange("r w -> (r w)").unsqueeze(1)
        block = ctx.enter_context(nc.Block())
        PS_xT = [PS[5], PS[0], PS[7], PS[6]]

        @block.sync
        def _(sp):
            def load(dst, src, s):
                sp.dma_start(dst, src).then_inc(G[s], 16)

            load(xT[:, :, 0:S], d["xT"][:, :, 0:S], "ld_x")
            load(w_qkv[:, :, :], d["w_qkv"], "ld_attn0")
            load(cst[:, :], d["cst"], "ld_const")
            load(xT[:, :, S:B * S], d["xT"][:, :, S:B * S], "ld_rest")
            load(w_o0, d["w_o0"], "ld_wo0")
            load(x_row[:, :, :], d["x"].rearrange("(t p) e -> p t e", p=P), "ld_xrow")
            for n in range(4):
                load(w_x0[:, n, :, :], d[f"w_x0_{n}"], "ld_x0")

            def load_ctxT(b):
                load(ctxT[LO], d["ctxT"][b], "ld_ctxT")

            def load_ctxR(b):
                src = d["ctx"][b]
                load(ctxR[LO][:, 0:CB - 1, 0:E], src[0:(CB - 1) * P, :].rearrange("(t p) e -> p t e", p=P), "ld_ctxR")
                load(ctxR[LO][0:CLAST, CB - 1, 0:E], src[(CB - 1) * P:CTX, :], "ld_ctxR")

            load_ctxT(0)
            load_ctxR(0)
            for n in range(5):
                load(w_x1[:, n, :, :], d[f"w_x1_{n}"], "ld_x1")
            load(bg[:, :], d["bg"], "ld_x1")
            for n in range(3):
                load(w_f32[:, n, :], d[f"w_f{n}"], "ld_ffn")
            sp.wait_ge(G["const_set"], 6)
            xs_tiles = xs.rearrange("(t p) e -> p t e", p=P)
            for at in range(0, ROWS // P, NT):
                n = min(NT, ROWS // P - at)
                load(xs_tiles[:, at:at + n, :], zeros.unsqueeze(1).broadcast_to([P, n, E + 2]), "ld_zero")
            load(w_kvc[:, :, :], d["w_kvc"], "ld_lat")
            load(w_ki[:, :, 0:LAT], d["eye4"], "ld_lat")
            load(w_kr[:, :, :], d["w_kr"], "ld_lat")
            load(w_kd[:, :, :], d["w_kd"], "ld_lat")
            load(w_vd[:, :, :], d["w_vd"], "ld_lat")
            load(w_rt[:, :, :], d["w_rt"], "ld_lat")
            for b in range(1, B):
                sp.wait_ge(G["b_s"], 4 * TPB * b)
                sp.wait_ge(G["x_k"], CP * b)
                load_ctxT(b)
                sp.wait_ge(G["b_o"], TPB * b)
                sp.wait_ge(G["x_m1"], CP * b)
                load_ctxR(b)
            sp.wait_ge(G["w_tern"], 3)
            load(w_oh, d["w_oh"], "ld_wo")
            sp.wait_ge(G["b_o"], 2 * B)
            load(w_qT, d["w_qT"], "ld_wq")
            load(w_qr, d["w_qr"], "ld_wq")
            for n in range(NE):
                if n == 0:
                    sp.wait_ge(G["d_w"], NT)
                if n == 1:
                    sp.wait_ge(G["d_y"], NT)
                    sp.wait_ge(G["d_o"], B * PAIRS)
                load(w_all[:, n, :], d["w_exp"][:, n, :], "ld_exp")

            def load_rows(i, slot):
                row = sp.value_load(table[0:1, 1, bass.ds(i, 1)], min_val=0, max_val=ROWS - P)
                sp.dma_start(xg[:, slot, :], xs[bass.ds(row, P), :]).then_inc(G[f"m_x{slot}"], 16)

            def m_step(i, slot):
                sp.wait_ge(G["m_xT"], i + 1)
                sp.wait_ge(G["m_ids"], i + 1)
                load_rows(i + 2, slot)

            sp.wait_ge(G["r_table"], 2)
            sp.wait_ge(G["r_scat"], 16 * TOPK * NT)
            load_rows(0, 0)
            load_rows(1, 1)
            m_step(0, 0)
            m_step(1, 1)
            m_step(2, 0)
            with sp.Fori(1, TILES // 2 - 1) as h:
                m_step(h * 2 + 1, 1)
                m_step(h * 2 + 2, 0)
            sp.wait_ge(G["m_st0"], 16 * (TILES // 2 + 1))
            sp.wait_ge(G["m_st1"], 16 * (TILES // 2))
            for t in range(0, NT, 2):
                for c, o in enumerate((y_lo, y_hi)):
                    at = 1 + c * TOKENS + t * P
                    load(o[:, t:t + 2, :], ys[at:at + 2 * P, :].rearrange("(t p) e -> p t e", p=P), y_got[t // 2])
            for t in range(NT):
                sp.wait_ge(G["ln_done"], 5 * NT + t + 1)
                sp.dma_start(out[t * P:(t + 1) * P, :], x_row[:, t, :]).then_inc(G["ld_out"], 16)
            sp.wait_ge(G["ld_out"], 16 * NT)

        @block.gpsimd
        def _(pool):
            g = nc.gpsimd
            g.memset(vpad, 0.0).then_inc(G["const_set"], 1)
            g.memset(ones[:, :], 1.0).then_inc(G["const_set"], 1)
            g.memset(magic[:, :], MAGIC).then_inc(G["const_set"], 1)
            g.memset(mhalf[:, :], -0.5).then_inc(G["const_set"], 1)
            pool.wait_ge(G["const_set"], 2)
            g.tensor_scalar(r32(ctxR[LO][:, :, E:E + 2]), ones[:, 0:2 * CB].rearrange("p (t c) -> p t c", t=CB), 0.0, None, ALU.mult).then_inc(G["const_set"], 1)
            g.memset(zeros, 0.0).then_inc(G["const_set"], 1)
            pool.wait_ge(G["ld_const"], 16)
            g.tensor_copy(ident16[:, :], ident).then_inc(G["const_set"], 1)
            g.tensor_copy(wmask16, cst[:, C_WMASK:C_WMASK + 2 * P].rearrange("p (t k) -> p t k", t=2)).then_inc(G["const_set"], 1)
            pool.dma_start(cbias[:, :], d["cbias"]).then_inc(G["ld_cbias"], 16)
            steps = [0]

            def rstd_of(n):
                s = n % 4
                pool.wait_ge(G["ln_var"], n + 1)
                g.tensor_scalar(rstd[:, s:s + 1], mv[:, s, 1:2], LN_EPS, None, ALU.add).then_inc(G["pool_step"], 1)
                steps[0] += 1
                pool.wait_ge(G["pool_step"], steps[0])
                g.tensor_tensor(rstd[:, s:s + 1], rstd[:, s:s + 1], mhalf[:, :], ALU.pow).then_inc(G["ln_rstd"], 1)

            for n in range(FILLS * B + 8):
                b, i = divmod(n, FILLS)
                if n < FILLS * B:
                    pool.wait_ge(G["a_rinv"], n + 1)
                    g.tensor_tensor(sm[:, n % 4, :, :], sm[:, n % 4, :, :],
                                    rinv[:, n % 8, :].unsqueeze(2).broadcast_to([P, 4, P]), ALU.mult).then_inc(G["a_norm"], 1)
                if i == 5 and b > 0:
                    for t in range(TPB):
                        rstd_of(2 * (b - 1) + t)
            pool.wait_ge(G["a_y"], B)
            pool.wait_ge(G["ld_zero"], 16 * (NE + 1))
            g.tensor_scalar(r32(ctxR[HI][:, :, E:E + 2]), ones[:, 0:2 * CB].rearrange("p (t c) -> p t c", t=CB), 1.0, None, ALU.mult).then_inc(G["const_set"], 1)
            for c in range(TOPK):
                g.tensor_copy(x_ids[:, :, E + c], cst[:, C_TOK + c * NT:C_TOK + (c + 1) * NT]).then_inc(G["const_set"], 1)
            for b in range(B):
                if b > 0:
                    rstd_of(NT + 2 * b - 1)
                for n in range(CP * b, CP * (b + 1)):
                    words = 2 * E if n % CP < CP - 1 else E
                    pool.wait_ge(G["x_kf_hi"], n + 1)
                    low, high = r32(kf_lo[:, n % 3, 0:words]), r32(kf_hi[:, n % 2, 0:words])
                    g.tensor_tensor(low, kf_lo[:, n % 3, 0:words], high.bitcast(F32), ALU.subtract).then_inc(G["x_kf_lo"], 1)
                rstd_of(NT + 2 * b)
            rstd_of(2 * NT - 1)

            def rotate(dst, src, parts, heads, half):
                cos = cst[0:parts, C_COS:C_COS + heads * RH].rearrange("p (h r) -> p h r", h=heads)
                sin = cst[0:parts, C_SIN:C_SIN + heads * RH].rearrange("p (h r) -> p h r", h=heads)
                x1, x2 = src[:, :, 0:RH], src[:, :, RH:RD]
                o1, o2 = dst[:, :, 0:RH], dst[:, :, RH:RD]
                t = w_rot[0:parts, 0:heads, :]
                o, a1, b1, op = ((o1, x1, x2, ALU.subtract), (o2, x2, x1, ALU.add))[half]
                for dst1, p0, p1, f in ((o, a1, cos, ALU.mult), (t, b1, sin, ALU.mult), (o, o, t, op)):
                    g.tensor_tensor(dst1, p0, p1, f).then_inc(G["d_rot"], 1)
                    rots[0] += 1
                    pool.wait_ge(G["d_rot"], rots[0])

            rots = [0]
            pool.wait_ge(G["ld_lat"], 96)
            pool.wait_ge(G["ld_wq"], 32)
            for n in range(NT):
                if n < 2:
                    rotate(w_ki[:, :, LAT:P], w_kr[:, :, :], LAT, KV1, n)
                elif n < 2 + 2 * KT:
                    k, half = divmod(n - 2, 2)
                    rotate(w_qe[:, k, :, LAT:P], w_qr[:, k, :, :], P, H1, half)
                rstd_of(2 * NT + n)
            def norm_p(p):
                for h in (2 * p, 2 * p + 1):
                    pool.wait_ge(G["d_rinv"], h + 1)
                    for j, (a, z) in enumerate(((0, 1), (1, 3))):
                        g.tensor_scalar(dp[:, h % 6, a:z, :], dp[:, h % 6, a:z, :], dri[:, h % 8, j:j + 1], 1.0,
                                        ALU.mult, ALU.mult).then_inc(G["d_norm"], 1)

            for p in range(B * PAIRS + 1):
                b, q = divmod(p, PAIRS)
                if p > 0:
                    norm_p(p - 1)
                if q == 5 and b > 0:
                    for t in range(TPB):
                        rstd_of(3 * NT + 2 * (b - 1) + t)
            for t in range(TPB):
                rstd_of(3 * NT + 2 * (B - 1) + t)
            for b in range(B + 2):
                if b < B:
                    for t in range(TPB):
                        rstd_of(4 * NT + 2 * b + t)
                if b >= 2:
                    pool.wait_ge(G["r_rows"], 2 * b - 2)
                if b == 2:
                    pool.wait_ge(G["const_set"], 11)
                for t in range(2 * b - 4, 2 * b - 2) if b >= 2 else ():
                    for c in range(TOPK):
                        z = E + 1 + c
                        g.indirect_dma_start(xs_words, bass.IndirectOffsetOnAxis(ap=tok_rows[:, c, t:t + 1], axis=0),
                                             x_ids[:, t, 0:z], None).then_inc(G["r_scat"], 16)

            def m_ids(i):
                slot = i % 2
                pool.wait_ge(G[f"m_x{slot}"], 16 * (i // 2 + 1))
                if i >= 2:
                    pool.wait_ge(G[f"m_st{slot}"], 16 * (i // 2))
                g.tensor_scalar(y_ids[:, slot:slot + 1], xg[:, slot, E:E + 1], xg[:, slot, E + 1:E + 2], None, ALU.add).then_inc(G["m_ids"], 1)

            m_ids(0)
            for i in range(TILES):
                slot = i % 2
                if i + 1 < TILES:
                    m_ids(i + 1)
                else:
                    pool.wait_ge(G[f"m_st{1 - slot}"], 16 * ((i + 1) // 2))
                pool.wait_ge(G["m_ids"], i + 1)
                pool.wait_ge(G["m_y_sb"], i + 1)
                g.indirect_dma_start(ys, bass.IndirectOffsetOnAxis(ap=y_ids[:, slot:slot + 1], axis=0),
                                     yt[:, slot, :], None).then_inc(G[f"m_st{slot}"], 16)
            for t in range(NT):
                n = 5 * NT + t
                rstd_of(n)
                pool.wait_ge(G["ln_rstd"], 5 * NT + 2 * t + 1)
                g.tensor_scalar(nmr[:, n % 4:n % 4 + 1], mv[:, n % 4, 0:1], rstd[:, n % 4:n % 4 + 1], -1.0,
                                ALU.mult, ALU.mult).then_inc(G["ln_rstd"], 1)

        @block.scalar
        def _(act):
            a = nc.scalar
            act.wait_ge(G["const_set"], 8)

            def xT_copy(stage, b):
                n = stage * B + b
                act.wait_ge(G["xT_raw"], n + 1)
                a.activation(xT[:, :, b * S:(b + 1) * S], PS_xT[stage][:, :].rearrange("p (k t) -> p k t", k=KT),
                             ACT.Copy).then_inc(G["xT_done"], 1)

            def a_query(b):
                act.wait_ge(G["a_q"], b + 1)
                a.activation(qT[:, b % 2, :, :], PS[5][:, :].rearrange("p (k t) -> p k t", k=KT), ACT.Copy,
                             scale=float(D0) ** -0.5).then_inc(G["a_q_sb"], 1)

            def a_values(b, bank, at, w):
                a.activation(vpad[:, b % 2, w, :].rearrange("p (h c) -> p h c", c=D0P)[:, :, 0:D0],
                             PS[bank][:, at:at + E].rearrange("p (h c) -> p h c", c=D0), ACT.Copy).then_inc(G["a_v_sb"], 1)

            def a_keys1(b, g):
                act.wait_ge(G["a_k1v0"], b + 1)
                for h in range(4 * g, 4 * g + 4):
                    a.activation(kmask[:, b % 2, 1, h, :], PS[5][:, 0:S], ACT.Copy, scale=hmask[:, h:h + 1]).then_inc(G["a_k1_sb"], 1)

            def a_outT(b, f):
                act.wait_ge(G["a_o"], 2 * b + f + 1)
                if b > 0 and f == 0:
                    act.wait_ge(G["a_y"], b)
                a.activation(oT[:, 2 * f:2 * f + 2, :], PS[7][:, :].rearrange("p (k t) -> p k t", k=2), ACT.Copy).then_inc(G["a_o_sb"], 1)

            a_query(0)
            a_keys1(0, 0)
            a_values(0, 5, S, 0)
            a_keys1(0, 1)
            for n in range(FILLS * B + 8):
                b, i = divmod(n, FILLS)
                if i == 0 and 0 < b < B:
                    a_keys1(b, 1)
                if n < FILLS * B:
                    act.wait_ge(G["a_max"], n + 1)
                    if n >= 4:
                        act.wait_ge(G["a_pt"], n - 3)
                    for h in range(4):
                        a.activation(sm[:, n % 4, h, :], PS[n % 3][:, h * P:(h + 1) * P], ACT.Exp, bias=mx[:, n % 8, h:h + 1],
                                     accum_out=rsum[:, n % 8, h:h + 1]).then_inc(G["a_exp"], 1)
                if 3 <= n < FILLS * B + 3 and n % 2 == 0:
                    act.wait_ge(G["a_pt"], n - 2)
                    a.activation(PT[:, (n - 3) % 4, :, :], PS[4][:, :].rearrange("p (h q) -> p h q", h=4),
                                 ACT.Copy).then_inc(G["a_pt_odd"], 1)
                if i in (0, 4) and b > 0:
                    a_outT(b - 1, i // 4)
                if i == 3 and b < B:
                    act.wait_ge(G["a_v12"], b + 1)
                    a_values(b, 6, 0, 1)
                    a_values(b, 6, E, 2)
                if i == 3 and b >= 2:
                    xT_copy(0, b - 2)
                if i == 6 and b + 1 < B:
                    a_query(b + 1)
                if i == 7 and b + 1 < B:
                    a_keys1(b + 1, 0)
                    a_values(b + 1, 5, S, 0)
            xT_copy(0, B - 1)

            def hi(out, src, s, **k):
                a.activation(r32(out), src, ACT.Copy, **k).then_inc(G[s], 1)

            def c_split(b):
                act.wait_ge(G["ld_ctxT"], 16 * (b + 1))
                for lo, z in TCOLS:
                    hi(ctxT[HI][:, :, lo:z], ctxT[LO][:, :, lo:z], "c_Thi")

            def c_split_rows(c):
                lo, z = RBLOCKS[c]
                full = min(z, CB - 1)
                hi(ctxR[HI][:, lo:full, 0:E], ctxR[LO][:, lo:full, 0:E], "c_Rhi")
                if z == CB:
                    hi(ctxR[HI][0:CLAST, CB - 1, 0:E], ctxR[LO][0:CLAST, CB - 1, 0:E], "c_Rhi")

            def b_exp(u):
                act.wait_ge(G["b_max"], u + 1)
                for c, (lo, z) in enumerate(SCOLS):
                    a.activation(prob[:, lo:z], PS[c][:, 0:z - lo], ACT.Exp, bias=bmx[:, 4:5],
                                 accum_out=bsum[:, c:c + 1]).then_inc(G["b_exp"], 1)

            def b_probT(u, c):
                nb = 4 if c < 3 else 3
                act.wait_ge(G["b_t"], 4 * u + c + 1)
                hi(probT[HI][:, 4 * c:4 * c + nb, :], PS[4 + c % 2][:, 0:nb * P].rearrange("p (j q) -> p j q", j=nb), "b_pt_hi")

            def b_oT(u):
                act.wait_ge(G["b_ot"], u + 1)
                a.activation(xoT, PS[7 if u % 2 else 6][:, 0:KT * P].rearrange("p (k t) -> p k t", k=KT),
                             ACT.Copy).then_inc(G["b_ot_sb"], 1)

            def f_round(t):
                act.wait_ge(G["f_sc"], t + 1)
                if t > 0:
                    act.wait_ge(G["f_q"], t)
                a.activation(fr, x_row[:, t, :], ACT.Identity, scale=fs[:, t, 2:3],
                             bias=magic[:, :]).then_inc(G["f_round"], 1)

            def x_exp(n):
                c = n % CP
                words = 2 * E if c < CP - 1 else E
                act.wait_ge(G["x_k"], n + 1)
                if n >= 3:
                    act.wait_ge(G["x_m1"], n - 2)
                a.activation(kf_lo[:, n % 3, 0:words], PS[KBANKS[c % 4]][:, 0:words], ACT.Exp).then_inc(G["x_exp"], 1)

            act.wait_ge(G["ld_x1"], 96)
            hi(wk_hi[:, :, :], w_x1[:, 0, :, :], "wk_split")
            c_split(0)
            def b_split_qk(b):
                act.wait_ge(G["b_q"], b + 1)
                hi(xq[HI], PS[0][:, :].rearrange("p (k t) -> p k t", k=KT), "hi_part", scale=float(E) ** -0.5)
                act.wait_ge(G["b_k"], b + 1)
                hi(xk[HI], PS[1][:, :].rearrange("p (k t) -> p k t", k=KT), "hi_part")

            def b_split_v(b):
                act.wait_ge(G["b_v"], b + 1)
                hi(xv[HI], PS[2][:, :].rearrange("p (t e) -> p t e", t=TPB), "hi_part")

            b_split_qk(0)
            b_split_v(0)
            for b in range(B):
                if b > 0:
                    b_oT(2 * b - 1)
                b_exp(2 * b)
                x_exp(CP * b)
                act.wait_ge(G["ld_ctxR"], 32 * (b + 1))
                for c in range(CP):
                    n = CP * b + c
                    words = 2 * E if c < CP - 1 else E
                    if c in RSTEPS:
                        c_split_rows(RSTEPS.index(c))
                    if c + 1 < CP:
                        x_exp(n + 1)
                    act.wait_ge(G["x_kf"], n + 1)
                    if n >= 2:
                        act.wait_ge(G["x_m1"], n - 1)
                    hi(kf_hi[:, n % 2, 0:words], kf_lo[:, n % 3, 0:words], "x_kf_hi")
                    if c in (4, 6) and b > 0:
                        f_round(2 * b - (2 if c == 4 else 1))
                for c in range(4):
                    b_probT(2 * b, c)
                act.wait_ge(G["x_m1T"], b + 1)
                a.activation(m1T, PS[6][:, :].rearrange("p (k t) -> p k t", k=KT), ACT.Copy).then_inc(G["x_m1T_sb"], 1)
                b_exp(2 * b + 1)
                if b + 1 < B:
                    b_split_qk(b + 1)
                for c in range(4):
                    b_probT(2 * b + 1, c)
                if b + 1 < B:
                    c_split(b + 1)
                b_oT(2 * b)
                if b + 1 < B:
                    b_split_v(b + 1)
                if b < 3:
                    act.wait_ge(G["w_scale"], b + 1)
                    a.activation(w_f32[:, b, :], w_f32[:, b, :], ACT.Identity, scale=wsi[:, b:b + 1],
                                 bias=magic[:, :]).then_inc(G["w_round"], 1)
            def d_folded(t):
                act.wait_ge(G["d_w"], t + 1)
                a.activation(w_qe[:, :, 2 * t:2 * t + 2, 0:LAT],
                             PS[7][:, 0:2 * KT * LAT].rearrange("p (k h c) -> p k h c", k=KT, h=2),
                             ACT.Copy).then_inc(G["d_w_sb"], 1)
                a.activation(w_vo[:, t, :], PS[7][:, 256:256 + E], ACT.Copy).then_inc(G["d_w_sb"], 1)

            def d_latent(b):
                act.wait_ge(G["d_c"], b + 1)
                a.activation(cT[0:LAT, :], PS[7][0:LAT, 0:S], ACT.Copy).then_inc(G["d_c_sb"], 1)
                a.activation(cR[:, b % 2, :, :], PS[7][:, S:S + TPB * LAT].rearrange("p (t c) -> p t c", t=TPB),
                             ACT.Copy).then_inc(G["d_c_sb"], 1)

            def d_keys(b, h):
                act.wait_ge(G["d_k"], 2 * b + h + 1)
                a.activation(kg[:, b % 2, 2 * h:2 * h + 2, :], PS[7][:, :].rearrange("p (h q) -> p h q", h=2), ACT.Copy,
                             scale=SC1).then_inc(G["d_k_sb"], 1)

            def f_rowsT(b):
                act.wait_ge(G["f_qT"], b + 1)
                a.activation(fqT[:, b % 2, :, :], PS[0][:, 0:S].bitcast(BF16).rearrange("p (k t) -> p k t", k=KT),
                             ACT.Copy).then_inc(G["f_qT_sb"], 1)

            f_rowsT(0)
            b_oT(2 * B - 1)
            def f_gate(t):
                if t in (0, NT - TPB):
                    act.wait_ge(G["f_fac"], 1 if t == 0 else 2)
                for c in range(2):
                    act.wait_ge(G["f_gu"], 4 * t + 2 * c + 1)
                    if 2 * t + c >= 2:
                        act.wait_ge(G["f_h"], 2 * t + c - 1)
                    a.activation(sg[:, c, :], PS[1 + 2 * c][:, :], ACT.Sigmoid,
                                 scale=fs[:, t, 3:4]).then_inc(G["f_sig"], 1)

            f_gate(0)
            for t in range(NT + 1):
                if t > 0:
                    act.wait_ge(G["f_hqT"], t)
                    a.activation(hqT[:, (t - 1) % 2, :, :], PS[5][:, :].bitcast(BF16).rearrange("p (k t) -> p k t", k=FF // P),
                                 ACT.Copy).then_inc(G["f_hqT_sb"], 1)
                if t < NT:
                    act.wait_ge(G["f_hsc"], t + 1)
                    a.activation(hr, hh[:, t % 2, :], ACT.Identity, scale=fh[:, t % 2, 3:4],
                                 bias=magic[:, :]).then_inc(G["f_hround"], 1)
                if t + 1 < NT:
                    f_gate(t + 1)
                if t == 1:
                    f_round(NT - 2)
                    f_round(NT - 1)
                if 0 < t < NT:
                    d_folded(t - 1)
                if t % TPB == 0 and t // TPB + 1 < B:
                    f_rowsT(t // TPB + 1)
                if t >= 3 and t % TPB:
                    xT_copy(1, t // TPB - 1)
            def d_split_x(b):
                if b >= 2:
                    act.wait_ge(G["d_q"], PAIRS * (b - 1))
                hi(dx[HI][:, b % 2, :, :], xT[:, :, b * S:(b + 1) * S], "hi_part")

            def d_split_w(q):
                hi(w_qh[:, :, 2 * q:2 * q + 2, :], w_qe[:, :, 2 * q:2 * q + 2, :], "hi_part")

            def d_split_out(q):
                hi(w_vh[:, q, :], w_vo[:, q, :], "hi_part")

            d_folded(NT - 1)
            act.wait_ge(G["d_rot"], 6 * (1 + KT))
            act.wait_ge(G["xT_done"], B + 1)
            d_split_x(0)
            d_latent(0)
            act.wait_ge(G["d_w"], NT)
            act.wait_ge(G["d_w_sb"], 2 * NT)
            d_split_w(0)
            d_keys(0, 0)
            xT_copy(1, B - 1)
            act.wait_ge(G["xT_done"], 2 * B)
            d_split_w(1)
            d_keys(0, 1)

            NP = B * PAIRS
            for p in range(NP + 4):
                b, q = divmod(p, PAIRS)
                if q == 6 and b + 1 < B:
                    d_split_x(b + 1)
                if p + 2 < PAIRS:
                    d_split_w(p + 2)
                if PAIRS <= p < PAIRS + 3:
                    for n in range(3 * (p - PAIRS), min(3 * (p - PAIRS) + 3, PAIRS)):
                        d_split_out(n)
                if p < NP:
                    for h in (2 * p, 2 * p + 1):
                        for j, (at, z) in enumerate(((0, 1), (1, 3))):
                            if j == 0:
                                act.wait_ge(G["d_max"], 2 * h + 2)
                            a.activation(dp[:, h % 6, at:z, :],
                                         PS[2 + h % 2][:, at * P:z * P].rearrange("p (c k) -> p c k", k=P), ACT.Exp,
                                         bias=dmx[:, h % 8, j:j + 1],
                                         accum_out=dsm[:, h % 8, j:j + 1]).then_inc(G["d_exp"], 1)
                if 2 <= p < NP + 2:
                    for h in (2 * p - 4, 2 * p - 3):
                        act.wait_ge(G["d_t"], h + 1)
                        a.activation(dpT[:, h % 4, :], PS[4 + h % 2][:, 0:3 * P], ACT.Copy).then_inc(G["d_t_sb"], 1)
                if 3 <= p < NP + 3:
                    act.wait_ge(G["d_o"], p - 2)
                    hi(doT[HI][:, (p - 3) % DO_RING, :], PS[6][:, 0:S], "d_o_sb")
                if q == 4 and b + 1 < B:
                    d_latent(b + 1)
                if q == 5 and b + 1 < B:
                    d_keys(b + 1, 0)
                    d_keys(b + 1, 1)
                if q == 6 and b > 0:
                    xT_copy(2, b - 1)
            def e_gate(b):
                act.wait_ge(G["e_g"], b + 1)
                for k in range(KT):
                    a.activation(gate[:, b, k, :], PS[b][:, k * S:(k + 1) * S], ACT.Sigmoid, bias=bg[:, k:k + 1]).then_inc(G["e_sig"], 1)

            def e_exp(b):
                act.wait_ge(G["e_q"], b + 1)
                a.activation(eq[:, b % 2, :], PS[4 + b % 2][:, :], ACT.Exp).then_inc(G["e_exp"], 1)

            def r_tanh(b):
                act.wait_ge(G["r_log"], b + 1)
                a.activation(rt[:, 2 * b:2 * b + 2, :], PS[7][:, 0:TPB * NE].rearrange("p (t e) -> p t e", t=TPB), ACT.Tanh,
                             scale=1.0 / CAP).then_inc(G["r_act"], 1)

            def r_exp(b):
                act.wait_ge(G["r_v"], b + 1)
                a.activation(rt[:, 2 * b:2 * b + 2, :], rt2[:, 2 * b:2 * b + 2, :], ACT.Exp, scale=CAP).then_inc(G["r_exp"], 1)

            for b in range(B - 1):
                e_gate(b)
            xT_copy(2, B - 1)
            e_gate(B - 1)
            e_exp(0)
            for b in range(B + 3):
                if b + 1 < B:
                    e_exp(b + 1)
                if b >= 3:
                    r_exp(b - 3)
                if 2 <= b <= B + 1:
                    xT_copy(3, b - 2)
                    r_tanh(b - 2)

            def m_rows(i, slot, used=None):
                act.wait_ge(G["m_y"], i + 1)
                if used is not None:
                    act.wait_ge(G[f"m_st{slot}"], used)
                a.activation(yt[:, slot, :], PS[4][:, 0:E], ACT.Copy).then_inc(G["m_y_sb"], 1)

            def m_tokens(i, slot):
                act.wait_ge(G["m_xT"], i + 1)
                a.activation(xgT[:, slot, :, :], PS[5][:, 0:KT * P].rearrange("p (k t) -> p k t", k=KT),
                             ACT.Copy).then_inc(G["m_xT_sb"], 1)

            def m_step(i, h, slot, first=False, last=False, used=True):
                act.wait_ge(G["m_g"], i + 1)
                if not first:
                    act.wait_ge(G["m_h"], i)
                a.activation(sa, PS[0][:, :], ACT.Silu).then_inc(G["m_silu"], 1)
                if not last:
                    m_tokens(i + 1, 1 - slot)
                if not first:
                    m_rows(i - 1, 1 - slot, (h if slot else h - 1) * 16 if used else None)

            m_tokens(0, 0)
            m_step(0, 0, 0, first=True)
            m_step(1, 0, 1, used=False)
            m_step(2, 1, 0, used=False)
            with act.Fori(1, TILES // 2 - 1) as h:
                m_step(h * 2 + 1, h, 1)
                m_step(h * 2 + 2, h + 1, 0)
            m_step(TILES - 2, TILES // 2 - 1, 1)
            m_step(TILES - 1, TILES // 2, 0, last=True)
            m_rows(TILES - 1, 0, TILES // 2 * 16)

            for t in range(NT):
                n = 5 * NT + t
                act.wait_ge(G["ln_rstd"], 5 * NT + 2 * (t + 1))
                a.activation(x_row[:, t, :], res[:, n % 4, :], ACT.Identity, scale=rstd[:, n % 4:n % 4 + 1],
                             bias=nmr[:, n % 4:n % 4 + 1]).then_inc(G["ln_done"], 1)

        @block.vector
        def _(dve):
            v = nc.vector
            steps = [0]

            def step(ins):
                ins.then_inc(G["dve_step"], 1)
                steps[0] += 1
                return steps[0]

            def link(ins):
                ins.then_inc(G["dve_step"], 1)
                steps[0] += 1
                dve.wait_ge(G["dve_step"], steps[0])

            def ln_begin(n, add):
                s = n % 4
                link(add(res[:, s, :]))
                link(v.bn_stats(stats[:, s, :], res[:, s, :]))
                v.bn_aggr(mv[:, s, :], stats[:, s, :]).then_inc(G["ln_var"], 1)

            def ln_end(n):
                s, t = n % 4, n % NT
                dve.wait_ge(G["ln_rstd"], n + 1)
                v.tensor_scalar(x_row[:, t, :], res[:, s, :], mv[:, s, 0:1], rstd[:, s:s + 1], ALU.subtract,
                                ALU.mult).then_inc(G["ln_done"], 1)

            def add_rows(bank, at, t):
                return lambda o: v.tensor_tensor(o, PS[bank][:, at:at + E], x_row[:, t, :], ALU.add)

            dve.wait_ge(G["const_set"], 8)

            def a_keys0(b, g):
                dve.wait_ge(G["a_k0"], b + 1)
                v.tensor_tensor(kmask[:, b % 2, 0, 4 * g:4 * g + 4, :], PS[6][:, 0:S].unsqueeze(1).broadcast_to([P, 4, S]),
                                hmask[:, 4 * g:4 * g + 4].unsqueeze(2).broadcast_to([P, 4, S]), ALU.mult).then_inc(G["a_k0_sb"], 1)

            a_keys0(0, 0)
            a_keys0(0, 1)
            for n in range(FILLS * B + 8):
                b, i = divmod(n, FILLS)
                if n < FILLS * B:
                    dve.wait_ge(G["a_s"], n + 1)
                    v.tensor_reduce(mx[:, n % 8, :], PS[n % 3][:, :].rearrange("p (h k) -> p h k", h=4), AX, ALU.max,
                                    negate=True).then_inc(G["a_max"], 1)
                if 1 <= n <= FILLS * B:
                    dve.wait_ge(G["a_exp"], 4 * n)
                    v.reciprocal(rinv[:, (n - 1) % 8, :], rsum[:, (n - 1) % 8, :]).then_inc(G["a_rinv"], 1)
                if 3 <= n < FILLS * B + 3 and n % 2:
                    dve.wait_ge(G["a_pt"], n - 2)
                    v.tensor_copy(PT[:, (n - 3) % 4, :, :], PS[3][:, :].rearrange("p (h q) -> p h q", h=4)).then_inc(G["a_pt_even"], 1)
                if i == 6 and b > 0:
                    if b == 1:
                        dve.wait_ge(G["ld_xrow"], 16)
                    dve.wait_ge(G["a_y"], b)
                    for t in range(TPB):
                        ln_begin(2 * (b - 1) + t, add_rows(5, t * E, 2 * (b - 1) + t))
                if i in (6, 7) and b + 1 < B:
                    a_keys0(b + 1, i - 6)
                if i == 7 and b > 0:
                    for t in range(TPB):
                        ln_end(2 * (b - 1) + t)

            def lo(out, src, high, s):
                v.tensor_tensor(r32(out), src, r32(high).bitcast(F32), ALU.subtract).then_inc(G[s], 1)

            def c_split(b):
                for c, (at, z) in enumerate(TCOLS):
                    dve.wait_ge(G["c_Thi"], 4 * b + c + 1)
                    lo(ctxT[LO][:, :, at:z], ctxT[LO][:, :, at:z], ctxT[HI][:, :, at:z], "c_Tlo")

            def c_split_rows(b, c):
                at, z = RBLOCKS[c]
                full = min(z, CB - 1)
                dve.wait_ge(G["c_Rhi"], NR * b + c + 1)
                lo(ctxR[LO][:, at:full, 0:E], ctxR[LO][:, at:full, 0:E], ctxR[HI][:, at:full, 0:E], "c_Rlo")
                if z == CB:
                    dve.wait_ge(G["c_Rhi"], NR * (b + 1))
                    lo(ctxR[LO][0:CLAST, CB - 1, 0:E], ctxR[LO][0:CLAST, CB - 1, 0:E], ctxR[HI][0:CLAST, CB - 1, 0:E], "c_Rlo")

            def b_max(u):
                for c, (at, z) in enumerate(SCOLS):
                    dve.wait_ge(G["b_s"], 4 * u + c + 1)
                    ins = v.tensor_reduce(bmx[:, c:c + 1], PS[c][:, 0:z - at], AX, ALU.max)
                    if c < 3:
                        ins.then_inc(G["dve_step"], 1)
                        steps[0] += 1
                    else:
                        link(ins)
                v.tensor_reduce(bmx[:, 4:5], bmx[:, 0:4], AX, ALU.max, negate=True).then_inc(G["b_max"], 1)

            def b_probT(u, c):
                nb = 4 if c < 3 else 3
                dve.wait_ge(G["b_pt_hi"], 4 * u + c + 1)
                lo(probT[LO][:, 4 * c:4 * c + nb, :], PS[4 + c % 2][:, 0:nb * P].rearrange("p (j q) -> p j q", j=nb),
                   probT[HI][:, 4 * c:4 * c + nb, :], "b_pt")

            def b_rinv(u):
                dve.wait_ge(G["b_exp"], 4 * u + 4)
                link(v.tensor_reduce(bsum[:, 4:5], bsum[:, 0:4], AX, ALU.add))
                link(v.reciprocal(bsum[:, 5:6], bsum[:, 4:5]))

            def b_out(u):
                dve.wait_ge(G["b_o"], u + 1)
                v.tensor_scalar(xo, PS[7][:, 0:E], bsum[:, 5:6], None, ALU.mult).then_inc(G["b_o_sb"], 1)

            def f_scales(t):
                j = t
                dve.wait_ge(G["ln_done"], NT + t + 1)
                link(v.tensor_reduce(fs[:, j, 0:1], x_row[:, t, :], AX, ALU.max, apply_absolute_value=True))
                link(v.tensor_scalar(fs[:, j, 1:2], fs[:, j, 0:1], Q_EPS, 1.0 / QMAX, ALU.max, ALU.mult))
                v.reciprocal(fs[:, j, 2:3], fs[:, j, 1:2]).then_inc(G["f_sc"], 1)

            def f_quant(t):
                dve.wait_ge(G["f_round"], t + 1)
                v.tensor_scalar(fq[:, t, :], fr, MAGIC, QMAX, ALU.subtract, ALU.min).then_inc(G["f_q"], 1)

            def f_factors(a, z):
                dve.wait_ge(G["f_sc"], z)
                v.tensor_tensor(fs[:, a:z, 3:5], fs[:, a:z, 1:2].broadcast_to([P, z - a, 2]),
                                wsc[:, 0:2].unsqueeze(1).broadcast_to([P, z - a, 2]), ALU.mult).then_inc(G["f_fac"], 1)

            def b_ln(u):
                dve.wait_ge(G["b_y"], u + 1)
                ln_begin(NT + u, add_rows(7 if u % 2 else 6, 0, u))

            dve.wait_ge(G["ld_ffn"], 48)
            dve.wait_ge(G["wk_split"], 1)
            lo(w_x1[:, 0, :, :], w_x1[:, 0, :, :], wk_hi[:, :, :], "wk_split")
            c_split(0)
            def b_split_qk(b):
                dve.wait_ge(G["hi_part"], 3 * b + 1)
                v.scalar_tensor_tensor(out=r32(xq[LO]), in0=PS[0][:, :].rearrange("p (k t) -> p k t", k=KT), scalar=float(E) ** -0.5,
                                       in1=r32(xq[HI]).bitcast(F32), op0=ALU.mult, op1=ALU.subtract).then_inc(G["lo_part"], 1)
                dve.wait_ge(G["hi_part"], 3 * b + 2)
                lo(xk[LO], PS[1][:, :].rearrange("p (k t) -> p k t", k=KT), xk[HI], "lo_part")

            def b_split_v(b):
                dve.wait_ge(G["hi_part"], 3 * b + 3)
                lo(xv[LO], PS[2][:, :].rearrange("p (t e) -> p t e", t=TPB), xv[HI], "lo_part")

            def w_quant(n):
                dve.wait_ge(G["w_round"], n + 1)
                link(v.tensor_scalar(w_f32[:, n, :], w_f32[:, n, :], MAGIC, 1.0, ALU.subtract, ALU.min))
                v.tensor_scalar(w_ff[:, n, :], w_f32[:, n, :], -1.0, None, ALU.max).then_inc(G["w_tern"], 1)

            b_split_qk(0)
            b_split_v(0)
            for b in range(B):
                b_max(2 * b)
                if b > 0:
                    b_ln(2 * b - 1)
                if b < 3:
                    v.tensor_reduce(wabs[:, b:b + 1], w_f32[:, b, :], AX, ALU.add,
                                    apply_absolute_value=True).then_inc(G["w_abs"], 1)
                for c in range(CP):
                    n = CP * b + c
                    words = 2 * E if c < CP - 1 else E
                    dve.wait_ge(G["x_exp"], n + 1)
                    k1 = kf_lo[:, n % 3, 0:words]
                    link(v.tensor_scalar(k1, k1, 1.0, None, ALU.min))
                    v.scalar_tensor_tensor(out=k1, in0=PS[KBANKS[c % 4]][:, 0:words], scalar=0.0,
                                           in1=k1, op0=ALU.max, op1=ALU.add).then_inc(G["x_kf"], 1)
                    if c in RSTEPS:
                        c_split_rows(b, RSTEPS.index(c))
                    if c == 2 and b > 0:
                        ln_end(NT + 2 * b - 2)
                        ln_end(NT + 2 * b - 1)
                    if c in (3, 4) and b > 0:
                        f_scales(2 * b - 5 + c)
                    if c in (5, 6) and b > 0:
                        f_quant(2 * b - 7 + c)
                b_rinv(2 * b)
                for c in range(4):
                    b_probT(2 * b, c)
                dve.wait_ge(G["x_m1"], CP * (b + 1))
                for k in range(KT):
                    v.tensor_copy(m1[:, k, 0:E + 1], PS[6 + k][:, 0:E + 1]).then_inc(G["x_m1_sb"], 1)
                b_max(2 * b + 1)
                b_out(2 * b)
                dve.wait_ge(G["x_kv"], b + 1)
                for k in range(KT):
                    v.tensor_scalar(kvd[:, b, k, P:P + HT], hmask, m1[:, k, E:E + 1], None, ALU.mult).then_inc(G["dve_step"], 1)
                    steps[0] += 1
                v.tensor_tensor(kvd[:, b, :, 0:P], PS[6][:, 0:KT * P].rearrange("p (k e) -> p k e", k=KT),
                                blk.unsqueeze(1).broadcast_to([P, KT, P]), ALU.mult).then_inc(G["x_kvbd"], 1)
                if b + 1 < B:
                    b_split_qk(b + 1)
                for c in range(4):
                    b_probT(2 * b + 1, c)
                b_rinv(2 * b + 1)
                if b + 1 < B:
                    c_split(b + 1)
                if b > 0:
                    w_quant(b - 1)
                b_out(2 * b + 1)
                b_ln(2 * b)
                if b + 1 < B:
                    b_split_v(b + 1)
                if b < 3:
                    dve.wait_ge(G["w_sum"], b + 1)
                    link(v.tensor_scalar(wsc[:, b:b + 1], PS[6][:, 0:1], 1.0 / (FF * E), Q_EPS, ALU.mult, ALU.add))
                    v.reciprocal(wsi[:, b:b + 1], wsc[:, b:b + 1]).then_inc(G["w_scale"], 1)
            f_factors(0, NT - TPB)
            b_ln(2 * B - 1)

            def f_hidden(t):
                j, i = t % 2, t
                for c in range(2):
                    dve.wait_ge(G["f_sig"], 2 * t + c + 1)
                    dve.wait_ge(G["f_gu"], 4 * t + 2 * c + 2)
                    v.tensor_tensor(hh[:, j, c * 512:(c + 1) * 512], sg[:, c, :], PS[2 + 2 * c][:, :], ALU.mult).then_inc(G["f_h"], 1)
                dve.wait_ge(G["f_h"], 2 * t + 2)
                link(v.tensor_reduce(fh[:, j, 0:1], hh[:, j, :], AX, ALU.max, apply_absolute_value=True))
                link(v.tensor_scalar(fh[:, j, 1:2], fh[:, j, 0:1], fs[:, i, 4:5], Q_EPS, ALU.mult, ALU.max))
                link(v.tensor_scalar(fh[:, j, 1:2], fh[:, j, 1:2], 1.0 / QMAX, None, ALU.mult))
                link(v.reciprocal(fh[:, j, 2:3], fh[:, j, 1:2]))
                v.tensor_tensor(fh[:, j, 3:4], fh[:, j, 2:3], fs[:, i, 4:5], ALU.mult).then_inc(G["f_hsc"], 1)
                v.tensor_tensor(fh[:, j, 4:5], fh[:, j, 1:2], wsc[:, 2:3], ALU.mult).then_inc(G["dve_step"], 1)
                steps[0] += 1

            def f_hidden_quant(t):
                j = t % 2
                dve.wait_ge(G["f_hround"], t + 1)
                v.tensor_scalar(hq[:, j, :], hr, MAGIC, QMAX, ALU.subtract, ALU.min).then_inc(G["f_hq"], 1)

            def f_out(t):
                n = 2 * NT + t
                dve.wait_ge(G["f_y"], t + 1)
                ln_begin(n, lambda o: v.scalar_tensor_tensor(out=o, in0=PS[6][:, 0:E], scalar=fh[:, t % 2, 4:5],
                                                             in1=x_row[:, t, :], op0=ALU.mult, op1=ALU.add))

            def d_split_x(b):
                dve.wait_ge(G["hi_part"], 3 * B + split_of(b))
                lo(dx[LO][:, b % 2, :, :], xT[:, :, b * S:(b + 1) * S], dx[HI][:, b % 2, :, :], "lo_part")

            def d_split_w(q):
                dve.wait_ge(G["hi_part"], 3 * B + q + 2)
                pair = w_qe[:, :, 2 * q:2 * q + 2, :]
                lo(pair, pair, w_qh[:, :, 2 * q:2 * q + 2, :], "lo_part")

            def d_split_out(q):
                dve.wait_ge(G["hi_part"], 3 * B + PAIRS + 3 + q)
                lo(w_vo[:, q, :], w_vo[:, q, :], w_vh[:, q, :], "lo_part")

            for t in range(NT + 1):
                if t < NT:
                    f_hidden(t)
                if t == 0:
                    for n in (NT - 2, NT - 1):
                        ln_end(NT + n)
                    for n in (NT - 2, NT - 1):
                        f_scales(n)
                    f_factors(NT - TPB, NT)
                if t > 0:
                    f_out(t - 1)
                if t < NT:
                    f_hidden_quant(t)
                else:
                    d_split_x(0)
                if t == 1:
                    f_quant(NT - 2)
                    f_quant(NT - 1)
                if t > 0:
                    ln_end(2 * NT + t - 1)

            def d_query(p):
                dve.wait_ge(G["d_q"], p + 1)
                v.tensor_copy(qe[:, p % 3, :, :], PS[1 - p % 2][:, :].rearrange("p (h q) -> p h q", h=2)).then_inc(G["d_q_sb"], 1)

            def d_rinv(p):
                for h in (2 * p, 2 * p + 1):
                    dve.wait_ge(G["d_exp"], 2 * h + 2)
                    v.reciprocal(dri[:, h % 8, :], dsm[:, h % 8, :]).then_inc(G["d_rinv"], 1)

            def d_ln(t):
                dve.wait_ge(G["d_y"], t + 1)
                ln_begin(3 * NT + t, add_rows(7, t % TPB * E, t))

            def d_outputs(p):
                dve.wait_ge(G["d_o_sb"], p + 1)
                lo(doT[LO][:, p % DO_RING, :], PS[6][:, 0:S], doT[HI][:, p % DO_RING, :], "d_o_lo")

            NP = B * PAIRS
            d_split_w(0)
            d_split_w(1)
            d_query(0)
            for p in range(NP + 1):
                b, q = divmod(p, PAIRS)
                if p >= 4:
                    d_outputs(p - 4)
                if p + 2 < PAIRS:
                    d_split_w(p + 2)
                if PAIRS <= p < PAIRS + 3:
                    for n in range(3 * (p - PAIRS), min(3 * (p - PAIRS) + 3, PAIRS)):
                        d_split_out(n)
                if q == 6 and b + 1 < B:
                    d_split_x(b + 1)
                if q == 4 and b > 0:
                    d_ln(2 * (b - 1) + 1)
                if p + 1 < NP:
                    d_query(p + 1)
                if p < NP:
                    for h in (2 * p, 2 * p + 1):
                        dve.wait_ge(G["d_s"], h + 1)
                        bank = PS[2 + h % 2]
                        v.tensor_reduce(dmx[:, h % 8, 0:1], bank[:, 0:P], AX, ALU.max, negate=True).then_inc(G["d_max"], 1)
                        v.tensor_reduce(dmx[:, h % 8, 1:2], bank[:, P:3 * P], AX, ALU.max, negate=True).then_inc(G["d_max"], 1)
                if p > 0:
                    d_rinv(p - 1)
                if q == 3 and b > 0:
                    d_ln(2 * (b - 1))
                if q == 5 and b > 0:
                    for t in range(TPB):
                        ln_end(3 * NT + 2 * (b - 1) + t)
            for p in range(NP - 3, NP):
                d_outputs(p)
            d_ln(NT - 2)
            d_ln(NT - 1)
            for t in range(TPB):
                ln_end(3 * NT + 2 * (B - 1) + t)

            def pair_rows(o, at, s):
                step(v.tensor_reduce(shi[:, at], slots[:, at, :], AX, ALU.max))
                link(v.tensor_reduce(ssm[:, at], slots[:, at, :], AX, ALU.add))
                link(v.scalar_tensor_tensor(out=ssm[:, at], in0=ssm[:, at], scalar=-1.0, in1=shi[:, at],
                                            op0=ALU.add, op1=ALU.subtract))
                v.tensor_scalar(o[:, 1, at], shi[:, at], -1.0, float(E + 2), ALU.add, ALU.mult).then_inc(G[s], 1)
                v.tensor_scalar(o[:, 0, at], ssm[:, at], float(E + 2), None, ALU.mult).then_inc(G[s], 1)

            def r_top(b):
                at = slice(2 * b, 2 * b + 2)
                dve.wait_ge(G["r_act"], b + 1)
                link(v.tensor_reduce(rtop[:, at], rt[:, at, :], AX, ALU.max))
                v.tensor_tensor(rt2[:, at, :], rt[:, at, :], each(rtop, at), ALU.subtract).then_inc(G["r_v"], 1)

            def each(x, at):
                return x[:, at].unsqueeze(2).broadcast_to([P, TPB, NE])

            def r_choose(b):
                at = slice(2 * b, 2 * b + 2)
                dve.wait_ge(G["r_exp"], b + 1)
                link(v.tensor_reduce(rsm[:, at], rt[:, at, :], AX, ALU.add))
                link(v.reciprocal(rsi[:, at], rsm[:, at]))
                link(v.tensor_tensor(wgt[:, at, :], rt[:, at, :], each(rsi, at), ALU.mult))
                other = wgt[:, at, :].unsqueeze(2).broadcast_to([P, TPB, NE, NE])
                own = wgt[:, at, :].unsqueeze(3).broadcast_to([P, TPB, NE, NE])
                step(v.tensor_tensor(rcm2, other, own, ALU.is_equal))
                link(v.tensor_tensor(rcmp, other, own, ALU.is_gt))
                link(v.tensor_tensor(rcm2, rcm2, tri.unsqueeze(1).broadcast_to([P, TPB, NE, NE]), ALU.mult))
                link(v.tensor_tensor(rcmp, rcmp, rcm2, ALU.add))
                link(v.tensor_reduce(rt[:, at, :], rcmp, AX, ALU.add))
                v.tensor_scalar(kept16[:, at, :], rt[:, at, :], float(TOPK), None, ALU.is_lt).then_inc(G["r_kept"], 1)
                link(v.tensor_scalar(rt2[:, at, :], rt[:, at, :], float(TOPK), None, ALU.is_lt))
                step(v.tensor_tensor(wgt[:, at, :], wgt[:, at, :], rt2[:, at, :], ALU.mult))

            def r_place(b):
                at = slice(2 * b, 2 * b + 2)
                dve.wait_ge(G["r_count"], b + 1)
                first = cst[:, C_EROW:C_EROW + NE].unsqueeze(1).broadcast_to([P, TPB, NE])
                link(v.tensor_tensor(slots[:, at, :], PS[7][:, TPB * NE:2 * TPB * NE].rearrange("p (t e) -> p t e", t=TPB),
                                     first, ALU.add))
                link(v.tensor_tensor(slots[:, at, :], slots[:, at, :], rt2[:, at, :], ALU.mult))
                pair_rows(tok_rows, at, "r_rows")

            def r_weights():
                every = shi.unsqueeze(2).broadcast_to([P, NT, NE])
                link(v.tensor_tensor(chosen, slots, every, ALU.is_equal))
                link(v.tensor_tensor(chosen, chosen, wgt, ALU.mult))
                link(v.tensor_reduce(w_hi, chosen, AX, ALU.add))
                link(v.tensor_reduce(w_lo, wgt, AX, ALU.add))
                link(v.tensor_tensor(w_lo, w_lo, w_hi, ALU.subtract))

            dve.wait_ge(G["ld_cbias"], 16)
            v.tensor_scalar(before16, cbias[:, 0:P], 0.0, None, ALU.is_lt).then_inc(G["r_set"], 1)
            v.tensor_copy(ones16, ones[:, :]).then_inc(G["r_set"], 1)

            def e_ln(b):
                dve.wait_ge(G["e_y"], b + 1)
                for t in range(TPB):
                    ln_begin(4 * NT + 2 * b + t, add_rows(3, t * E, 2 * b + t))

            def e_features(b):
                s = b % 2
                dve.wait_ge(G["e_exp"], b + 1)
                link(v.tensor_scalar(eq[:, s, :], eq[:, s, :], 1.0, None, ALU.min))
                v.scalar_tensor_tensor(out=qf[:, s, :, :].rearrange("p k t -> p (k t)"), in0=PS[4 + s][:, :], scalar=0.0,
                                       in1=eq[:, s, :], op0=ALU.max, op1=ALU.add).then_inc(G["e_qf"], 1)

            def e_divide(b):
                dve.wait_ge(G["e_nd"], 2 * b + 2)
                parts = lambda t: PS[t][:, 0:KT * (P + HT)].rearrange("p (f c) -> p f c", f=KT)
                for t in range(TPB):
                    ins = v.tensor_scalar(eri[:, t, :].rearrange("p (f h) -> p f h", f=KT), parts(t)[:, :, P:P + HT],
                                          Z_EPS, None, ALU.add)
                    if t < TPB - 1:
                        ins.then_inc(G["dve_step"], 1)
                        steps[0] += 1
                link(ins)
                link(v.reciprocal(eri[:, :, :], eri[:, :, :]))
                for t in range(TPB):
                    v.tensor_tensor(eav[:, b % 2, t, :].rearrange("p (f h d) -> p f h d", f=KT, h=HT),
                                    parts(t)[:, :, 0:P].rearrange("p f (h d) -> p f h d", h=HT),
                                    eri[:, t, :].rearrange("p (f h) -> p f h", f=KT).unsqueeze(3).broadcast_to([P, KT, HT, DX]),
                                    ALU.mult).then_inc(G["e_av"], 1)

            def e_gated(b):
                dve.wait_ge(G["e_avT"], b + 1)
                v.tensor_tensor(eat[:, b % 2, :, :], PS[2][:, :].rearrange("p (k t) -> p k t", k=KT), gate[:, b, :, :],
                                ALU.mult).then_inc(G["e_at"], 1)

            e_features(0)
            for b in range(B + 3):
                if b < B:
                    e_divide(b)
                if 1 <= b <= B:
                    e_ln(b - 1)
                if b >= 3:
                    r_top(b - 3)
                if b + 1 < B:
                    e_features(b + 1)
                if b < B:
                    e_gated(b)
                if 1 <= b <= B:
                    for t in range(TPB):
                        ln_end(4 * NT + 2 * (b - 1) + t)
                if b >= 3:
                    r_choose(b - 3)
                    r_place(b - 3)

            count = PS[7][:, 2 * TPB * NE:(2 * TPB + 1) * NE]
            thr, tile_no = cst[:, C_THR:C_THR + NE], cst[:, C_TILE:C_TILE + TILES]
            ecmp, ecm2 = rcmp[:, 0, :, :], rcm2[:, 0, :, :]
            link(v.tensor_tensor(ecmp, count.unsqueeze(2).broadcast_to([P, NE, NE]),
                                 thr.unsqueeze(1).broadcast_to([P, NE, NE]), ALU.is_gt))
            link(v.tensor_reduce(etiles, ecmp, AX, ALU.add))
            step(v.tensor_scalar(eskip, etiles, -float(P), float(TOKENS), ALU.mult, ALU.add))
            link(v.tensor_tensor(ecm2, tri, etiles.unsqueeze(1).broadcast_to([P, NE, NE]), ALU.mult))
            link(v.tensor_reduce(eends, ecm2, AX, ALU.add))
            link(v.tensor_tensor(eends, eends, etiles, ALU.add))
            link(v.tensor_tensor(tcmp, tile_no.unsqueeze(2).broadcast_to([P, TILES, NE]),
                                 eends.unsqueeze(1).broadcast_to([P, TILES, NE]), ALU.is_ge))
            link(v.tensor_reduce(tab[:, 0, :], tcmp, AX, ALU.add))
            link(v.tensor_tensor(tcmp, tcmp, eskip.unsqueeze(1).broadcast_to([P, TILES, NE]), ALU.mult))
            link(v.tensor_reduce(tab[:, 1, :], tcmp, AX, ALU.add))
            link(v.scalar_tensor_tensor(out=tab[:, 1, :], in0=tile_no, scalar=float(P), in1=tab[:, 1, :], op0=ALU.mult, op1=ALU.add))
            v.tensor_scalar(table[:, 0, :], tab[:, 0, :], float(NE - 1), None, ALU.min).then_inc(G["r_table"], 1)
            v.tensor_copy(table[:, 1, :], tab[:, 1, :]).then_inc(G["r_table"], 1)

            r_weights()
            def m_hidden(i):
                dve.wait_ge(G["m_silu"], i + 1)
                dve.wait_ge(G["m_u"], i + 1)
                v.tensor_tensor(hs, sa, PS[1][:, :], ALU.mult).then_inc(G["m_h"], 1)

            def m_hiddenT(i):
                dve.wait_ge(G["m_hT"], i + 1)
                v.tensor_copy(hT, PS[2][:, :].rearrange("p (m t) -> p m t", m=FM)).then_inc(G["m_hT_sb"], 1)

            m_hidden(0)
            with dve.Fori(0, TILES - 1) as i:
                m_hiddenT(i)
                m_hidden(i + 1)
            m_hiddenT(TILES - 1)

            def add_first(t):
                return v.scalar_tensor_tensor(out=res[:, t % 4, :], in0=y_lo[:, t, :], scalar=w_lo[:, t:t + 1], in1=x_row[:, t, :],
                                              op0=ALU.mult, op1=ALU.add)

            def add_second(t):
                return v.scalar_tensor_tensor(out=res[:, t % 4, :], in0=y_hi[:, t, :], scalar=w_hi[:, t:t + 1], in1=res[:, t % 4, :],
                                              op0=ALU.mult, op1=ALU.add)

            def row_stats(t):
                return v.bn_stats(stats[:, t % 4, :], res[:, t % 4, :])

            for t in range(0, NT, 2):
                dve.wait_ge(G[y_got[t // 2]], 16 * TOPK)
                if t >= 4:
                    dve.wait_ge(G["ln_done"], 5 * NT + t - 2)
                done = [0, 0]
                for part in (add_first, add_second, row_stats):
                    for j in range(2):
                        if done[j]:
                            dve.wait_ge(G["dve_step"], done[j])
                        done[j] = step(part(t + j))
                for j in range(2):
                    dve.wait_ge(G["dve_step"], done[j])
                    v.bn_aggr(mv[:, (t + j) % 4, :], stats[:, (t + j) % 4, :]).then_inc(G["ln_var"], 1)

        @block.tensor
        def _(pe):
            def mm(o, w, x, start=True, stop=True, **k):
                return nc.tensor.matmul(o, w, x, start=start, stop=stop, **k)

            def project(o, w, x):
                for k in range(KT):
                    ins = mm(o, w(k), x(k), start=k == 0, stop=k == KT - 1)
                return ins

            def to_xT(stage, b):
                pe.wait_ge(G["ln_done"], (0, 2, 3, 4)[stage] * NT + 2 * b + 2)
                for k in range(KT):
                    for t in range(TPB):
                        ins = mm(PS_xT[stage][:, k * S + t * P:k * S + (t + 1) * P], x_row[:, 2 * b + t, k * P:(k + 1) * P],
                                 ident, is_transpose=True)
                ins.then_inc(G["xT_raw"], 1)

            pe.wait_ge(G["const_set"], 8)

            def a_query_key(b):
                seq = lambda k: xT[:, k, b * S:(b + 1) * S]
                if b == 1:
                    pe.wait_ge(G["a_k1_sb"], 8)
                    pe.wait_ge(G["a_v_sb"], 1)
                elif b > 1:
                    pe.wait_ge(G["ln_var"], 2 * (b - 1))
                for f in range(KT):
                    ins = project(PS[5][:, f * S:(f + 1) * S], lambda k: w_qkv[:, k, f * P:(f + 1) * P], seq)
                ins.then_inc(G["a_q"], 1)
                if b > 0:
                    pe.wait_ge(G["a_v_sb"], 3 * b)
                project(PS[6][:, 0:S], lambda k: w_qkv[:, k, E:E + P], seq).then_inc(G["a_k0"], 1)

            def a_value(o, b, w):
                return project(o, lambda k: xT[:, k, b * S + w:b * S + w + P], lambda k: w_qkv[:, k, 2 * E:3 * E])

            def a_key_value(b):
                pe.wait_ge(G["a_q_sb"], b + 1)
                project(PS[5][:, 0:S], lambda k: w_qkv[:, k, E + P:2 * E], lambda k: xT[:, k, b * S:(b + 1) * S])
                a_value(PS[5][:, S:S + E], b, 0).then_inc(G["a_k1v0"], 1)

            def a_scores(n):
                b, i = divmod(n, FILLS)
                f, g, t = i // 4, (i // 2) % 2, i % 2
                if i == 0:
                    pe.wait_ge(G["a_q_sb"], b + 1)
                if t == 0:
                    pe.wait_ge(*((G["a_k0_sb"], 2 * b + g + 1) if f == 0 else (G["a_k1_sb"], 8 * b + 4 * g + 4)))
                if n >= 3:
                    pe.wait_ge(G["a_exp"], 4 * (n - 2))
                mask = wmask16[:, t, :].unsqueeze(1).broadcast_to([P, 4, P])
                q = qT[:, b % 2, f, :]
                k = kmask[:, b % 2, f, 4 * g:4 * g + 4, :]
                o = PS[n % 3]
                if t == 0:
                    mm(o[:, :], ident16[:, :], mask, stop=False)
                    ins = mm(o[:, :], q[:, 0:P], k[:, :, 0:P], start=False)
                else:
                    for c in range(2):
                        mm(o[c * WIN:(c + 1) * WIN, :], ident16[:, c * WIN:(c + 1) * WIN], mask, stop=False)
                    for c in range(2):
                        ins = mm(o[c * WIN:(c + 1) * WIN, :], q[:, P + c * WIN:P + (c + 1) * WIN],
                                 k[:, :, (c + 1) * WIN:(c + 1) * WIN + P], start=False)
                ins.then_inc(G["a_s"], 1)

            def a_transpose(n):
                pe.wait_ge(G["a_norm"], n + 1)
                if n >= 2:
                    pe.wait_ge(G["a_pt_odd" if n % 2 else "a_pt_even"], n // 2)
                for h in range(4):
                    ins = mm(PS[3 + n % 2][:, h * P:(h + 1) * P], sm[:, n % 4, h, :], ident, is_transpose=True)
                ins.then_inc(G["a_pt"], 1)

            def a_output(n):
                b, i = divmod(n, FILLS)
                f, g, t = i // 4, (i // 2) % 2, i % 2
                pe.wait_ge(G["a_pt_odd" if n % 2 else "a_pt_even"], n // 2 + 1)
                pe.wait_ge(G["a_v_sb"], 3 * b + (3 if t else 1))
                if i % 4 == 0 and n > 0:
                    pe.wait_ge(G["a_o_sb"], 2 * b + f)
                for h in range(4):
                    for w, lo, hi in ((0, 0, P),) if t == 0 else ((1, P, P + WIN), (2, P + WIN, S)):
                        head = (8 * f + 4 * g + h) * D0P
                        ins = mm(PS[7][h * D0P:(h + 1) * D0P, g * S + lo:g * S + hi], vpad[:, b % 2, w, head:head + D0P],
                                 PT[:, n % 4, h, lo - t * P:hi - t * P], tile_position=(0, h * D0P))
                if i % 4 == 3:
                    ins.then_inc(G["a_o"], 1)

            def a_project_out(b):
                pe.wait_ge(G["a_o_sb"], 2 * b + 2)
                if b == 0:
                    pe.wait_ge(G["a_k1_sb"], 16)
                    pe.wait_ge(G["a_v_sb"], 4)
                else:
                    pe.wait_ge(G["xT_done"], b)
                last = H0 * D0P // P - 1
                for t in range(TPB):
                    for k in range(last + 1):
                        ins = mm(PS[5][:, t * E:(t + 1) * E], oT[:, k, t * P:(t + 1) * P], w_o0[:, k, :], start=k == 0, stop=k == last)
                ins.then_inc(G["a_y"], 1)

            pe.wait_ge(G["ld_x"], 16)
            pe.wait_ge(G["ld_attn0"], 16)
            a_query_key(0)
            a_key_value(0)
            for n in range(FILLS * B + 8):
                b, i = divmod(n, FILLS)
                if n < FILLS * B:
                    a_scores(n)
                if 3 <= n < FILLS * B + 3:
                    a_transpose(n - 3)
                if 5 <= n < FILLS * B + 5:
                    a_output(n - 5)
                if i == 2 and b < B:
                    pe.wait_ge(G["a_k0_sb"], 2 * b + 2)
                    a_value(PS[6][:, 0:E], b, WIN)
                    a_value(PS[6][:, E:2 * E], b, P).then_inc(G["a_v12"], 1)
                if i == 2 and b >= 2:
                    if b < B:
                        pe.wait_ge(G["a_k1_sb"], 8 * b + 8)
                        pe.wait_ge(G["a_v_sb"], 3 * b + 1)
                    to_xT(0, b - 2)
                if i == 5 and b > 0:
                    if b == 1:
                        pe.wait_ge(G["ld_wo0"], 16)
                    a_project_out(b - 1)
                if i == 6 and b + 1 < B:
                    if b == 0:
                        pe.wait_ge(G["ld_rest"], 16)
                    a_query_key(b + 1)
                if i == 7 and b + 1 < B:
                    a_key_value(b + 1)
            to_xT(0, B - 1)

            pe.wait_ge(G["ld_x0"], 64)
            pe.wait_ge(G["ld_x1"], 96)

            def split(o, w, x, start=True, stop=True):
                mm(o, r32(w[HI]), r32(x[HI]), start=start, stop=False)
                mm(o, r32(w[HI]), r32(x[LO]), start=False, stop=False)
                return mm(o, r32(w[LO]), r32(x[HI]), start=False, stop=stop)

            def b_project_qk(b):
                seq = lambda k: xT[:, k, b * S:(b + 1) * S]
                pe.wait_ge(G["xT_done"], b + 1)
                if b == 0:
                    pe.wait_ge(G["a_exp"], 4 * FILLS * B)
                for n, s in enumerate(("b_q", "b_k")):
                    if b > 0:
                        pe.wait_ge(G["b_exp"], 4 * (2 * b - 1) + n + 1)
                    for f in range(KT):
                        ins = project(PS[n][:, f * S:(f + 1) * S], lambda k: w_x0[:, n, k, f * P:(f + 1) * P], seq)
                    ins.then_inc(G[s], 1)

            def b_project_v(b):
                if b > 0:
                    pe.wait_ge(G["b_exp"], 4 * (2 * b - 1) + 3)
                for t in range(TPB):
                    ins = project(PS[2][:, t * E:(t + 1) * E], lambda k: xT[:, k, b * S + t * P:b * S + (t + 1) * P],
                                  lambda k: w_x0[:, 2, k, :])
                ins.then_inc(G["b_v"], 1)

            def b_score(u, c):
                b, t = divmod(u, TPB)
                lo, hi = CCOLS[c]
                if u == 0 and c == 3:
                    pe.wait_ge(G["a_pt_even"], FILLS * B // 2)
                if t == 0 and c < 3:
                    pe.wait_ge(G["lo_part"], 3 * b + c + 1)
                else:
                    if u > 0:
                        pe.wait_ge(G["b_exp"], 4 * (u - 1) + c + 1)
                    if t > 0 and c < 2:
                        pe.wait_ge(G["x_kf"], CP * (b + 1))
                pe.wait_ge(G["c_Tlo"], 4 * b + c + 1)
                part = lambda x, k, a, z: [x[n][:, k, a:z] for n in (LO, HI)]
                q = lambda k: part(xq, k, t * P, (t + 1) * P)
                for k in range(KT):
                    ins = split(PS[c][:, 0:hi - lo], q(k), part(ctxT, k, lo, hi), start=k == 0, stop=k == KT - 1)
                if c == 3:
                    for k in range(KT):
                        ins = split(PS[c][:, hi - lo:hi - lo + S], q(k), part(xk, k, 0, S), start=k == 0, stop=k == KT - 1)
                ins.then_inc(G["b_s"], 1)

            def b_transpose(u, c):
                if c == 0:
                    pe.wait_ge(G["b_exp"], 4 * u + 4)
                if c >= 2 or u % 2:
                    pe.wait_ge(G["b_pt"], 4 * u + c - 1)
                else:
                    pe.wait_ge(G["x_kf"], CP * (u // 2 + 1))
                for j in range(4 if c < 3 else 3):
                    n = 4 * c + j
                    lo, hi = key_block(n)
                    ins = mm(PS[4 + c % 2][0:hi - lo, j * P:(j + 1) * P], prob[:, lo:hi], ident, is_transpose=True)
                ins.then_inc(G["b_t"], 1)

            def key_block(n):
                if n < CB:
                    return n * P, min((n + 1) * P, CTX)
                return CTX + (n - CB) * P, CTX + (n - CB + 1) * P

            def b_values(u):
                b = u // TPB
                pe.wait_ge(G["b_pt"], 4 * u + 4)
                if u % 2:
                    pe.wait_ge(G["b_o_sb"], u)
                else:
                    pe.wait_ge(G["x_m1_sb"], 2 * b + 2)
                for n in range(CB + TPB):
                    at, z = key_block(n)
                    rows = z - at
                    x = [ctxR[i][0:rows, n, 0:E] if n < CB else xv[i][:, n - CB, :] for i in (LO, HI)]
                    ins = split(PS[7][:, 0:E], [probT[i][0:rows, n, :] for i in (LO, HI)], x, start=n == 0, stop=n == CB + TPB - 1)
                ins.then_inc(G["b_o"], 1)

            def b_outT(u):
                pe.wait_ge(G["b_o_sb"], u + 1)
                if u % 2 == 0:
                    pe.wait_ge(G["x_kvbd"], u // 2 + 1)
                for k in range(KT):
                    ins = mm(PS[7 if u % 2 else 6][:, k * P:(k + 1) * P], xo[:, k * P:(k + 1) * P], ident, is_transpose=True)
                ins.then_inc(G["b_ot"], 1)

            def b_project_out(u):
                pe.wait_ge(G["b_ot_sb"], u + 1)
                ins = project(PS[7 if u % 2 else 6][:, 0:E], lambda k: xoT[:, k, :], lambda k: w_x0[:, 3, k, :])
                ins.then_inc(G["b_y"], 1)

            def x_keys(b):
                wk = lambda k: [w_x1[:, 0, k, :], wk_hi[:, k, :]]

                def key_fill(c):
                    if c < 2:
                        if b > 0:
                            pe.wait_ge(G["b_pt"], 8 * b)
                        else:
                            pe.wait_ge(*((G["xT_done"], B) if c else (G["a_pt_odd"], FILLS * B // 2)))
                    elif c < 4:
                        pe.wait_ge(G["b_exp"], 8 * b + c - 1)
                    else:
                        pe.wait_ge(G["x_kf"], CP * b + c - 3)
                    for t in range(2 * c, min(2 * c + 2, CB)):
                        rows = P if t < CB - 1 else CLAST
                        for k in range(KT):
                            ins = split(PS[KBANKS[c % 4]][0:rows, t % 2 * E:(t % 2 + 1) * E],
                                        [ctxT[i][:, k, t * P:t * P + rows] for i in (LO, HI)], wk(k), start=k == 0, stop=k == KT - 1)
                    ins.then_inc(G["x_k"], 1)

                for c in range(4):
                    key_fill(c)
                if b == 0:
                    pe.wait_ge(G["a_v_sb"], 3 * B)
                else:
                    pe.wait_ge(G["w_scale"], b)
                pe.wait_ge(G["ln_var"], NT + 2 * b)
                for c in range(CP):
                    n = CP * b + c
                    for i, (at, z) in enumerate(RBLOCKS):
                        if 2 * c == at:
                            pe.wait_ge(G["c_Rlo"], NR * b + i + 1)
                    if c == CP - 1:
                        pe.wait_ge(G["c_Rlo"], NR * (b + 1))
                    pe.wait_ge(G["x_kf_lo"], n + 1)
                    for t in range(2 * c, min(2 * c + 2, CB)):
                        rows = P if t < CB - 1 else CLAST
                        for h in range(KT):
                            at = t % 2 * E + h * P
                            ins = split(PS[6 + h][:, 0:E + 2], [kf_lo[0:rows, n % 3, at:at + P], kf_hi[0:rows, n % 2, at:at + P]],
                                        [ctxR[i][0:rows, t, :] for i in (LO, HI)], start=t == 0, stop=t == CB - 1)
                    ins.then_inc(G["x_m1"], 1)
                    if c + 4 < CP:
                        key_fill(c + 4)

            def x_transpose(b):
                pe.wait_ge(G["x_m1_sb"], 2 * b + 2)
                for k in range(KT):
                    for h in range(KT):
                        ins = mm(PS[6][:, k * S + h * P:k * S + (h + 1) * P], m1[:, h, k * P:(k + 1) * P], ident, is_transpose=True)
                ins.then_inc(G["x_m1T"], 1)

            def x_values(b):
                pe.wait_ge(G["x_m1T_sb"], b + 1)
                for h in range(KT):
                    ins = project(PS[6][:, h * P:(h + 1) * P], lambda k: m1T[:, k, h * P:(h + 1) * P],
                                  lambda k: w_x1[:, 1, k, h * P:(h + 1) * P])
                ins.then_inc(G["x_kv"], 1)

            def f_transpose(b):
                pe.wait_ge(G["f_q"], 2 * b + 2)
                if b == 0:
                    pe.wait_ge(G["b_exp"], 8 * NT // 2)
                else:
                    pe.wait_ge(*((G["f_qT_sb"], b) if b < 3 else (G["xT_done"], B + b - 2)))
                o = PS[0][:, 0:S].bitcast(BF16)
                for k in range(KT):
                    for t in range(TPB):
                        ins = mm(o[:, k * S + t * P:k * S + (t + 1) * P], fq[:, TPB * b + t, k * P:(k + 1) * P], ident16[:, :], is_transpose=True)
                ins.then_inc(G["f_qT"], 1)

            def f_gate_up(t):
                b, j = divmod(t, TPB)
                pe.wait_ge(G["f_qT_sb"], b + 1)
                for c in range(2):
                    for n in range(2):
                        if t > 0:
                            pe.wait_ge(*((G["f_sig"], 2 * t + c - 1) if n == 0 else (G["f_h"], 2 * t + c - 1)))
                        if t == 0 and (n, c) == (1, 1):
                            pe.wait_ge(G["b_pt"], 4 * NT)
                        ins = project(PS[1 + 2 * c + n][:, :], lambda k: fqT[:, b % 2, k, j * P:(j + 1) * P],
                                      lambda k: w_ff[:, n, k * FF + c * 512:k * FF + (c + 1) * 512])
                        ins.then_inc(G["f_gu"], 1)

            b_project_qk(0)
            b_project_v(0)
            pe.wait_ge(G["const_set"], 9)
            pe.wait_ge(G["wk_split"], 2)
            for b in range(B):
                for c in range(4):
                    b_score(2 * b, c)
                if b > 0:
                    b_project_out(2 * b - 1)
                x_keys(b)
                for c in range(4):
                    b_transpose(2 * b, c)
                    b_score(2 * b + 1, c)
                x_transpose(b)
                b_values(2 * b)
                x_values(b)
                if b + 1 < B:
                    b_project_qk(b + 1)
                for c in range(4):
                    b_transpose(2 * b + 1, c)
                b_outT(2 * b)
                b_values(2 * b + 1)
                if b + 1 < B:
                    b_project_v(b + 1)
                b_project_out(2 * b)
                if b + 1 < B:
                    b_outT(2 * b + 1)
                if b < 3:
                    pe.wait_ge(G["w_abs"], b + 1)
                    pe.wait_ge(G["ln_var"], NT + 2 * b + 1)
                    mm(PS[6][:, 0:1], ones[:, :], wabs[:, b:b + 1]).then_inc(G["w_sum"], 1)
            f_transpose(0)
            b_outT(2 * B - 1)
            f_gate_up(0)
            b_project_out(2 * B - 1)

            def f_hiddenT(t):
                pe.wait_ge(G["f_hq"], t + 1)
                if t == 0:
                    pe.wait_ge(G["b_pt"], 4 * NT)
                else:
                    pe.wait_ge(G["f_hqT_sb"], t)
                o = PS[5][:, :].bitcast(BF16)
                for k in range(FF // P):
                    ins = mm(o[:, k * P:(k + 1) * P], hq[:, t % 2, k * P:(k + 1) * P], ident16[:, :], is_transpose=True)
                ins.then_inc(G["f_hqT"], 1)

            def f_down(t):
                pe.wait_ge(G["f_hqT_sb"], t + 1)
                pe.wait_ge(G["ln_var"], 2 * NT - 1 if t == 0 else 2 * NT + t)
                for k in range(FF // P):
                    ins = mm(PS[6][:, 0:E], hqT[:, t % 2, k, :], w_ff[:, 2, k * E:(k + 1) * E], start=k == 0, stop=k == FF // P - 1)
                ins.then_inc(G["f_y"], 1)

            def d_fold(t):
                if t == 0:
                    pe.wait_ge(G["ld_lat"], 96)
                    pe.wait_ge(G["ld_wq"], 32)
                    pe.wait_ge(G["ld_wo"], 16)
                    pe.wait_ge(G["ln_var"], 2 * NT)
                else:
                    pe.wait_ge(G["d_w_sb"], 2 * t)
                g = 2 * t // (H1 // KV1)
                for k in range(KT):
                    for i in range(2):
                        at = (2 * k + i) * LAT
                        mm(PS[7][:, at:at + LAT], w_qT[:, 2 * t + i, k * P:(k + 1) * P], w_kd[:, g, :])
                for i in range(2):
                    ins = mm(PS[7][i * LAT:(i + 1) * LAT, 256:256 + E], w_vd[:, g, :], w_oh[:, 2 * t + i, :])
                ins.then_inc(G["d_w"], 1)

            def d_latent(b):
                seq = lambda k: xT[:, k, b * S:(b + 1) * S]
                pe.wait_ge(G["xT_done"], B + b + 1)
                if b == 0:
                    pe.wait_ge(G["d_w_sb"], 2 * PAIRS)
                elif b == 1:
                    pe.wait_ge(G["d_k_sb"], 2)
                else:
                    pe.wait_ge(G["ln_var"], 3 * NT + 2 * (b - 1))
                project(PS[7][0:LAT, 0:S], lambda k: w_kvc[:, k, :], seq)
                for t in range(TPB):
                    ins = project(PS[7][:, S + t * LAT:S + (t + 1) * LAT], lambda k: xT[:, k, b * S + t * P:b * S + (t + 1) * P],
                                  lambda k: w_kvc[:, k, :])
                ins.then_inc(G["d_c"], 1)

            def d_keys(b, h):
                pe.wait_ge(G["d_c_sb"], 2 * b + 2)
                if h == 1:
                    pe.wait_ge(G["d_k_sb"], 2 * b + 1)
                for i in range(2):
                    ins = mm(PS[7][:, i * S:(i + 1) * S], w_ki[:, 2 * h + i, :], cT[0:LAT, :])
                ins.then_inc(G["d_k"], 1)

            for t in range(NT + 1):
                if t > 0:
                    f_hiddenT(t - 1)
                    f_down(t - 1)
                if t + 1 < NT:
                    f_gate_up(t + 1)
                if 0 < t < NT:
                    d_fold(t - 1)
                if t % TPB == 0 and t // TPB + 1 < B:
                    f_transpose(t // TPB + 1)
                if t >= 3 and t % TPB:
                    pe.wait_ge(G["f_qT_sb"], min(t // TPB + 2, B))
                    to_xT(1, t // TPB - 1)
            def d_query(p):
                b, q = divmod(p, PAIRS)
                pe.wait_ge(G["xT_done"], B + b + 1)
                if p == 0:
                    pe.wait_ge(G["f_sig"], 2 * NT)
                elif p == 1:
                    pe.wait_ge(G["xT_done"], 2 * B)
                else:
                    pe.wait_ge(G["d_q_sb"], p - 1)
                pe.wait_ge(G["lo_part"], 3 * B + (split_of(b) if b else q + 2))
                for i in range(2):
                    for k in range(KT):
                        ins = split(PS[1 - p % 2][:, i * S:(i + 1) * S], [w[:, k, 2 * q + i, :] for w in (w_qe, w_qh)],
                                    [dx[n][:, b % 2, k, :] for n in (LO, HI)], start=k == 0, stop=k == KT - 1)
                ins.then_inc(G["d_q"], 1)

            d_fold(NT - 1)
            pe.wait_ge(G["d_rot"], 6 * (1 + KT))
            d_latent(0)
            d_keys(0, 0)
            pe.wait_ge(G["xT_done"], 2 * B - 1)
            to_xT(1, B - 1)
            d_query(0)
            d_keys(0, 1)

            def d_scores(h):
                p, b, g = h // 2, h // H1, (h % H1) // (H1 // KV1)
                pe.wait_ge(G["d_q_sb"], p + 1)
                pe.wait_ge(G["d_k_sb"], 2 * b + 2)
                o = PS[2 + h % 2]
                if h < 2:
                    pe.wait_ge(*((G["f_h"], 2 * NT) if h == 0 else (G["f_sig"], 2 * NT)))
                else:
                    pe.wait_ge(G["d_exp"], 2 * (h - 2) + 2)
                q = qe[:, p % 3, h % 2, :]
                k = kg[:, b % 2, g, :]
                mm(o[:, 0:3 * P], ident16[:, :], cbias[:, :], stop=False)
                mm(o[:, 0:P], q[:, 0:P], k[:, 0:P], start=False, stop=False)
                mm(o[:, P:3 * P], q[:, P:S], k, start=False, stop=True).then_inc(G["d_s"], 1)

            def d_transpose(h):
                pe.wait_ge(G["d_norm"], 2 * h + 2)
                if h < 2:
                    pe.wait_ge(*((G["f_h"], 2 * NT) if h == 0 else (G["f_hqT_sb"], NT)))
                else:
                    pe.wait_ge(G["d_t_sb"], h - 1)
                for c in range(3):
                    ins = mm(PS[4 + h % 2][:, c * P:(c + 1) * P], dp[:, h % 6, c, :], ident, is_transpose=True)
                ins.then_inc(G["d_t"], 1)

            def d_values(p):
                b = p // PAIRS
                pe.wait_ge(G["d_t_sb"], 2 * p + 2)
                if p == 0:
                    pe.wait_ge(G["ln_var"], 3 * NT)
                else:
                    pe.wait_ge(G["d_o_lo"], p)
                for h in (2 * p, 2 * p + 1):
                    o = PS[6][(h % 2) * LAT:(h % 2 + 1) * LAT, :]
                    mm(o[:, 0:S], cR[:, b % 2, 0, :], dpT[:, h % 4, 0:S], stop=False)
                    ins = mm(o[:, P:S], cR[:, b % 2, 1, :], dpT[:, h % 4, S:3 * P], start=False)
                ins.then_inc(G["d_o"], 1)

            def d_out(t):
                b = t // TPB
                pe.wait_ge(G["d_o_lo"], PAIRS * (b + 1))
                pe.wait_ge(G["lo_part"], 3 * B + 2 * PAIRS + 2)
                if t % TPB == 0 and b > 0:
                    pe.wait_ge(G["xT_done"], 2 * B + b)
                if t % TPB == 1:
                    pe.wait_ge(G["ln_var"], 3 * NT + t)
                for i in range(PAIRS):
                    ins = split(PS[7][:, t % TPB * E:(t % TPB + 1) * E],
                                [o[:, (PAIRS * b + i) % DO_RING, t % TPB * P:(t % TPB + 1) * P] for o in doT],
                                [w[:, i, :] for w in (w_vo, w_vh)], start=i == 0, stop=i == PAIRS - 1)
                ins.then_inc(G["d_y"], 1)

            pe.wait_ge(G["ld_cbias"], 16)
            NP = B * PAIRS
            for p in range(NP + 4):
                b, q = divmod(p, PAIRS)
                if p + 1 < NP:
                    d_query(p + 1)
                if q == 6 and b > 0:
                    pe.wait_ge(*((G["d_k_sb"], 2 * b + 4) if b + 1 < B else (G["ln_var"], 3 * NT + 2 * b)))
                    to_xT(2, b - 1)
                if p < NP:
                    d_scores(2 * p)
                    d_scores(2 * p + 1)
                if q == 3 and b > 0:
                    d_out(2 * (b - 1))
                if 2 <= p < NP + 2:
                    d_transpose(2 * p - 4)
                    d_transpose(2 * p - 3)
                if 3 <= p < NP + 3:
                    d_values(p - 3)
                if q == 3 and b > 0:
                    d_out(2 * (b - 1) + 1)
                if q == 4 and b + 1 < B:
                    d_latent(b + 1)
                if q == 5 and b + 1 < B:
                    d_keys(b + 1, 0)
                    d_keys(b + 1, 1)
            def e_feature_rows(bank, b, n, s):
                pe.wait_ge(G["xT_done"], 2 * B + b + 1)
                for f in range(KT):
                    ins = project(PS[bank][:, f * S:(f + 1) * S], lambda k: w_x1[:, n, k, f * P:(f + 1) * P],
                                  lambda k: xT[:, k, b * S:(b + 1) * S])
                ins.then_inc(G[s], 1)

            def e_gate(b):
                if b == 0:
                    pe.wait_ge(G["d_q_sb"], NP)
                elif b == 2:
                    pe.wait_ge(G["d_exp"], 4 * NP)
                e_feature_rows(b, b, 3, "e_g")

            def e_query(b):
                pe.wait_ge(*((G["e_qf"], b - 1) if b >= 2 else (G["d_t_sb"], 2 * NP)))
                e_feature_rows(4 + b % 2, b, 2, "e_q")

            def e_attend(b):
                pe.wait_ge(G["e_qf"], b + 1)
                pe.wait_ge(*((G["e_av"], 2 * b) if b else (G["e_sig"], 4)))
                for t in range(TPB):
                    for f in range(KT):
                        ins = mm(PS[t][:, f * (P + HT):(f + 1) * (P + HT)], qf[:, b % 2, f, t * P:(t + 1) * P], kvd[:, b, f, :])
                    ins.then_inc(G["e_nd"], 1)

            def e_transpose(b):
                pe.wait_ge(G["e_av"], 2 * b + 2)
                pe.wait_ge(*((G["e_at"], b) if b else (G["e_sig"], 6)))
                for k in range(KT):
                    for t in range(TPB):
                        ins = mm(PS[2][:, k * S + t * P:k * S + (t + 1) * P], eav[:, b % 2, t, k * P:(k + 1) * P], ident, is_transpose=True)
                ins.then_inc(G["e_avT"], 1)

            def e_out(b):
                pe.wait_ge(G["e_at"], b + 1)
                pe.wait_ge(*((G["ln_var"], 4 * NT + 2 * b) if b else (G["e_sig"], 8)))
                for t in range(TPB):
                    ins = project(PS[3][:, t * E:(t + 1) * E], lambda k: eat[:, b % 2, k, t * P:(t + 1) * P], lambda k: w_x1[:, 4, k, :])
                ins.then_inc(G["e_y"], 1)

            def r_logits(b):
                pe.wait_ge(G["xT_done"], 3 * B + b + 1)
                if b > 1:
                    pe.wait_ge(G["r_rows"], 2 * (b - 1))
                for t in range(TPB):
                    ins = project(PS[7][:, t * NE:(t + 1) * NE], lambda k: xT[:, k, b * S + t * P:b * S + (t + 1) * P],
                                  lambda k: w_rt[:, k, :])
                ins.then_inc(G["r_log"], 1)

            def r_count(b):
                pe.wait_ge(G["r_kept"], b + 1)
                if b + 1 < B:
                    pe.wait_ge(G["r_act"], b + 2)
                if b > 0:
                    pe.wait_ge(G["r_rows"], 2 * b)
                else:
                    pe.wait_ge(G["r_set"], 2)
                for t in range(2 * b, 2 * b + 2):
                    at = TPB * NE + t % 2 * NE
                    o = PS[7][:, at:at + NE]
                    for u in range(t):
                        mm(o, ones16, kept16[:, u, :], start=u == 0, stop=False)
                    ins = mm(o, before16, kept16[:, t, :], start=t == 0)
                if b == B - 1:
                    at = 2 * TPB * NE
                    for t in range(NT):
                        ins = mm(PS[7][:, at:at + NE], ones16, kept16[:, t, :], start=t == 0, stop=t == NT - 1)
                ins.then_inc(G["r_count"], 1)

            for b in range(B - 1):
                e_gate(b)
            pe.wait_ge(G["ln_var"], 4 * NT)
            to_xT(2, B - 1)
            e_query(0)
            e_gate(B - 1)
            for b in range(B + 3):
                if b + 1 < B:
                    e_query(b + 1)
                if b < B:
                    e_attend(b)
                if 1 <= b <= B:
                    e_out(b - 1)
                if b < B:
                    e_transpose(b)
                if 2 <= b <= B + 1:
                    pe.wait_ge(*((G["xT_done"], 3 * B + b - 2) if b > 2 else (G["d_o_lo"], NP)))
                    to_xT(3, b - 2)
                    r_logits(b - 2)
                if b >= 3:
                    r_count(b - 3)

            def expert(i):
                return pe.value_load(table[0:1, 0, bass.ds(i, 1)], min_val=0, max_val=NE - 1)

            def m_tokens(slot, count):
                pe.wait_ge(G[f"m_x{slot}"], count)
                for k in range(KT):
                    ins = mm(PS[5][:, k * P:(k + 1) * P], xg[:, slot, k * P:(k + 1) * P], ident, is_transpose=True)
                ins.then_inc(G["m_xT"], 1)

            def m_half(n, e, slot, s):
                ins = project(PS[n][:, :], lambda k: xgT[:, slot, k, :],
                              lambda k: w_all[:, bass.ds(e, 1), (n * KT + k) * FI:(n * KT + k + 1) * FI])
                ins.then_inc(G[s], 1)

            def m_hiddenT(i):
                pe.wait_ge(G["m_h"], i + 1)
                for m in range(FM):
                    ins = mm(PS[2][:, m * P:(m + 1) * P], hs[:, m * P:(m + 1) * P], ident, is_transpose=True)
                ins.then_inc(G["m_hT"], 1)

            def m_down(i, e, free=True):
                pe.wait_ge(G["m_hT_sb"], i + 1)
                if free:
                    pe.wait_ge(G["m_y_sb"], i)
                for m in range(FM):
                    at = 2 * KT * FI + m * E
                    ins = mm(PS[4][:, 0:E], hT[:, m, :], w_all[:, bass.ds(e, 1), at:at + E], start=m == 0, stop=m == FM - 1)
                ins.then_inc(G["m_y"], 1)

            def m_step(i, h, slot, first=False, last=False, free=True):
                e = expert(i)
                pe.wait_ge(G["m_xT_sb"], i + 1)
                m_half(0, e, slot, "m_g")
                if not first:
                    m_hiddenT(i - 1)
                if not last:
                    m_tokens(1 - slot, (h + (2 if slot else 1)) * 16)
                m_half(1, e, slot, "m_u")
                if not first:
                    m_down(i - 1, expert(i - 1), free)

            pe.wait_ge(G["ld_exp"], 16 * NE)
            pe.wait_ge(G["r_table"], 1)
            m_tokens(0, 16)
            m_step(0, 0, 0, first=True)
            m_step(1, 0, 1, free=False)
            m_step(2, 1, 0)
            with pe.Fori(1, TILES // 2 - 1) as h:
                m_step(h * 2 + 1, h, 1)
                m_step(h * 2 + 2, h + 1, 0)
            m_step(TILES - 2, TILES // 2 - 1, 1)
            m_step(TILES - 1, TILES // 2, 0, last=True)
            m_hiddenT(TILES - 1)
            m_down(TILES - 1, expert(TILES - 1))


def pack(w):
    return np.ascontiguousarray(w.reshape(-1, P, w.shape[1]).transpose(1, 0, 2))


def kernel(**inputs):
    import concourse.bacc as bacc
    from concourse.bass_utils import run_bass_kernel_spmd as run

    i = {k: np.asarray(v) for k, v in inputs.items() if k != "mask_BxSx4224_bf0"}
    x = i["x"].reshape(B * S, E)
    a = {"x": x, "xT": pack(x.T), "cst": constants(), "cbias": causal_bias()}
    a["w_qkv"] = pack(i["L0_attn_w_qkv"].T)
    w_o0 = np.zeros((H0, D0P, E), np.float32)
    w_o0[:, :D0] = i["L0_attn_w_out"].T.reshape(H0, D0, E)
    a["w_o0"] = pack(w_o0.reshape(H0 * D0P, E))
    for n, k in enumerate("qkvo"):
        a[f"w_x0_{n}"] = pack(i[f"L0_xattn_w{k}"].T)
    a["ctx"] = i["ctx_2048"]
    a["ctxT"] = np.ascontiguousarray(i["ctx_2048"].transpose(0, 2, 1).reshape(B, KT, P, CTX).transpose(0, 2, 1, 3))
    wkv = i["L1_xattn_Wkv"]
    for n, w in enumerate((wkv[:E], wkv[E:], i["L1_xattn_Wq"], i["L1_xattn_Wg"], i["L1_xattn_Wo"])):
        a[f"w_x1_{n}"] = pack(w.T)
    a["bg"] = np.ascontiguousarray(i["L1_xattn_bg"].reshape(KT, P).T)
    for n, k in enumerate(("gate", "up", "down")):
        a[f"w_f{n}"] = pack(i[f"L0_ffn_w_{k}"].T).reshape(P, 2 * FF)
    a["w_kvc"] = pack(i["L1_attn_Wkvc"])
    a["eye4"] = np.ascontiguousarray(np.broadcast_to(np.eye(LAT, dtype=np.float32)[:, None], (LAT, KV1, LAT)))
    halves = lambda w, h: w.reshape(-1, h, RH, 2).transpose(0, 1, 3, 2).reshape(-1, h, RD)
    a["w_kr"] = np.ascontiguousarray(halves(i["L1_attn_Wkrope"], KV1))
    a["w_kd"] = np.ascontiguousarray(i["L1_attn_Wkdec"].reshape(LAT, KV1, HD).transpose(2, 1, 0))
    a["w_vd"] = np.ascontiguousarray(i["L1_attn_Wvdec"].reshape(LAT, KV1, HD).transpose(2, 1, 0))
    a["w_rt"] = pack(i["L1_ffn_w_gate"])
    a["w_qT"] = np.ascontiguousarray(i["L1_attn_Wq"].reshape(E, H1, HD).transpose(2, 1, 0))
    a["w_qr"] = np.ascontiguousarray(halves(i["L1_attn_Wqrope"], H1).reshape(KT, P, H1, RD).transpose(1, 0, 2, 3))
    a["w_oh"] = np.ascontiguousarray(i["L1_attn_Wo"].reshape(H1, HD + RD, E)[:, :HD].transpose(1, 0, 2))
    per = lambda w: w.reshape(NE, -1, P, w.shape[2]).transpose(2, 0, 1, 3).reshape(P, NE, -1)
    a["w_exp"] = np.concatenate([per(i[f"L1_ffn_w{n}"]) for n in (1, 3, 2)], axis=2)

    nc = bacc.Bacc("TRN2", target_bir_lowering=False, num_devices=1)
    dr = {k: nc.dram_tensor(f"in_{k}", v.shape, F32, kind="ExternalInput").ap() for k, v in a.items()}
    out = nc.dram_tensor("out", (B * S, E), F32, kind="ExternalOutput").ap()
    xs = nc.dram_tensor("xs", (ROWS, E + 2), F32, kind="Internal").ap()
    ys = nc.dram_tensor("ys", (1 + TOPK * TOKENS, E), F32, kind="Internal").ap()
    build(nc, dr, xs, ys, out)
    r = run(nc, [{f"in_{k}": v for k, v in a.items()}], core_ids=[0])
    return r.results[0]["out"].reshape(B, S, E)
```
